# Optimizing a Trainium2 kernel written in Bass

```python
import numpy as np
import jax
import jax.numpy as jnp

def _softmax(x, axis=-1):
    return jax.nn.softmax(x, axis=axis)

def _gelu(x):
    return jax.nn.gelu(x, approximate=True)

def _silu(x):
    return jax.nn.silu(x)

def _sigmoid(x):
    return jax.nn.sigmoid(x)

def _layernorm(x, axis=-1, eps=1e-05):
    m = jnp.mean(x, axis=axis, keepdims=True)
    v = jnp.var(x, axis=axis, keepdims=True)
    return (x - m) / jnp.sqrt(v + eps)

def _scatter_add(tgt, idx, src, axis=0):
    return tgt.at[idx].add(src)

def _segment_sum(src, seg, n):
    return jax.ops.segment_sum(src, seg, n)
kernel_name = 'mk_vit_tower_postln_d4_tok_img1024_r4_2a0a34'

def setup_inputs(seed: int=0):
    np.random.seed(seed)
    _w = jnp.asarray

    def _rec_inputs():
        import jax
        import jax.numpy as jnp
        _rk = jax.random.key(seed)
        x = -0.000125008 + 0.999885 * jax.random.normal(jax.random.fold_in(_rk, 1), (4, 512, 256, 4), jnp.float32)
        return x
    x = _rec_inputs()

    def _L0_tok_setup():
        import jax, jax.numpy as jnp
        import numpy as np
        key = jax.random.key(seed)
        k1, k2, k3 = jax.random.split(key, 3)
        B, H, I, O, Dp1 = (4, 512, 256, 256, 4)
        x = jax.random.normal(k1, (B, H, I, Dp1), dtype=jnp.float32)
        weight = 0.1 * jax.random.normal(k2, (O, Dp1), dtype=jnp.float32)
        weighted_sum = 0.1 * jax.random.normal(k3, (O, I), dtype=jnp.float32)
        return {'x': x, 'weight': weight, 'weighted_sum': weighted_sum}
    _L0_tok_all = _L0_tok_setup()
    _L0_tok_in = {k: v for k, v in _L0_tok_all.items() if k in ('weight', 'weighted_sum')}
    del _L0_tok_all

    def _L0_attn_setup():
        import jax, jax.numpy as jnp
        import numpy as np
        B, T, D = (8, 512, 256)
        H, N = (8, 32)

        def _xavier(key, shape, fan_in, fan_out):
            lim = float(np.sqrt(6.0 / (fan_in + fan_out)))
            return jax.random.uniform(key, shape, jnp.float32, -lim, lim)

        def _reference_tuple_inner(x, W_in, W_k, W_v, W_q, W_beta, b_beta, W_out):
            b, t, d = x.shape
            h, n = b_beta.shape
            xp = jax.nn.silu(jnp.einsum('btd,ed->bte', x, W_in))

            def proj(W):
                return jnp.einsum('btd,md->btm', xp, W).reshape(b, t, h, n).transpose(1, 0, 2, 3)
            k_all = proj(W_k)
            v_all = proj(W_v)
            q_all = proj(W_q)
            beta_all = jax.nn.sigmoid(proj(W_beta) + b_beta)
            S0 = jnp.zeros((b, h, n, n), x.dtype)

            def step(S, inp):
                k, v, q, beta = inp
                kn = k / (jnp.linalg.norm(k, axis=-1, keepdims=True) + 1e-06)
                retrieved = jnp.einsum('bhij,bhj->bhi', S, kn)
                delta = v - retrieved
                S = jnp.tanh(beta[..., None] * S + delta[..., None] * kn[..., None, :])
                Sq = jnp.einsum('bhij,bhj->bhi', S, q)
                out = Sq * jax.nn.silu(Sq)
                return (S, out)
            S_final, outs = jax.lax.scan(step, S0, (k_all, v_all, q_all, beta_all))
            cell_out = outs.transpose(1, 0, 2, 3).reshape(b, t, h * n)
            y = jnp.einsum('btm,dm->btd', cell_out, W_out)
            return (y, S_final)
        key = jax.random.key(seed)
        ks = jax.random.split(key, 8)
        x = jax.random.normal(ks[0], (B, T, D), jnp.float32)
        W_in = _xavier(ks[1], (D, D), D, D)
        W_k = _xavier(ks[2], (H * N, D), N, D)
        W_v = _xavier(ks[3], (H * N, D), N, D)
        W_q = _xavier(ks[4], (H * N, D), N, D)
        W_beta = _xavier(ks[5], (H * N, D), N, D)
        b_beta = jnp.full((H, N), 2.0, jnp.float32)
        W_out = _xavier(ks[6], (D, H * N), H * N, D)
        return {'x': x, 'W_in': W_in, 'W_k': W_k, 'W_v': W_v, 'W_q': W_q, 'W_beta': W_beta, 'b_beta': b_beta, 'W_out': W_out}
    _L0_attn_all = _L0_attn_setup()
    _L0_attn_in = {k: v for k, v in _L0_attn_all.items() if k in ('W_in', 'W_k', 'W_v', 'W_q', 'W_beta', 'b_beta', 'W_out')}
    del _L0_attn_all

    def _L0_ffn_setup():
        import jax, jax.numpy as jnp
        import numpy as np
        DIM = 256
        N_HEADS = 16
        N_KV_HEADS = 4
        HEAD_DIM = DIM // N_HEADS
        N_REP = N_HEADS // N_KV_HEADS
        N_EXPERTS = 4
        TOP_K = 2
        HIDDEN = 3 * DIM
        EPS = 1.1920928955078125e-07

        def _rmsnorm(x, g):
            var = jnp.mean(jnp.square(x), axis=-1, keepdims=True)
            return x * jax.lax.rsqrt(var + EPS) * g

        def _rotate_half(x):
            x1, x2 = jnp.split(x, 2, axis=-1)
            return jnp.concatenate([-x2, x1], axis=-1)

        def _rope_tables(S):
            inv_freq = 1.0 / 10000.0 ** (jnp.arange(0, HEAD_DIM, 2, dtype=jnp.float32) / HEAD_DIM)
            freqs = jnp.arange(S, dtype=jnp.float32)[:, None] * inv_freq[None, :]
            emb = jnp.concatenate([freqs, freqs], axis=-1)
            return (jnp.cos(emb), jnp.sin(emb))

        def _attention(x, wq, wk, wv, wo):
            B, S, D = x.shape
            q = (x @ wq).reshape(B, S, N_HEADS, HEAD_DIM).transpose(0, 2, 1, 3)
            k = (x @ wk).reshape(B, S, N_KV_HEADS, HEAD_DIM).transpose(0, 2, 1, 3)
            v = (x @ wv).reshape(B, S, N_KV_HEADS, HEAD_DIM).transpose(0, 2, 1, 3)
            cos, sin = _rope_tables(S)
            q = q * cos + _rotate_half(q) * sin
            k = k * cos + _rotate_half(k) * sin
            k = jnp.repeat(k, N_REP, axis=1)
            v = jnp.repeat(v, N_REP, axis=1)
            scores = jnp.einsum('bhqd,bhkd->bhqk', q, k) / jnp.sqrt(jnp.float32(HEAD_DIM))
            causal = jnp.tril(jnp.ones((S, S), dtype=bool))
            scores = jnp.where(causal, scores, -jnp.inf)
            attn = jax.nn.softmax(scores, axis=-1)
            out = jnp.einsum('bhqk,bhkd->bhqd', attn, v)
            return out.transpose(0, 2, 1, 3).reshape(B, S, D) @ wo

        def _moe(x, gate, w1, w2, w3):
            B, S, D = x.shape
            xf = x.reshape(-1, D)
            probs = jax.nn.softmax(xf @ gate, axis=-1)
            w, idx = jax.lax.top_k(probs, TOP_K)
            w = w / jnp.sum(w, axis=-1, keepdims=True)
            oh = jax.nn.one_hot(idx, N_EXPERTS, dtype=xf.dtype)
            comb = jnp.einsum('nk,nke->ne', w, oh)
            out = jnp.zeros_like(xf)
            for e in range(N_EXPERTS):
                h = jax.nn.silu(xf @ w1[e]) * (xf @ w3[e])
                out = out + comb[:, e:e + 1] * (h @ w2[e])
            return out.reshape(B, S, D)
        key = jax.random.key(seed)
        ks = jax.random.split(key, 12)
        s = 0.02
        B, S = (2, 512)
        return {'x': jax.random.normal(ks[0], (B, S, DIM), jnp.float32), 'g1': jnp.ones((DIM,), jnp.float32), 'g2': jnp.ones((DIM,), jnp.float32), 'wq': jax.random.normal(ks[1], (DIM, N_HEADS * HEAD_DIM), jnp.float32) * s, 'wk': jax.random.normal(ks[2], (DIM, N_KV_HEADS * HEAD_DIM), jnp.float32) * s, 'wv': jax.random.normal(ks[3], (DIM, N_KV_HEADS * HEAD_DIM), jnp.float32) * s, 'wo': jax.random.normal(ks[4], (N_HEADS * HEAD_DIM, DIM), jnp.float32) * s, 'gate': jax.random.normal(ks[5], (DIM, N_EXPERTS), jnp.float32) * s, 'w1': jax.random.normal(ks[6], (N_EXPERTS, DIM, HIDDEN), jnp.float32) * s, 'w2': jax.random.normal(ks[7], (N_EXPERTS, HIDDEN, DIM), jnp.float32) * s, 'w3': jax.random.normal(ks[8], (N_EXPERTS, DIM, HIDDEN), jnp.float32) * s}
    _L0_ffn_all = _L0_ffn_setup()
    _L0_ffn_in = {k: v for k, v in _L0_ffn_all.items() if k in ('g1', 'g2', 'wq', 'wk', 'wv', 'wo', 'gate', 'w1', 'w2', 'w3')}
    del _L0_ffn_all

    def _L1_attn_setup():
        import jax, jax.numpy as jnp
        from jax import lax
        import numpy as np
        DIM = 256
        HEADS = 16
        B, N = (2, 512)

        def sn_dense(x, W, u, sigma_param):
            v = lax.stop_gradient(W @ u)
            v = lax.stop_gradient(v / jnp.linalg.norm(v, ord=2))
            u2 = lax.stop_gradient(W.T @ v)
            u2 = lax.stop_gradient(u2 / jnp.linalg.norm(u2, ord=2))
            sigma = jnp.einsum('c,cd,d->', v, W, u2)
            return x @ (sigma_param[0] / sigma * W)
        key = jax.random.key(seed)
        ks = jax.random.split(key, 5)
        std = 0.1
        batch = jax.random.normal(ks[0], (B, N, DIM), dtype=jnp.float32)
        W_qkv = jax.random.normal(ks[1], (DIM, 3 * DIM), dtype=jnp.float32) * std
        W_proj = jax.random.normal(ks[2], (DIM, DIM), dtype=jnp.float32) * std
        u_qkv = jax.random.normal(ks[3], (3 * DIM,), dtype=jnp.float32)
        u_qkv = u_qkv / jnp.linalg.norm(u_qkv)
        u_proj = jax.random.normal(ks[4], (DIM,), dtype=jnp.float32)
        u_proj = u_proj / jnp.linalg.norm(u_proj)
        sigma_qkv = jnp.ones((1,), dtype=jnp.float32)
        sigma_proj = jnp.ones((1,), dtype=jnp.float32)
        return {'batch': batch, 'W_qkv': W_qkv, 'u_qkv': u_qkv, 'sigma_qkv': sigma_qkv, 'W_proj': W_proj, 'u_proj': u_proj, 'sigma_proj': sigma_proj}
    _L1_attn_all = _L1_attn_setup()
    _L1_attn_in = {k: v for k, v in _L1_attn_all.items() if k in ('W_qkv', 'u_qkv', 'sigma_qkv', 'W_proj', 'u_proj', 'sigma_proj')}
    del _L1_attn_all

    def _L1_ffn_setup():
        import jax, jax.numpy as jnp
        import numpy as np
        B, S, H, E, DFF = (4, 1024, 256, 8, 1024)
        key = jax.random.key(seed)
        k0, k1, k2, k3 = jax.random.split(key, 4)
        hidden_states = jax.random.normal(k0, (B, S, H), dtype=jnp.float32)
        gate_w = jax.random.normal(k1, (E, H), dtype=jnp.float32) * 0.02
        w1 = jax.random.normal(k2, (E, H, DFF), dtype=jnp.float32) * 0.02
        b1 = jnp.zeros((E, DFF), dtype=jnp.float32)
        w2 = jax.random.normal(k3, (E, DFF, H), dtype=jnp.float32) * 0.02
        b2 = jnp.zeros((E, H), dtype=jnp.float32)
        return {'hidden_states': hidden_states, 'gate_w': gate_w, 'w1': w1, 'b1': b1, 'w2': w2, 'b2': b2}
    _L1_ffn_all = _L1_ffn_setup()
    _L1_ffn_in = {k: v for k, v in _L1_ffn_all.items() if k in ('gate_w', 'w1', 'b1', 'w2', 'b2')}
    del _L1_ffn_all

    def _L2_attn_setup():
        import jax, jax.numpy as jnp
        import numpy as np
        HEADS = 16

        def _binarize(W):
            alpha = jnp.mean(jnp.abs(W), axis=tuple(range(1, W.ndim)), keepdims=True)
            B = W + jax.lax.stop_gradient(jnp.sign(W) - W)
            return alpha * B

        def _binlinear(x, W, b):
            Wb = _binarize(W)
            return jnp.einsum('btc,oc->bto', x, Wb) + b
        key = jax.random.key(seed)
        ks = jax.random.split(key, 9)
        dim = 256
        B, T = (4, 512)
        inp = {'x': jax.random.normal(ks[0], (B, T, dim), jnp.float32), 'Wq': jax.random.normal(ks[1], (dim, dim), jnp.float32) * 0.02, 'bq': jax.random.normal(ks[2], (dim,), jnp.float32) * 0.02, 'Wk': jax.random.normal(ks[3], (dim, dim), jnp.float32) * 0.02, 'bk': jax.random.normal(ks[4], (dim,), jnp.float32) * 0.02, 'Wv': jax.random.normal(ks[5], (dim, dim), jnp.float32) * 0.02, 'bv': jax.random.normal(ks[6], (dim,), jnp.float32) * 0.02, 'Wp': jax.random.normal(ks[7], (dim, dim), jnp.float32) * 0.02, 'bp': jax.random.normal(ks[8], (dim,), jnp.float32) * 0.02}
        return inp
    _L2_attn_all = _L2_attn_setup()
    _L2_attn_in = {k: v for k, v in _L2_attn_all.items() if k in ('Wq', 'bq', 'Wk', 'bk', 'Wv', 'bv', 'Wp', 'bp')}
    del _L2_attn_all

    def _L2_ffn_setup():
        import jax, jax.numpy as jnp
        import numpy as np
        EPS = 1e-05

        def _layernorm(x, w, b):
            mu = jnp.mean(x, axis=-1, keepdims=True)
            var = jnp.mean((x - mu) ** 2, axis=-1, keepdims=True)
            return (x - mu) * jax.lax.rsqrt(var + EPS) * w + b

        def _rope_tables(T, D, base=10000.0):
            inv_freq = 1.0 / base ** (jnp.arange(0, D, 2, dtype=jnp.float32) / D)
            t = jnp.arange(T, dtype=jnp.float32)
            freqs = jnp.einsum('i,j->ij', t, inv_freq)
            emb = jnp.concatenate([freqs, freqs], axis=-1)
            return (jnp.cos(emb), jnp.sin(emb))

        def _rotate_half(x):
            x1, x2 = (x[..., :x.shape[-1] // 2], x[..., x.shape[-1] // 2:])
            return jnp.concatenate([-x2, x1], axis=-1)

        def _attn(x, ln_w, ln_b, conv_w, attn_w, proj_w, n_head):
            B, T, C = x.shape
            D = C // n_head
            h = _layernorm(x, ln_w, ln_b)
            hc = jnp.transpose(h, (0, 2, 1))
            hc = jnp.pad(hc, ((0, 0), (0, 0), (2, 0)))
            hc = jax.lax.conv_general_dilated(hc, conv_w, window_strides=(1,), padding='VALID', dimension_numbers=('NCH', 'OIH', 'NCH'), feature_group_count=C)
            h = jnp.transpose(hc, (0, 2, 1))
            qkv = h @ attn_w
            q, k, v = jnp.split(qkv, 3, axis=-1)
            q = q.reshape(B, T, n_head, D)
            k = k.reshape(B, T, n_head, D)
            v = v.reshape(B, T, n_head, D)
            cos, sin = _rope_tables(T, D)
            cos = cos[None, :, None, :]
            sin = sin[None, :, None, :]
            q = q * cos + _rotate_half(q) * sin
            k = k * cos + _rotate_half(k) * sin
            scores = jnp.einsum('bqhd,bkhd->bhqk', q, k) / jnp.sqrt(jnp.float32(D))
            causal = jnp.tril(jnp.ones((T, T), dtype=bool))
            scores = jnp.where(causal, scores, jnp.float32(-1e+30))
            p = jax.nn.softmax(scores, axis=-1)
            y = jnp.einsum('bhqk,bkhd->bqhd', p, v).reshape(B, T, C)
            return y @ proj_w

        def _moe(x, ln_w, ln_b, router_w, expert_wv, expert_proj):
            h = _layernorm(x, ln_w, ln_b)
            logits = h @ router_w
            expert_idx = jnp.argmax(logits, axis=-1)
            E = router_w.shape[-1]
            out = jnp.zeros_like(x)
            for e in range(E):
                gv = h @ expert_wv[e]
                gate_raw, value = jnp.split(gv, 2, axis=-1)
                y = gate_raw * jax.nn.sigmoid(gate_raw) * value @ expert_proj[e]
                out = out + jnp.where((expert_idx == e)[..., None], y, 0.0)
            return out
        C, H, E, B, T = (256, 16, 4, 4, 256)
        Dff = 4 * C
        key = jax.random.key(seed)
        ks = jax.random.split(key, 8)
        s = 0.02
        return {'x': jax.random.normal(ks[0], (B, T, C), dtype=jnp.float32), 'ln1_w': jnp.ones((C,), jnp.float32), 'ln1_b': jnp.zeros((C,), jnp.float32), 'ln2_w': jnp.ones((C,), jnp.float32), 'ln2_b': jnp.zeros((C,), jnp.float32), 'conv_w': jax.random.normal(ks[1], (C, 1, 3), dtype=jnp.float32) * 0.1, 'attn_w': jax.random.normal(ks[2], (C, 3 * C), dtype=jnp.float32) * s, 'proj_w': jax.random.normal(ks[3], (C, C), dtype=jnp.float32) * s, 'router_w': jax.random.normal(ks[4], (C, E), dtype=jnp.float32) * s, 'expert_wv': jax.random.normal(ks[5], (E, C, 2 * Dff), dtype=jnp.float32) * s, 'expert_proj': jax.random.normal(ks[6], (E, Dff, C), dtype=jnp.float32) * s}
    _L2_ffn_all = _L2_ffn_setup()
    _L2_ffn_in = {k: v for k, v in _L2_ffn_all.items() if k in ('ln1_w', 'ln1_b', 'ln2_w', 'ln2_b', 'conv_w', 'attn_w', 'proj_w', 'router_w', 'expert_wv', 'expert_proj')}
    del _L2_ffn_all

    def _L3_attn_setup():
        import jax, jax.numpy as jnp
        import numpy as np
        EPS = 1e-05

        def layer_norm(x, w, b):
            mu = jnp.mean(x, axis=-1, keepdims=True)
            var = jnp.var(x, axis=-1, keepdims=True)
            return (x - mu) / jnp.sqrt(var + EPS) * w + b
        key = jax.random.key(seed)
        B, N, C = (4, 1024, 256)
        H = 16
        MW = 4 * C
        ks = jax.random.split(key, 8)
        s = 0.02
        return {'x': jax.random.normal(ks[0], (B, N, C), dtype=jnp.float32), 'ln1_w': jnp.ones((C,), jnp.float32), 'ln1_b': jnp.zeros((C,), jnp.float32), 'q_w': jax.random.normal(ks[1], (C, C), jnp.float32) * s, 'q_b': jnp.zeros((C,), jnp.float32), 'k_w': jax.random.normal(ks[2], (C, C), jnp.float32) * s, 'k_b': jnp.zeros((C,), jnp.float32), 'v_w': jax.random.normal(ks[3], (C, C), jnp.float32) * s, 'v_b': jnp.zeros((C,), jnp.float32), 'o_w': jax.random.normal(ks[4], (C, C), jnp.float32) * s, 'o_b': jnp.zeros((C,), jnp.float32), 'ln2_w': jnp.ones((C,), jnp.float32), 'ln2_b': jnp.zeros((C,), jnp.float32), 'fc_w': jax.random.normal(ks[5], (MW, C), jnp.float32) * s, 'fc_b': jnp.zeros((MW,), jnp.float32), 'proj_w': jax.random.normal(ks[6], (C, MW), jnp.float32) * s, 'proj_b': jnp.zeros((C,), jnp.float32)}
    _L3_attn_all = _L3_attn_setup()
    _L3_attn_in = {k: v for k, v in _L3_attn_all.items() if k in ('ln1_w', 'ln1_b', 'q_w', 'q_b', 'k_w', 'k_b', 'v_w', 'v_b', 'o_w', 'o_b', 'ln2_w', 'ln2_b', 'fc_w', 'fc_b', 'proj_w', 'proj_b')}
    del _L3_attn_all

    def _L3_ffn_setup():
        import jax, jax.numpy as jnp
        import numpy as np
        EPS = 1e-05

        def _quantize(W):
            gamma = jnp.mean(jnp.abs(W))
            return jnp.clip(jnp.round(W / (gamma + EPS)), -1.0, 1.0)
        key = jax.random.key(seed)
        k_x, k_w1, k_b1, k_w2, k_b2 = jax.random.split(key, 5)
        n_embd = 256
        d_ff = 4 * n_embd
        B, S = (4, 1024)
        bound1 = 1.0 / np.sqrt(n_embd)
        bound2 = 1.0 / np.sqrt(d_ff)
        x = jax.random.normal(k_x, (B, S, n_embd), dtype=jnp.float32)
        W1 = jax.random.uniform(k_w1, (d_ff, n_embd), jnp.float32, -bound1, bound1)
        b1 = jax.random.uniform(k_b1, (d_ff,), jnp.float32, -bound1, bound1)
        W2 = jax.random.uniform(k_w2, (n_embd, d_ff), jnp.float32, -bound2, bound2)
        b2 = jax.random.uniform(k_b2, (n_embd,), jnp.float32, -bound2, bound2)
        return {'x': x, 'W1': W1, 'b1': b1, 'W2': W2, 'b2': b2}
    _L3_ffn_all = _L3_ffn_setup()
    _L3_ffn_in = {k: v for k, v in _L3_ffn_all.items() if k in ('W1', 'b1', 'W2', 'b2')}
    del _L3_ffn_all
    return {'x': x, 'L0_tok_weight': _L0_tok_in['weight'], 'L0_tok_weighted_sum': _L0_tok_in['weighted_sum'], 'L0_attn_W_in': _L0_attn_in['W_in'], 'L0_attn_W_k': _L0_attn_in['W_k'], 'L0_attn_W_v': _L0_attn_in['W_v'], 'L0_attn_W_q': _L0_attn_in['W_q'], 'L0_attn_W_beta': _L0_attn_in['W_beta'], 'L0_attn_b_beta': _L0_attn_in['b_beta'], 'L0_attn_W_out': _L0_attn_in['W_out'], 'L0_ffn_g1': _L0_ffn_in['g1'], 'L0_ffn_g2': _L0_ffn_in['g2'], 'L0_ffn_wq': _L0_ffn_in['wq'], 'L0_ffn_wk': _L0_ffn_in['wk'], 'L0_ffn_wv': _L0_ffn_in['wv'], 'L0_ffn_wo': _L0_ffn_in['wo'], 'L0_ffn_gate': _L0_ffn_in['gate'], 'L0_ffn_w1': _L0_ffn_in['w1'], 'L0_ffn_w2': _L0_ffn_in['w2'], 'L0_ffn_w3': _L0_ffn_in['w3'], 'L1_attn_W_qkv': _L1_attn_in['W_qkv'], 'L1_attn_u_qkv': _L1_attn_in['u_qkv'], 'L1_attn_sigma_qkv': _L1_attn_in['sigma_qkv'], 'L1_attn_W_proj': _L1_attn_in['W_proj'], 'L1_attn_u_proj': _L1_attn_in['u_proj'], 'L1_attn_sigma_proj': _L1_attn_in['sigma_proj'], 'L1_ffn_gate_w': _L1_ffn_in['gate_w'], 'L1_ffn_w1': _L1_ffn_in['w1'], 'L1_ffn_b1': _L1_ffn_in['b1'], 'L1_ffn_w2': _L1_ffn_in['w2'], 'L1_ffn_b2': _L1_ffn_in['b2'], 'L2_attn_Wq': _L2_attn_in['Wq'], 'L2_attn_bq': _L2_attn_in['bq'], 'L2_attn_Wk': _L2_attn_in['Wk'], 'L2_attn_bk': _L2_attn_in['bk'], 'L2_attn_Wv': _L2_attn_in['Wv'], 'L2_attn_bv': _L2_attn_in['bv'], 'L2_attn_Wp': _L2_attn_in['Wp'], 'L2_attn_bp': _L2_attn_in['bp'], 'L2_ffn_ln1_w': _L2_ffn_in['ln1_w'], 'L2_ffn_ln1_b': _L2_ffn_in['ln1_b'], 'L2_ffn_ln2_w': _L2_ffn_in['ln2_w'], 'L2_ffn_ln2_b': _L2_ffn_in['ln2_b'], 'L2_ffn_conv_w': _L2_ffn_in['conv_w'], 'L2_ffn_attn_w': _L2_ffn_in['attn_w'], 'L2_ffn_proj_w': _L2_ffn_in['proj_w'], 'L2_ffn_router_w': _L2_ffn_in['router_w'], 'L2_ffn_expert_wv': _L2_ffn_in['expert_wv'], 'L2_ffn_expert_proj': _L2_ffn_in['expert_proj'], 'L3_attn_ln1_w': _L3_attn_in['ln1_w'], 'L3_attn_ln1_b': _L3_attn_in['ln1_b'], 'L3_attn_q_w': _L3_attn_in['q_w'], 'L3_attn_q_b': _L3_attn_in['q_b'], 'L3_attn_k_w': _L3_attn_in['k_w'], 'L3_attn_k_b': _L3_attn_in['k_b'], 'L3_attn_v_w': _L3_attn_in['v_w'], 'L3_attn_v_b': _L3_attn_in['v_b'], 'L3_attn_o_w': _L3_attn_in['o_w'], 'L3_attn_o_b': _L3_attn_in['o_b'], 'L3_attn_ln2_w': _L3_attn_in['ln2_w'], 'L3_attn_ln2_b': _L3_attn_in['ln2_b'], 'L3_attn_fc_w': _L3_attn_in['fc_w'], 'L3_attn_fc_b': _L3_attn_in['fc_b'], 'L3_attn_proj_w': _L3_attn_in['proj_w'], 'L3_attn_proj_b': _L3_attn_in['proj_b'], 'L3_ffn_W1': _L3_ffn_in['W1'], 'L3_ffn_b1': _L3_ffn_in['b1'], 'L3_ffn_W2': _L3_ffn_in['W2'], 'L3_ffn_b2': _L3_ffn_in['b2']}

def reference(x, L0_tok_weight, L0_tok_weighted_sum, L0_attn_W_in, L0_attn_W_k, L0_attn_W_v, L0_attn_W_q, L0_attn_W_beta, L0_attn_b_beta, L0_attn_W_out, L0_ffn_g1, L0_ffn_g2, L0_ffn_wq, L0_ffn_wk, L0_ffn_wv, L0_ffn_wo, L0_ffn_gate, L0_ffn_w1, L0_ffn_w2, L0_ffn_w3, L1_attn_W_qkv, L1_attn_u_qkv, L1_attn_sigma_qkv, L1_attn_W_proj, L1_attn_u_proj, L1_attn_sigma_proj, L1_ffn_gate_w, L1_ffn_w1, L1_ffn_b1, L1_ffn_w2, L1_ffn_b2, L2_attn_Wq, L2_attn_bq, L2_attn_Wk, L2_attn_bk, L2_attn_Wv, L2_attn_bv, L2_attn_Wp, L2_attn_bp, L2_ffn_ln1_w, L2_ffn_ln1_b, L2_ffn_ln2_w, L2_ffn_ln2_b, L2_ffn_conv_w, L2_ffn_attn_w, L2_ffn_proj_w, L2_ffn_router_w, L2_ffn_expert_wv, L2_ffn_expert_proj, L3_attn_ln1_w, L3_attn_ln1_b, L3_attn_q_w, L3_attn_q_b, L3_attn_k_w, L3_attn_k_b, L3_attn_v_w, L3_attn_v_b, L3_attn_o_w, L3_attn_o_b, L3_attn_ln2_w, L3_attn_ln2_b, L3_attn_fc_w, L3_attn_fc_b, L3_attn_proj_w, L3_attn_proj_b, L3_ffn_W1, L3_ffn_b1, L3_ffn_W2, L3_ffn_b2):
    import jax
    import jax.numpy as jnp

    def _L0_tok_ref(x, weight, weighted_sum):
        import jax, jax.numpy as jnp
        import numpy as np
        return jnp.einsum('bhid,oi,od->bho', x, weighted_sum, weight)

    def _L0_attn_ref(x, W_in, W_k, W_v, W_q, W_beta, b_beta, W_out):
        import jax, jax.numpy as jnp
        import numpy as np
        B, T, D = (8, 512, 256)
        H, N = (8, 32)

        def _xavier(key, shape, fan_in, fan_out):
            lim = float(np.sqrt(6.0 / (fan_in + fan_out)))
            return jax.random.uniform(key, shape, jnp.float32, -lim, lim)

        def _reference_tuple_inner(x, W_in, W_k, W_v, W_q, W_beta, b_beta, W_out):
            b, t, d = x.shape
            h, n = b_beta.shape
            xp = jax.nn.silu(jnp.einsum('btd,ed->bte', x, W_in))

            def proj(W):
                return jnp.einsum('btd,md->btm', xp, W).reshape(b, t, h, n).transpose(1, 0, 2, 3)
            k_all = proj(W_k)
            v_all = proj(W_v)
            q_all = proj(W_q)
            beta_all = jax.nn.sigmoid(proj(W_beta) + b_beta)
            S0 = jnp.zeros((b, h, n, n), x.dtype)

            def step(S, inp):
                k, v, q, beta = inp
                kn = k / (jnp.linalg.norm(k, axis=-1, keepdims=True) + 1e-06)
                retrieved = jnp.einsum('bhij,bhj->bhi', S, kn)
                delta = v - retrieved
                S = jnp.tanh(beta[..., None] * S + delta[..., None] * kn[..., None, :])
                Sq = jnp.einsum('bhij,bhj->bhi', S, q)
                out = Sq * jax.nn.silu(Sq)
                return (S, out)
            S_final, outs = jax.lax.scan(step, S0, (k_all, v_all, q_all, beta_all))
            cell_out = outs.transpose(1, 0, 2, 3).reshape(b, t, h * n)
            y = jnp.einsum('btm,dm->btd', cell_out, W_out)
            return (y, S_final)
        return _reference_tuple_inner(x, W_in, W_k, W_v, W_q, W_beta, b_beta, W_out)[0]

    def _L0_ffn_ref(x, g1, g2, wq, wk, wv, wo, gate, w1, w2, w3):
        import jax, jax.numpy as jnp
        import numpy as np
        DIM = 256
        N_HEADS = 16
        N_KV_HEADS = 4
        HEAD_DIM = DIM // N_HEADS
        N_REP = N_HEADS // N_KV_HEADS
        N_EXPERTS = 4
        TOP_K = 2
        HIDDEN = 3 * DIM
        EPS = 1.1920928955078125e-07

        def _rmsnorm(x, g):
            var = jnp.mean(jnp.square(x), axis=-1, keepdims=True)
            return x * jax.lax.rsqrt(var + EPS) * g

        def _rotate_half(x):
            x1, x2 = jnp.split(x, 2, axis=-1)
            return jnp.concatenate([-x2, x1], axis=-1)

        def _rope_tables(S):
            inv_freq = 1.0 / 10000.0 ** (jnp.arange(0, HEAD_DIM, 2, dtype=jnp.float32) / HEAD_DIM)
            freqs = jnp.arange(S, dtype=jnp.float32)[:, None] * inv_freq[None, :]
            emb = jnp.concatenate([freqs, freqs], axis=-1)
            return (jnp.cos(emb), jnp.sin(emb))

        def _attention(x, wq, wk, wv, wo):
            B, S, D = x.shape
            q = (x @ wq).reshape(B, S, N_HEADS, HEAD_DIM).transpose(0, 2, 1, 3)
            k = (x @ wk).reshape(B, S, N_KV_HEADS, HEAD_DIM).transpose(0, 2, 1, 3)
            v = (x @ wv).reshape(B, S, N_KV_HEADS, HEAD_DIM).transpose(0, 2, 1, 3)
            cos, sin = _rope_tables(S)
            q = q * cos + _rotate_half(q) * sin
            k = k * cos + _rotate_half(k) * sin
            k = jnp.repeat(k, N_REP, axis=1)
            v = jnp.repeat(v, N_REP, axis=1)
            scores = jnp.einsum('bhqd,bhkd->bhqk', q, k) / jnp.sqrt(jnp.float32(HEAD_DIM))
            causal = jnp.tril(jnp.ones((S, S), dtype=bool))
            scores = jnp.where(causal, scores, -jnp.inf)
            attn = jax.nn.softmax(scores, axis=-1)
            out = jnp.einsum('bhqk,bhkd->bhqd', attn, v)
            return out.transpose(0, 2, 1, 3).reshape(B, S, D) @ wo

        def _moe(x, gate, w1, w2, w3):
            B, S, D = x.shape
            xf = x.reshape(-1, D)
            probs = jax.nn.softmax(xf @ gate, axis=-1)
            w, idx = jax.lax.top_k(probs, TOP_K)
            w = w / jnp.sum(w, axis=-1, keepdims=True)
            oh = jax.nn.one_hot(idx, N_EXPERTS, dtype=xf.dtype)
            comb = jnp.einsum('nk,nke->ne', w, oh)
            out = jnp.zeros_like(xf)
            for e in range(N_EXPERTS):
                h = jax.nn.silu(xf @ w1[e]) * (xf @ w3[e])
                out = out + comb[:, e:e + 1] * (h @ w2[e])
            return out.reshape(B, S, D)
        x = x + _attention(_rmsnorm(x, g1), wq, wk, wv, wo)
        x = x + _moe(_rmsnorm(x, g2), gate, w1, w2, w3)
        return x

    def _L1_attn_ref(batch, W_qkv, u_qkv, sigma_qkv, W_proj, u_proj, sigma_proj):
        import jax, jax.numpy as jnp
        from jax import lax
        import numpy as np
        DIM = 256
        HEADS = 16
        B, N = (2, 512)

        def sn_dense(x, W, u, sigma_param):
            v = lax.stop_gradient(W @ u)
            v = lax.stop_gradient(v / jnp.linalg.norm(v, ord=2))
            u2 = lax.stop_gradient(W.T @ v)
            u2 = lax.stop_gradient(u2 / jnp.linalg.norm(u2, ord=2))
            sigma = jnp.einsum('c,cd,d->', v, W, u2)
            return x @ (sigma_param[0] / sigma * W)
        b, n, d = batch.shape
        h = HEADS
        hd = d // h
        qkv = sn_dense(batch, W_qkv, u_qkv, sigma_qkv)
        q, k, v = jnp.split(qkv, 3, axis=-1)
        split_heads = lambda t: t.reshape(b, n, h, hd).transpose(0, 2, 1, 3)
        q, k, v = (split_heads(q), split_heads(k), split_heads(v))
        scale = hd ** (-0.5)
        att = jnp.einsum('bhqd,bhkd->bhqk', q, k) * scale
        causal = jnp.tril(jnp.ones((n, n), dtype=jnp.float32))
        big_neg = jnp.finfo(att.dtype).min
        att = jnp.where(causal[None, None] == 0, big_neg, att)
        att = jax.nn.softmax(att, axis=-1)
        x = jnp.einsum('bhqk,bhkd->bhqd', att, v)
        x = x.transpose(0, 2, 1, 3).reshape(b, n, d)
        x = sn_dense(x, W_proj, u_proj, sigma_proj)
        return x

    def _L1_ffn_ref(hidden_states, gate_w, w1, b1, w2, b2):
        import jax, jax.numpy as jnp
        import numpy as np
        B, S, H, E, DFF = (4, 1024, 256, 8, 1024)
        b, s, h = hidden_states.shape
        x = hidden_states.reshape(-1, h)
        gate_logits = x @ gate_w.T
        gate_probs = jax.nn.softmax(gate_logits, axis=-1)
        expert_idx = jnp.argmax(gate_probs, axis=-1)
        expert_w = jnp.take_along_axis(gate_probs, expert_idx[:, None], axis=1)[:, 0]
        out = jnp.zeros_like(x)
        n_experts = w1.shape[0]
        for e in range(n_experts):
            ye = jax.nn.relu(x @ w1[e] + b1[e]) @ w2[e] + b2[e]
            sel = (expert_idx == e)[:, None]
            out = out + jnp.where(sel, ye * expert_w[:, None], 0.0)
        return out.reshape(b, s, h)

    def _L2_attn_ref(x, Wq, bq, Wk, bk, Wv, bv, Wp, bp):
        import jax, jax.numpy as jnp
        import numpy as np
        HEADS = 16

        def _binarize(W):
            alpha = jnp.mean(jnp.abs(W), axis=tuple(range(1, W.ndim)), keepdims=True)
            B = W + jax.lax.stop_gradient(jnp.sign(W) - W)
            return alpha * B

        def _binlinear(x, W, b):
            Wb = _binarize(W)
            return jnp.einsum('btc,oc->bto', x, Wb) + b
        B, T, C = x.shape
        H = HEADS
        Dh = C // H
        scale = Dh ** (-0.5)

        def split_heads(t):
            return t.reshape(B, T, H, Dh).transpose(0, 2, 1, 3)
        q = split_heads(_binlinear(x, Wq, bq))
        k = split_heads(_binlinear(x, Wk, bk))
        v = split_heads(_binlinear(x, Wv, bv))
        att = jnp.einsum('bhtd,bhsd->bhts', q, k) * scale
        att = jax.nn.softmax(att, axis=-1)
        y = jnp.einsum('bhts,bhsd->bhtd', att, v)
        y = y.transpose(0, 2, 1, 3).reshape(B, T, C)
        return _binlinear(y, Wp, bp)

    def _L2_ffn_ref(x, ln1_w, ln1_b, ln2_w, ln2_b, conv_w, attn_w, proj_w, router_w, expert_wv, expert_proj):
        import jax, jax.numpy as jnp
        import numpy as np
        EPS = 1e-05

        def _layernorm(x, w, b):
            mu = jnp.mean(x, axis=-1, keepdims=True)
            var = jnp.mean((x - mu) ** 2, axis=-1, keepdims=True)
            return (x - mu) * jax.lax.rsqrt(var + EPS) * w + b

        def _rope_tables(T, D, base=10000.0):
            inv_freq = 1.0 / base ** (jnp.arange(0, D, 2, dtype=jnp.float32) / D)
            t = jnp.arange(T, dtype=jnp.float32)
            freqs = jnp.einsum('i,j->ij', t, inv_freq)
            emb = jnp.concatenate([freqs, freqs], axis=-1)
            return (jnp.cos(emb), jnp.sin(emb))

        def _rotate_half(x):
            x1, x2 = (x[..., :x.shape[-1] // 2], x[..., x.shape[-1] // 2:])
            return jnp.concatenate([-x2, x1], axis=-1)

        def _attn(x, ln_w, ln_b, conv_w, attn_w, proj_w, n_head):
            B, T, C = x.shape
            D = C // n_head
            h = _layernorm(x, ln_w, ln_b)
            hc = jnp.transpose(h, (0, 2, 1))
            hc = jnp.pad(hc, ((0, 0), (0, 0), (2, 0)))
            hc = jax.lax.conv_general_dilated(hc, conv_w, window_strides=(1,), padding='VALID', dimension_numbers=('NCH', 'OIH', 'NCH'), feature_group_count=C)
            h = jnp.transpose(hc, (0, 2, 1))
            qkv = h @ attn_w
            q, k, v = jnp.split(qkv, 3, axis=-1)
            q = q.reshape(B, T, n_head, D)
            k = k.reshape(B, T, n_head, D)
            v = v.reshape(B, T, n_head, D)
            cos, sin = _rope_tables(T, D)
            cos = cos[None, :, None, :]
            sin = sin[None, :, None, :]
            q = q * cos + _rotate_half(q) * sin
            k = k * cos + _rotate_half(k) * sin
            scores = jnp.einsum('bqhd,bkhd->bhqk', q, k) / jnp.sqrt(jnp.float32(D))
            causal = jnp.tril(jnp.ones((T, T), dtype=bool))
            scores = jnp.where(causal, scores, jnp.float32(-1e+30))
            p = jax.nn.softmax(scores, axis=-1)
            y = jnp.einsum('bhqk,bkhd->bqhd', p, v).reshape(B, T, C)
            return y @ proj_w

        def _moe(x, ln_w, ln_b, router_w, expert_wv, expert_proj):
            h = _layernorm(x, ln_w, ln_b)
            logits = h @ router_w
            expert_idx = jnp.argmax(logits, axis=-1)
            E = router_w.shape[-1]
            out = jnp.zeros_like(x)
            for e in range(E):
                gv = h @ expert_wv[e]
                gate_raw, value = jnp.split(gv, 2, axis=-1)
                y = gate_raw * jax.nn.sigmoid(gate_raw) * value @ expert_proj[e]
                out = out + jnp.where((expert_idx == e)[..., None], y, 0.0)
            return out
        n_head = 16
        x = x + _attn(x, ln1_w, ln1_b, conv_w, attn_w, proj_w, n_head)
        x = x + _moe(x, ln2_w, ln2_b, router_w, expert_wv, expert_proj)
        return x

    def _L3_attn_ref(x, ln1_w, ln1_b, q_w, q_b, k_w, k_b, v_w, v_b, o_w, o_b, ln2_w, ln2_b, fc_w, fc_b, proj_w, proj_b):
        import jax, jax.numpy as jnp
        import numpy as np
        EPS = 1e-05

        def layer_norm(x, w, b):
            mu = jnp.mean(x, axis=-1, keepdims=True)
            var = jnp.var(x, axis=-1, keepdims=True)
            return (x - mu) / jnp.sqrt(var + EPS) * w + b
        B, N, C = x.shape
        H = 16
        D = C // H
        xn = layer_norm(x, ln1_w, ln1_b)
        q = (xn @ q_w.T + q_b).reshape(B, N, H, D).transpose(0, 2, 1, 3)
        k = (xn @ k_w.T + k_b).reshape(B, N, H, D).transpose(0, 2, 1, 3)
        v = (xn @ v_w.T + v_b).reshape(B, N, H, D).transpose(0, 2, 1, 3)
        q = jax.nn.elu(q) + 1.0
        k = jax.nn.elu(k) + 1.0
        kv = jnp.einsum('bhnd,bhne->bnde', k, v)
        qkv = jnp.einsum('bhnd,bnde->bhne', q, kv)
        k_sum = k.sum(axis=1)
        qk = jnp.einsum('bhnd,bnd->bhn', q, k_sum)
        attn = qkv / qk[..., None]
        attn = attn.transpose(0, 2, 1, 3).reshape(B, N, C)
        attn = attn @ o_w.T + o_b
        x = x + attn
        xn2 = layer_norm(x, ln2_w, ln2_b)
        h = jax.nn.gelu(xn2 @ fc_w.T + fc_b, approximate=False)
        x = x + (h @ proj_w.T + proj_b)
        return x

    def _L3_ffn_ref(x, W1, b1, W2, b2):
        import jax, jax.numpy as jnp
        import numpy as np
        EPS = 1e-05

        def _quantize(W):
            gamma = jnp.mean(jnp.abs(W))
            return jnp.clip(jnp.round(W / (gamma + EPS)), -1.0, 1.0)
        Wq1 = _quantize(W1)
        Wq2 = _quantize(W2)
        h = jax.nn.relu(jnp.einsum('bsd,fd->bsf', x, Wq1) + b1)
        out = jnp.einsum('bsf,df->bsd', h, Wq2) + b2
        return out
    h = _L0_tok_ref(x, L0_tok_weight, L0_tok_weighted_sum)
    h = _layernorm(h + _L0_attn_ref(h, L0_attn_W_in, L0_attn_W_k, L0_attn_W_v, L0_attn_W_q, L0_attn_W_beta, L0_attn_b_beta, L0_attn_W_out), axis=-1)
    h = _layernorm(h + _L0_ffn_ref(h, L0_ffn_g1, L0_ffn_g2, L0_ffn_wq, L0_ffn_wk, L0_ffn_wv, L0_ffn_wo, L0_ffn_gate, L0_ffn_w1, L0_ffn_w2, L0_ffn_w3), axis=-1)
    h = _layernorm(h + _L1_attn_ref(h, L1_attn_W_qkv, L1_attn_u_qkv, L1_attn_sigma_qkv, L1_attn_W_proj, L1_attn_u_proj, L1_attn_sigma_proj), axis=-1)
    h = _layernorm(h + _L1_ffn_ref(h, L1_ffn_gate_w, L1_ffn_w1, L1_ffn_b1, L1_ffn_w2, L1_ffn_b2), axis=-1)
    h = _layernorm(h + _L2_attn_ref(h, L2_attn_Wq, L2_attn_bq, L2_attn_Wk, L2_attn_bk, L2_attn_Wv, L2_attn_bv, L2_attn_Wp, L2_attn_bp), axis=-1)
    h = _layernorm(h + _L2_ffn_ref(h, L2_ffn_ln1_w, L2_ffn_ln1_b, L2_ffn_ln2_w, L2_ffn_ln2_b, L2_ffn_conv_w, L2_ffn_attn_w, L2_ffn_proj_w, L2_ffn_router_w, L2_ffn_expert_wv, L2_ffn_expert_proj), axis=-1)
    h = _layernorm(h + _L3_attn_ref(h, L3_attn_ln1_w, L3_attn_ln1_b, L3_attn_q_w, L3_attn_q_b, L3_attn_k_w, L3_attn_k_b, L3_attn_v_w, L3_attn_v_b, L3_attn_o_w, L3_attn_o_b, L3_attn_ln2_w, L3_attn_ln2_b, L3_attn_fc_w, L3_attn_fc_b, L3_attn_proj_w, L3_attn_proj_b), axis=-1)
    h = _layernorm(h + _L3_ffn_ref(h, L3_ffn_W1, L3_ffn_b1, L3_ffn_W2, L3_ffn_b2), axis=-1)
    return h

_drawn_inputs = setup_inputs


def setup_inputs(seed=0):
    import zlib

    import numpy as np

    out = dict(_drawn_inputs(seed))
    spreads = {'L0_attn_b_beta': (2.0, 0.6),
     'L0_ffn_g1': (1.0, 0.6),
     'L0_ffn_g2': (1.0, 0.6),
     'L1_ffn_b1': (0.0, 0.8),
     'L1_ffn_b2': (0.0, 0.412),
     'L2_ffn_ln1_w': (1.0, 0.6),
     'L2_ffn_ln1_b': (0.0, 0.8),
     'L2_ffn_ln2_w': (1.0, 0.6),
     'L2_ffn_ln2_b': (0.0, 0.8),
     'L3_attn_ln1_w': (1.0, 0.6),
     'L3_attn_ln1_b': (0.0, 0.8),
     'L3_attn_q_b': (0.0, 0.8),
     'L3_attn_k_b': (0.0, 0.8),
     'L3_attn_v_b': (0.0, 0.8),
     'L3_attn_o_b': (0.0, 0.1),
     'L3_attn_ln2_w': (1.0, 0.6),
     'L3_attn_ln2_b': (0.0, 0.8),
     'L3_attn_fc_b': (0.0, 0.443),
     'L3_attn_proj_b': (0.0, 0.1)}
    factors = {'L0_attn_W_beta': 8.0,
     'L0_ffn_wq': 8.0,
     'L0_ffn_wk': 8.0,
     'L0_ffn_wv': 8.0,
     'L0_ffn_wo': 8.0,
     'L0_ffn_gate': 6.47,
     'L0_ffn_w1': 4.854,
     'L0_ffn_w2': 4.794,
     'L0_ffn_w3': 4.818,
     'L1_attn_u_qkv': 8.0,
     'L1_attn_u_proj': 8.0,
     'L2_attn_Wq': 8.0,
     'L2_attn_bq': 8.0,
     'L2_attn_Wk': 8.0,
     'L2_attn_bk': 64.0,
     'L2_attn_Wv': 8.0,
     'L2_attn_bv': 8.0,
     'L2_attn_Wp': 8.0,
     'L2_attn_bp': 3.076,
     'L2_ffn_conv_w': 8.0,
     'L2_ffn_attn_w': 8.0,
     'L2_ffn_proj_w': 8.0,
     'L2_ffn_router_w': 3.534,
     'L2_ffn_expert_wv': 3.02,
     'L2_ffn_expert_proj': 3.01,
     'L3_attn_q_w': 8.0,
     'L3_attn_k_w': 8.0,
     'L3_attn_v_w': 4.313,
     'L3_attn_o_w': 3.997,
     'L3_ffn_b1': 21.673,
     'L3_ffn_b2': 64.0}
    for name, (base, spread) in spreads.items():
        noise = np.random.default_rng([zlib.crc32(name.encode()), seed]).standard_normal(out[name].shape)
        drawn = base * np.exp(spread * noise) if base else spread * noise
        out[name] = jnp.asarray(drawn.astype(out[name].dtype))
    for name, factor in factors.items():
        out[name] = (out[name] * factor).astype(out[name].dtype)
    return out
```

```python
from contextlib import ExitStack

import numpy as np
import concourse.bass as bass
from concourse import mybir
from concourse.bass import ds

F32 = mybir.dt.float32
BF16 = mybir.dt.bfloat16
ALU = mybir.AluOpType
ACT = mybir.ActivationFunctionType
AX = mybir.AxisListType

P = 128
B, T, D = 4, 512, 256
KC = D // P
NT = B * T // P
TB = T // P
Q4 = 32


RETIRED = []
CLEAR_AT = 100


class Space:

    def __init__(self, nc, stack, name):
        self.nc, self.stack, self.name = nc, stack, name
        if len(RETIRED) > CLEAR_AT:
            nc.clear_and_free_semaphores(list(RETIRED))
            RETIRED.clear()
            nc.all_engine_barrier()

    def sb(self, name, shape, dt=F32):
        return self.stack.enter_context(self.nc.sbuf_tensor(f"{self.name}_{name}", shape, dt))

    def ps(self, name, shape, dt=F32):
        return self.stack.enter_context(self.nc.psum_tensor(f"{self.name}_{name}", shape, dt))

    def sem(self, name):
        made = self.nc.alloc_semaphore(name=f"{self.name}_{name}")
        self.stack.callback(RETIRED.append, made)
        return made


class Tally:

    def __init__(self, sem, base=0):
        self.sem, self.base, self.n = sem, base, 0

    def inc(self, ins):
        ins.then_inc(self.sem, 1)
        self.n += 1
        return self.n

    def wait(self, eng, n=None):
        eng.wait_ge(self.sem, self.base + (self.n if n is None else n))



def stage_tokens(nc, H, xk, wsT, wtok):
    NX = 4 * KC
    with ExitStack() as stack:
        s = Space(nc, stack, "tok")
        xg = [s.sb(f"xg{i}", [P, NX, T]) for i in range(2)]
        ws = s.sb("ws", [P, KC, D])
        wd = s.sb("wd", [P, 4, D])
        w2 = s.sb("w2", [P, NX, D])
        out = [s.ps(f"out{i}", [P, 2, 2, D]) for i in range(2)]
        w_loaded = s.sem("w_loaded")
        x_loaded = [s.sem(f"x_loaded{i}") for i in range(2)]
        w_ready = s.sem("w_ready")
        mm_done = s.sem("mm_done")
        out_free = s.sem("out_free")
        with nc.Block() as block:
            @block.sync
            def _(sp):
                sp.dma_start(ws[:], wsT.rearrange("c p o -> p c o")).then_inc(w_loaded, 16)
                sp.dma_start(wd[:], wtok.unsqueeze(0).to_broadcast([P, 4, D])).then_inc(w_loaded, 16)
                for b in range(B):
                    if b >= 2:
                        sp.wait_ge(mm_done, 2 * (b - 1))
                    sp.dma_start(xg[b % 2][:], xk[:, :, b * T:(b + 1) * T].rearrange("c p t -> p c t")) \
                        .then_inc(x_loaded[b % 2], 16)

            @block.vector
            def _(dve):
                dve.wait_ge(w_loaded, 32)
                for d in range(4):
                    dve.tensor_tensor(w2[:, KC * d:KC * d + KC, :], ws[:],
                                      wd[:, d:d + 1, :].to_broadcast([P, KC, D]), ALU.mult) \
                        .then_inc(w_ready, 1)

            @block.tensor
            def _(pe):
                pe.wait_ge(w_ready, 4)
                with pe.Fori(0, 2) as i:
                    for half in range(2):
                        pe.wait_ge(x_loaded[half], 16 * i + 16)
                        pe.wait_ge(out_free, 4 * i + 2 * half + 2)
                        for j in range(TB):
                            for c in range(NX):
                                mm = pe.matmul(out[half][:, j // 2, j % 2, :], xg[half][:, c, j * P:(j + 1) * P],
                                               w2[:, c, :], start=(c == 0), stop=(c == NX - 1))
                            if j % 2:
                                mm.then_inc(mm_done, 1)

            @block.scalar
            def _(act):
                act.sem_inc(out_free, 4)
                with act.Fori(0, 2) as i:
                    for half in range(2):
                        for u in range(2):
                            act.wait_ge(mm_done, 4 * i + 2 * half + u + 1)
                            act.activation(H[:, ds(8 * i + 4 * half + 2 * u, 2), :], out[half][:, u, :, :],
                                           ACT.Copy).then_inc(out_free, 1)



def stage_rows(nc, H, Y, XT, ident_d, post=None, second=None, w=None, b=None, out=None):
    with ExitStack() as stack:
        s = Space(nc, stack, "rows" + str(nc.next_id()))
        R = s.sb("R", [P, TB, D])
        S = s.sb("S", [P, TB, D])
        XN = s.sb("XN", [P, TB, D]) if second else R
        stats = s.sb("stats", [P, TB, 6])
        mv = s.sb("mv", [P, TB, 2])
        ms = s.sb("ms", [P, TB])
        sd = s.sb("sd", [P, TB])
        rstd = s.sb("rstd", [P, TB])
        epsc = s.sb("epsc", [P, 2])
        wb = s.sb("wb", [P, 2, D]) if w is not None else None
        ident = s.sb("ident", [P, P])
        tp = [s.ps(f"tp{i}", [P, KC, T]) for i in range(2)] if XT is not None else None
        w_loaded = s.sem("w_loaded")
        chain = s.sem("chain")
        stats_seen = s.sem("stats_seen")
        var_ready = s.sem("var_ready")
        sd_ready = s.sem("sd_ready")
        r_ready = s.sem("r_ready")
        r_copied = s.sem("r_copied")
        xn_ready = s.sem("xn_ready")
        turned = s.sem("turned")
        xt_copied = s.sem("xt_copied")
        stored = s.sem("stored")
        n_w = 1 + (w is not None) + (b is not None)
        norms = ([("ln", 1e-5)] if post == "ln" else []) + \
            ([(second, 1e-5 if second == "ln" else 1.1920928955078125e-07)] if second else [])
        NV = len(norms)
        keep = H if post == "ln" else Y if post == "add" else None
        with nc.Block() as block:
            @block.sync
            def _(sp):
                sp.dma_start(ident[:], ident_d).then_inc(w_loaded, 16)
                if w is not None:
                    sp.dma_start(wb[:, 0, :], w.unsqueeze(0).to_broadcast([P, D])).then_inc(w_loaded, 16)
                if b is not None:
                    sp.dma_start(wb[:, 1, :], b.unsqueeze(0).to_broadcast([P, D])).then_inc(w_loaded, 16)
                if out is not None:
                    for i in range(B):
                        sp.wait_ge(r_ready, i + 1)
                        sp.dma_start(out[i].rearrange("(j p) d -> p j d", p=P), R[:]).then_inc(stored, 16)
                    sp.wait_ge(stored, 16 * B)

            @block.vector
            def _(dve):
                for k, (_, eps) in enumerate(norms):
                    dve.memset(epsc[:, k:k + 1], eps).then_inc(chain, 1)
                dve.wait_ge(w_loaded, 16 * n_w)
                per = 0
                per += 1 if post else 0
                for kind, _ in norms:
                    per += 2 * TB + 1 + TB + (2 if kind == "rms" else 0)
                if w is not None:
                    per += 1 + (b is not None)
                with dve.Fori(0, B) as i:
                    c = Tally(chain, per * i + NV)

                    def norm(k, kind, src, dst):
                        for j in range(TB):
                            c.inc(dve.bn_stats(stats[:, j, :], src[:, j, :]))
                        c.wait(dve)
                        dve.sem_inc(stats_seen, 1)
                        for j in range(TB):
                            last = dve.bn_aggr(mv[:, j, :], stats[:, j, :])
                            c.inc(last)
                        if kind == "rms":
                            c.wait(dve)
                            c.inc(dve.tensor_tensor(ms[:], mv[:, :, 0], mv[:, :, 0], ALU.mult))
                            c.wait(dve)
                            c.inc(dve.tensor_tensor(ms[:], ms[:], mv[:, :, 1], ALU.add))
                        c.wait(dve)
                        dve.sem_inc(var_ready, 1)
                        dve.wait_ge(sd_ready, NV * i + k + 1)
                        c.inc(dve.reciprocal(rstd[:], sd[:]))
                        c.wait(dve)
                        for j in range(TB):
                            if kind == "rms":
                                c.inc(dve.tensor_scalar(dst[:, j, :], src[:, j, :], rstd[:, j:j + 1], None, ALU.mult))
                            else:
                                c.inc(dve.tensor_scalar(dst[:, j, :], src[:, j, :], mv[:, j, 0:1], rstd[:, j:j + 1],
                                                        ALU.subtract, ALU.mult))
                        c.wait(dve)

                    if XT is not None and not second:
                        dve.wait_ge(turned, i + 1)
                    if post:
                        if post == "add" or not norms:
                            dst = R
                        else:
                            dst = S
                        if keep is not None:
                            dve.wait_ge(r_copied, i + 1)
                        c.inc(dve.tensor_tensor(dst[:], H[:, ds(TB * i, TB), :], Y[:, ds(TB * i, TB), :], ALU.add))
                        c.wait(dve)
                        if post == "ln":
                            if out is not None:
                                dve.wait_ge(stored, 16 * i)
                            norm(0, "ln", S, R)
                        dve.sem_inc(r_ready, 1)
                    else:
                        dve.tensor_copy(R[:], H[:, ds(TB * i, TB), :]).then_inc(r_ready, 1)
                        dve.wait_ge(r_ready, i + 1)
                    if second:
                        dve.wait_ge(turned, i + 1)
                        norm(NV - 1, second, R, XN)
                        if w is not None:
                            c.inc(dve.tensor_tensor(XN[:], XN[:], wb[:, 0:1, :].to_broadcast([P, TB, D]), ALU.mult))
                            c.wait(dve)
                        if b is not None:
                            c.inc(dve.tensor_tensor(XN[:], XN[:], wb[:, 1:2, :].to_broadcast([P, TB, D]), ALU.add))
                            c.wait(dve)
                    dve.sem_inc(xn_ready, 1)

            @block.scalar
            def _(act):
                if NV:
                    act.wait_ge(chain, NV)
                if keep is not None:
                    act.sem_inc(r_copied, 1)
                act.sem_inc(xt_copied, 2)
                with act.Fori(0, B) as i:
                    for k, (kind, _) in enumerate(norms):
                        act.wait_ge(var_ready, NV * i + k + 1)
                        src = ms[:] if kind == "rms" else mv[:, :, 1]
                        act.activation(sd[:], src, ACT.Sqrt, bias=epsc[:, k:k + 1]).then_inc(sd_ready, 1)
                    if keep is not None:
                        act.wait_ge(r_ready, i + 1)
                        act.activation(keep[:, ds(TB * i, TB), :], R[:], ACT.Copy).then_inc(r_copied, 1)
                    if XT is not None:
                        act.wait_ge(turned, i + 2)
                        for k in range(KC):
                            act.activation(XT[:, k, ds(T * i, T)], tp[0][:, k, :], ACT.Copy).then_inc(xt_copied, 1)

            @block.tensor
            def _(pe):
                if XT is None:
                    return
                pe.wait_ge(w_loaded, 16 * n_w)
                pe.sem_inc(turned, 1)
                with pe.Fori(0, B) as i:
                    pe.wait_ge(xn_ready, i + 1)
                    pe.wait_ge(xt_copied, KC * i + KC)
                    for j in range(TB):
                        for k in range(KC):
                            last = pe.transpose(tp[0][:, k, j * P:(j + 1) * P], XN[:, j, k * P:(k + 1) * P], ident[:])
                    last.then_inc(turned, 1)



HN, HD = 8, 32
TL = 16
TH = T // TL


def stage_cell_inputs(nc, XT, KN, QR, V, BT, w_in, w_kq, w_vb, b_beta):
    with ExitStack() as stack:
        s = Space(nc, stack, "ci")
        XP = s.sb("XP", [P, KC, B * T])
        wi = s.sb("wi", [P, KC, D])
        wkq = s.sb("wkq", [P, KC, 2 * D])
        wvb = s.sb("wvb", [P, HN, KC, 2 * HD])
        wh = [s.sb(f"wh{i}", [P, KC, 2 * HD]) for i in range(2)]
        bb = s.sb("bb", [P, HN])
        xs = [s.sb(f"xs{i}", [P, KC, P]) for i in range(4)]
        sq = [s.sb(f"sq{i}", [P, D]) for i in range(4)]
        ss = s.sb("ss", [P, TL * HN])
        nrm = s.sb("nrm", [P, TL * HN])
        bank = [s.ps(f"bank{i}", [P, 512]) for i in range(8)]
        loaded = s.sem("loaded")
        xp_mm = s.sem("xp_mm")
        xp_ready = s.sem("xp_ready")
        xs_ready = s.sem("xs_ready")
        kq_mm = s.sem("kq_mm")
        k_copied = s.sem("k_copied")
        q_copied = s.sem("q_copied")
        sq_ready = s.sem("sq_ready")
        ss_ready = s.sem("ss_ready")
        nrm_ready = s.sem("nrm_ready")
        inv = s.sem("inv")
        wh_ready = s.sem("wh_ready")
        vb_mm = s.sem("vb_mm")
        vb_copied = s.sem("vb_copied")
        with nc.Block() as block:
            @block.sync
            def _(sp):
                sp.dma_start(wi[:], w_in.rearrange("c p o -> p c o")).then_inc(loaded, 16)
                sp.dma_start(wkq[:], w_kq.rearrange("c p o -> p c o")).then_inc(loaded, 16)
                sp.dma_start(wvb[:], w_vb.rearrange("h p c o -> p h c o")).then_inc(loaded, 16)
                sp.dma_start(bb[:], b_beta).then_inc(loaded, 16)

            @block.tensor
            def _(pe):
                pe.wait_ge(loaded, 64)
                with pe.Fori(0, B) as b:
                    for e in range(KC):
                        pe.wait_ge(xp_ready, KC * b + e + 1)
                        for k in range(KC):
                            mm = pe.matmul(bank[e][:], wi[:, k, e * P:(e + 1) * P], XT[:, k, ds(b * T, T)],
                                           start=(k == 0), stop=(k == KC - 1))
                        mm.then_inc(xp_mm, 1)
                with pe.Fori(0, TL // 4) as i:
                    for u in range(4):
                        pe.wait_ge(xs_ready, 4 * i + u + 1)
                        pe.wait_ge(k_copied, 4 * i + u + 1)
                        pe.wait_ge(q_copied, 4 * i + u + 1)
                        pe.wait_ge(sq_ready, 4 * i + u + 1)
                        for k in range(KC):
                            mm = pe.matmul(bank[2 + u][:], xs[u][:, k, :], wkq[:, k, :],
                                           start=(k == 0), stop=(k == KC - 1))
                        mm.then_inc(kq_mm, 1)
                with pe.Fori(0, HN // 2) as i:
                    for u in range(2):
                        pe.wait_ge(wh_ready, 2 * i + u + 1)
                        for ty in range(2):
                            pe.wait_ge(vb_copied, 4 * i + 2 * u + ty + 1)
                            for b in range(B):
                                for k in range(KC):
                                    mm = pe.matmul(bank[2 * ty + u][Q4 * b:Q4 * b + Q4, :],
                                                   wh[u][:, k, ty * HD:(ty + 1) * HD], XP[:, k, b * T:(b + 1) * T],
                                                   start=(k == 0), stop=(k == KC - 1))
                            mm.then_inc(vb_mm, 1)

            @block.scalar
            def _(act):
                act.sem_inc(xp_ready, 2)
                with act.Fori(0, B) as b:
                    for e in range(KC):
                        act.wait_ge(xp_mm, KC * b + e + 1)
                        act.activation(XP[:, e, ds(b * T, T)], bank[e][:], ACT.Silu).then_inc(xp_ready, 1)
                act.sem_inc(q_copied, 4)
                act.sem_inc(sq_ready, 4)
                with act.Fori(0, TL // 4) as i:
                    for u in range(4):
                        act.wait_ge(kq_mm, 4 * i + u + 1)
                        act.wait_ge(ss_ready, 4 * i + u + 1)
                        act.activation(sq[u][:], bank[2 + u][:, 0:D], ACT.Square).then_inc(sq_ready, 1)
                        act.activation(QR[:, ds(4 * i + u, 1), :], bank[2 + u][:, D:2 * D], ACT.Copy) \
                            .then_inc(q_copied, 1)
                act.wait_ge(ss_ready, 4 + TL)
                act.activation(nrm[:], ss[:], ACT.Sqrt).then_inc(nrm_ready, 1)
                act.sem_inc(vb_copied, 4)
                with act.Fori(0, HN // 2) as i:
                    for u in range(2):
                        act.wait_ge(vb_mm, 4 * i + 2 * u + 1)
                        act.activation(V[:, ds(2 * i + u, 1), :], bank[u][:], ACT.Copy).then_inc(vb_copied, 1)
                        act.wait_ge(vb_mm, 4 * i + 2 * u + 2)
                        act.activation(BT[:, ds(2 * i + u, 1), :], bank[2 + u][:], ACT.Sigmoid,
                                       bias=bb[:, ds(2 * i + u, 1)]).then_inc(vb_copied, 1)

            @block.vector
            def _(dve):
                dve.sem_inc(k_copied, 4)
                dve.sem_inc(ss_ready, 4)
                dve.wait_ge(xp_ready, 2 + KC * B)
                xpv = XP[:].rearrange("p k (n l) -> p k n l", l=TL)
                with dve.Fori(0, TL // 4) as i:
                    for u in range(4):
                        dve.wait_ge(sq_ready, 4 * i + u + 1)
                        dve.tensor_copy(xs[u][:], xpv[:, :, :, ds(4 * i + u, 1)]).then_inc(xs_ready, 1)
                    for u in range(4):
                        dve.wait_ge(q_copied, 4 * i + u + 5)
                        dve.tensor_copy(KN[:, ds(4 * i + u, 1), :], bank[2 + u][:, 0:D]).then_inc(k_copied, 1)
                        dve.wait_ge(sq_ready, 4 * i + u + 5)
                        dve.tensor_reduce(ss[:, ds(HN * (4 * i + u), HN)],
                                          sq[u][:].rearrange("p (h j) -> p h j", h=HN), AX.X, ALU.add) \
                            .then_inc(ss_ready, 1)
                dve.wait_ge(loaded, 64)
                dve.wait_ge(k_copied, 4 + TL)
                dve.wait_ge(nrm_ready, 1)
                dve.tensor_scalar(nrm[:], nrm[:], 1e-6, None, ALU.add).then_inc(inv, 1)
                dve.wait_ge(inv, 1)
                dve.reciprocal(ss[:], nrm[:]).then_inc(inv, 1)
                dve.wait_ge(inv, 2)
                knv = KN[:].rearrange("p l (h j) -> p (l h) j", h=HN)
                dve.tensor_tensor(knv, knv, ss[:].unsqueeze(2).to_broadcast([P, TL * HN, HD]), ALU.mult) \
                    .then_inc(inv, 1)

            @block.gpsimd
            def _(pool):
                pool.wait_ge(loaded, 64)
                with pool.Fori(0, HN // 2) as i:
                    for u in range(2):
                        if u == 0:
                            pool.wait_ge(vb_copied, 4 * i + 1)
                        pool.wait_ge(vb_copied, 4 * i + 2 * u + 1)
                        pool.wait_ge(vb_copied, 4 * i + 2 * u + 2)
                        pool.tensor_copy(wh[u][:], wvb[:, ds(2 * i + u, 1), :, :]).then_inc(wh_ready, 1)


def stage_cell(nc, KN, QR, V, BT, OUT, ident_d):
    NCH = 2
    CH = HN // NCH
    CW = CH * HD
    with ExitStack() as stack:
        s = Space(nc, stack, "cell")
        ident = s.sb("ident", [P, P])
        sel = s.sb("sel", [P, P])
        S = [s.sb(f"S{i}", [P, NCH, CW]) for i in range(2)]
        T1 = s.sb("T1", [P, NCH, CW])
        T2 = s.sb("T2", [P, NCH, CW])
        T3 = s.sb("T3", [P, NCH, CW])
        BS = s.sb("BS", [P, NCH, CW])
        R = s.sb("R", [P, NCH, CH])
        DL = s.sb("DL", [P, NCH, CH])
        QB = [s.sb(f"QB{i}", [P, 2, NCH, CW]) for i in range(2)]
        SQ = s.sb("SQ", [P, TL, NCH, CW])
        kb = [s.ps(f"kb{i}", [P, 2, NCH, CW]) for i in range(4)]
        qb = [s.ps(f"qb{i}", [P, 2, NCH, CW]) for i in range(2)]
        loaded = s.sem("loaded")
        sel_ready = s.sem("sel_ready")
        kb_ready = s.sem("kb_ready")
        qb_ready = s.sem("qb_ready")
        qb_copied = s.sem("qb_copied")
        sk_done = s.sem("sk_done")
        r_done = s.sem("r_done")
        delta_done = s.sem("delta_done")
        outer_done = s.sem("outer_done")
        sum_done = s.sem("sum_done")
        state_ready = s.sem("state_ready")
        bs_ready = s.sem("bs_ready")
        sq_done = s.sem("sq_done")
        out_done = s.sem("out_done")
        NP = TL // 2
        h4 = lambda ap: ap.rearrange("p (h j) -> p h j", h=CH)
        with nc.Block() as block:
            @block.sync
            def _(sp):
                sp.dma_start(ident[:], ident_d).then_inc(loaded, 16)

            @block.tensor
            def _(pe):
                with pe.Fori(0, TH) as i:
                    pe.wait_ge(sel_ready, i + 1)
                    for pp in range(NP):
                        pe.wait_ge(outer_done, 4 * (NP * i + pp) + 4)
                        pe.matmul(kb[pp % 4][:], sel[:], KN[:, 2 * pp:2 * pp + 2, :],
                                  start=True, stop=True).then_inc(kb_ready, 1)
                        pe.wait_ge(qb_copied, 2 * (NP * i + pp) + 2)
                        pe.matmul(qb[pp % 2][:], sel[:], QR[:, 2 * pp:2 * pp + 2, :],
                                  start=True, stop=True).then_inc(qb_ready, 1)

            @block.vector
            def _(dve):
                dve.memset(S[1][:], 0.0).then_inc(state_ready, 2)
                dve.sem_inc(outer_done, 16)
                dve.sem_inc(out_done, NP)
                with dve.Fori(0, TH) as i:
                    def reduce_out(pp):
                        dve.wait_ge(sq_done, 2 * TL * i + 8 + 4 * pp + 4)
                        dve.tensor_reduce(OUT[:, ds(TL * i + 2 * pp, 2), :],
                                          SQ[:, 2 * pp:2 * pp + 2, :, :].rearrange("p t c (h j) -> p t (c h) j", h=CH),
                                          AX.X, ALU.add).then_inc(out_done, 1)

                    for t in range(TL):
                        if t % 2 == 0:
                            dve.wait_ge(kb_ready, NP * i + t // 2 + 1)
                        kt = kb[(t // 2) % 4]
                        for c in range(NCH):
                            n = 2 * TL * i + 2 * t + c + 1
                            dve.wait_ge(state_ready, n)
                            dve.tensor_tensor(T1[:, c, :], S[(t + 1) % 2][:, c, :], kt[:, t % 2, c, :], ALU.mult) \
                                .then_inc(sk_done, 1)
                            dve.wait_ge(sk_done, n)
                            dve.tensor_reduce(R[:, c, :], h4(T1[:, c, :]), AX.X, ALU.add).then_inc(r_done, 1)
                            dve.wait_ge(r_done, n)
                            dve.tensor_tensor(DL[:, c, :], V[:, c * CH:(c + 1) * CH, ds(TL * i + t, 1)],
                                              R[:, c, :], ALU.subtract).then_inc(delta_done, 1)
                            dve.wait_ge(delta_done, n)
                            dve.tensor_tensor(h4(T2[:, c, :]), DL[:, c, :].unsqueeze(2).to_broadcast([P, CH, HD]),
                                              h4(kt[:, t % 2, c, :]), ALU.mult).then_inc(outer_done, 1)
                            dve.wait_ge(outer_done, n + 16)
                            dve.wait_ge(bs_ready, n)
                            dve.tensor_tensor(T3[:, c, :], T2[:, c, :], BS[:, c, :], ALU.add).then_inc(sum_done, 1)
                        if t % 2 == 1 and t >= 3:
                            reduce_out((t - 3) // 2)
                    reduce_out(NP - 1)

            @block.scalar
            def _(act):
                act.wait_ge(loaded, 16)
                act.sem_inc(qb_copied, 4)
                rows = ident[:].rearrange("p (b t) -> p b t", b=B)
                with act.Fori(0, TH) as i:
                    def copy_queries(pp, c):
                        act.wait_ge(qb_ready, NP * i + pp + 1)
                        act.wait_ge(sq_done, 2 * TL * i + 4 * pp + 4)
                        act.activation(QB[pp % 2][:, :, c, :], qb[pp % 2][:, :, c, :], ACT.Copy) \
                            .then_inc(qb_copied, 1)

                    act.wait_ge(qb_copied, 2 * NP * i + 4)
                    act.activation(sel[:].rearrange("p (b t) -> p b t", b=B),
                                   rows[:, :, ds(i, 1)].to_broadcast([P, B, Q4]), ACT.Copy).then_inc(sel_ready, 1)
                    copy_queries(0, 0)
                    copy_queries(0, 1)
                    for t in range(TL):
                        for c in range(NCH):
                            n = 2 * TL * i + 2 * t + c + 1
                            act.wait_ge(sum_done, n)
                            act.wait_ge(sq_done, n + 4)
                            act.activation(S[t % 2][:, c, :], T3[:, c, :], ACT.Tanh).then_inc(state_ready, 1)
                            if t % 2 == 1 and t < TL - 1:
                                copy_queries(t // 2 + 1, c)

            @block.gpsimd
            def _(pool):
                pool.sem_inc(sq_done, 8)
                with pool.Fori(0, TH) as i:
                    def query(t, c):
                        if t % 2 == 0:
                            pool.wait_ge(qb_copied, 2 * (NP * i + t // 2) + 4 + 2)
                            pool.wait_ge(out_done, NP * i + t // 2 + 1)
                        pool.tensor_tensor(SQ[:, t, c, :], S[t % 2][:, c, :], QB[(t // 2) % 2][:, t % 2, c, :],
                                           ALU.mult).then_inc(sq_done, 1)

                    for t in range(TL):
                        for c in range(NCH):
                            n = 2 * TL * i + 2 * t + c + 1
                            pool.wait_ge(state_ready, n)
                            pool.wait_ge(outer_done, n + 14)
                            pool.tensor_tensor(h4(BS[:, c, :]), h4(S[(t + 1) % 2][:, c, :]),
                                               BT[:, c * CH:(c + 1) * CH, ds(TL * i + t, 1)].to_broadcast([P, CH, HD]),
                                               ALU.mult).then_inc(bs_ready, 1)
                            if t:
                                query(t - 1, c)
                    for c in range(NCH):
                        pool.wait_ge(state_ready, 2 * TL * i + 2 * TL + c + 1)
                        query(TL - 1, c)


def stage_cell_out(nc, OUT, Y, w_out):
    with ExitStack() as stack:
        s = Space(nc, stack, "co")
        wo = s.sb("wo", [P, HN, D])
        si = s.sb("si", [P, HN, P])
        cc = s.sb("cc", [P, HN, P])
        y = [s.ps(f"y{i}", [P, 512]) for i in range(B)]
        loaded = s.sem("loaded")
        si_ready = s.sem("si_ready")
        cc_ready = s.sem("cc_ready")
        mm_done = s.sem("mm_done")
        copied = s.sem("copied")
        with nc.Block() as block:
            @block.sync
            def _(sp):
                sp.dma_start(wo[:], w_out).then_inc(loaded, 16)

            @block.scalar
            def _(act):
                act.sem_inc(copied, B)
                with act.Fori(0, TB) as j:
                    act.wait_ge(cc_ready, j + 1)
                    act.activation(si[:], OUT[:, ds(P * j, P), :].rearrange("p t h -> p h t"), ACT.Silu) \
                        .then_inc(si_ready, 1)
                    for b in range(B):
                        act.wait_ge(mm_done, B * j + b + 1)
                        act.activation(Y[:, ds(j + TB * b, 1), :], y[b][:, 0:D], ACT.Copy).then_inc(copied, 1)

            @block.vector
            def _(dve):
                dve.sem_inc(cc_ready, 1)
                with dve.Fori(0, TB) as j:
                    dve.wait_ge(si_ready, j + 1)
                    dve.wait_ge(copied, B * j + B)
                    dve.tensor_tensor(cc[:], si[:], OUT[:, ds(P * j, P), :].rearrange("p t h -> p h t"), ALU.mult) \
                        .then_inc(cc_ready, 1)

            @block.tensor
            def _(pe):
                pe.wait_ge(loaded, 16)
                with pe.Fori(0, TB) as j:
                    pe.wait_ge(cc_ready, j + 2)
                    pe.wait_ge(copied, B * j + B)
                    for b in range(B):
                        q = slice(Q4 * b, Q4 * b + Q4)
                        for h in range(HN):
                            mm = pe.matmul(y[b][:, 0:D], cc[q, h, :], wo[q, h, :], start=(h == 0), stop=(h == HN - 1))
                        mm.then_inc(mm_done, 1)



AH = 16
AD = D // AH
AG = 4
NG = AH // AG
ONE = AD


def stage_attention(nc, XT, Y, ident_d, w, bias_cols, causal, rope=None, out_bias=None):
    NPJ = 5 if rope is not None else 3
    NU = 2 * TB
    with ExitStack() as stack:
        s = Space(nc, stack, "at" + str(nc.next_id()))
        AOT = s.sb("AOT", [AG * AD, NG, B * T])
        with ExitStack() as inner:
            z = Space(nc, inner, s.name + "a")
            ident = z.sb("ident", [P, P])
            identb = z.sb("identb", [P, P], BF16)
            mask = z.sb("mask", [P, T], BF16)
            maskt = z.sb("maskt", [P, T], BF16)
            bc = z.sb("bc", [P, 3, NG])
            cs = z.sb("cs", [P, 2, T]) if rope is not None else None
            names = ["q", "k", "v"] + (["qr", "kr"] if rope is not None else [])
            ws = {n: z.sb("ws_" + n, [P, KC, P]) for n in names}
            QT = z.sb("QT", [P, T])
            KT = z.sb("KT", [P, T])
            VT = z.sb("VT", [P, T])
            RA = z.sb("RA", [P, T])
            RB = z.sb("RB", [P, T])
            VS = z.sb("VS", [P, TB, AG, Q4])
            MP = z.sb("MP", [P, TB, AG, Q4])
            EX = z.sb("EX", [P, TB, AG, T])
            RI = z.sb("RI", [P, TB * AG])
            OS = z.sb("OS", [P, TB, AG, AD])
            pj = [z.ps(f"pj{i}", [P, T]) for i in range(2)]
            misc = z.ps("misc", [P, TB, P])
            ob = z.ps("ob", [P, TB, AG, Q4])
            un = [z.ps(f"un{i}", [P, 2, T]) for i in range(2)]
            loaded = z.sem("loaded")
            mask_zero = z.sem("mask_zero")
            mask_ready = z.sem("mask_ready")
            identb_ready = z.sem("identb_ready")
            pe_passed = z.sem("pe_passed")
            w_ready = z.sem("w_ready")
            proj_mm = z.sem("proj_mm")
            p_free = [z.sem(f"p_free{i}") for i in range(2)]
            rot = z.sem("rot")
            qt_ready = z.sem("qt_ready")
            kt_ready = z.sem("kt_ready")
            vt_ready = z.sem("vt_ready")
            misc_full = z.sem("misc_full")
            v_copied = z.sem("v_copied")
            o_copied = z.sem("o_copied")
            a_mm = z.sem("a_mm")
            a_max = z.sem("a_max")
            b_mm = z.sem("b_mm")
            b_exp = z.sem("b_exp")
            shifted = z.sem("shifted")
            pv_mm = z.sem("pv_mm")
            ri_ready = z.sem("ri_ready")
            os_ready = z.sem("os_ready")
            mp_zero = z.sem("mp_zero")
            n_load = 2 + (cs is not None)
            with nc.Block() as block:
                @block.sync
                def _(sp):
                    sp.dma_start(ident[:], ident_d).then_inc(loaded, 16)
                    sp.dma_start(bc[:], bias_cols).then_inc(loaded, 16)
                    if cs is not None:
                        sp.dma_start(cs[:], rope).then_inc(loaded, 16)

                @block.gpsimd
                def _(pool):
                    pool.memset(MP[:], 0.0).then_inc(mp_zero, 1)
                    if causal:
                        pool.memset(mask[:], 0.0).then_inc(mask_zero, 1)
                        pool.wait_ge(mask_zero, 1)
                        pool.affine_select(out=mask[:, T - P:T], in_=mask[:, T - P:T], compare_op=ALU.is_ge,
                                           fill=-1e30, base=0, pattern=[[-1, P]], channel_multiplier=1) \
                            .then_inc(mask_ready, 1)
                        pool.memset(maskt[:], 0.0).then_inc(mask_zero, 1)
                        pool.wait_ge(mask_zero, 2)
                        pool.affine_select(out=maskt[:, 0:P], in_=maskt[:, 0:P], compare_op=ALU.is_ge,
                                           fill=-1e30, base=0, pattern=[[1, P]], channel_multiplier=-1) \
                            .then_inc(mask_ready, 1)
                    with pool.Fori(0, NG) as hg:
                        pool.wait_ge(proj_mm, NPJ * B * hg + 1)
                        for n in names:
                            last = pool.tensor_copy(ws[n][:], w[n][:, :, ds(hg, 1), :])
                        last.then_inc(w_ready, 1)
                @block.tensor
                def _(pe):
                    pe.wait_ge(loaded, 16 * n_load)
                    pe.sem_inc(proj_mm, 1)
                    pe.sem_inc(misc_full, 1)
                    if causal:
                        pe.wait_ge(mask_ready, 2)
                        pe.wait_ge(identb_ready, 1)
                    with pe.Fori(0, NG) as hg:
                        pe.wait_ge(w_ready, hg + 1)
                        pe.sem_inc(pe_passed, 1)
                        with pe.Fori(0, B) as b:
                            g = B * hg + b
                            order = ["q", "qr", "k", "kr", "v"] if cs is not None else ["q", "k", "v"]
                            uses = [0, 0]
                            per = [(NPJ + 1) // 2, NPJ // 2]
                            for m, n in enumerate(order):
                                f = m % 2
                                pe.wait_ge(p_free[f], per[f] * g + uses[f] + 1)
                                uses[f] += 1
                                for k in range(KC):
                                    mm = pe.matmul(pj[f][:], ws[n][:, k, :], XT[:, k, ds(b * T, T)],
                                                   start=(k == 0), stop=(k == KC - 1))
                                mm.then_inc(proj_mm, 1)
                            pe.wait_ge(vt_ready, g + 1)
                            pe.wait_ge(o_copied, g + 1)
                            for j in range(TB):
                                mm = pe.transpose(misc[:, j, :], VT[:, j * P:(j + 1) * P], ident[:])
                            mm.then_inc(misc_full, 1)
                            pe.wait_ge(qt_ready, g + 1)
                            pe.wait_ge(kt_ready, g + 1)
                            for qt in range(TB):
                                nk = (qt + 1) * P if causal else T
                                for hp in range(2):
                                    u = 2 * qt + hp
                                    if u < 2:
                                        pe.wait_ge(b_exp, NU * g + 1)
                                    else:
                                        pe.wait_ge(a_max, NU * g + u - 1)
                                    if causal:
                                        for h in range(2):
                                            pe.matmul(un[u % 2][:, h, 0:nk], identb[:], mask[:, T - nk:T],
                                                      start=True, stop=False)
                                    for h in range(2):
                                        r = slice(Q4 * (2 * hp + h), Q4 * (2 * hp + h) + Q4)
                                        mm = pe.matmul(un[u % 2][:, h, 0:nk], QT[r, qt * P:(qt + 1) * P], KT[r, 0:nk],
                                                       start=not causal, stop=True)
                                    mm.then_inc(a_mm, 1)
                            pe.wait_ge(a_max, NU * g + NU)
                            pe.wait_ge(v_copied, g + 1)
                            for qt in range(TB):
                                mm = pe.transpose(misc[:, qt, :], MP[:, qt, :, :].rearrange("p h c -> p (h c)"),
                                                  ident[:])
                            mm.then_inc(misc_full, 1)
                            pe.wait_ge(shifted, g + 1)
                            for kt in range(TB):
                                q0 = kt * P if causal else 0
                                for hp in range(2):
                                    u = 2 * kt + hp
                                    if u >= 2:
                                        pe.wait_ge(b_exp, NU * g + u)
                                    if causal:
                                        for h in range(2):
                                            pe.matmul(un[u % 2][:, h, q0:T], identb[:], maskt[:, 0:T - q0],
                                                      start=True, stop=False)
                                    for h in range(2):
                                        r = slice(Q4 * (2 * hp + h), Q4 * (2 * hp + h) + Q4)
                                        mm = pe.matmul(un[u % 2][:, h, q0:T], KT[r, kt * P:(kt + 1) * P], QT[r, q0:T],
                                                       start=not causal, stop=True)
                                    mm.then_inc(b_mm, 1)
                            pe.wait_ge(os_ready, g + 1)
                            pe.wait_ge(b_exp, NU * g + NU + 1)
                            for qt in range(TB):
                                nk = qt + 1 if causal else TB
                                for h in range(AG):
                                    for kt in range(nk):
                                        mm = pe.matmul(ob[:, qt, h, 0:AD + 1], EX[:, kt, h, qt * P:(qt + 1) * P],
                                                       VS[:, kt, h, 0:AD + 1], start=(kt == 0), stop=(kt == nk - 1))
                            mm.then_inc(pv_mm, 1)
                            pe.wait_ge(os_ready, g + 2)
                            pe.sem_inc(pe_passed, 1)
                            for qt in range(TB):
                                mm = pe.transpose(misc[0:AG * AD, qt, :], OS[:, qt, :, :].rearrange("p h c -> p (h c)"),
                                                  ident[:])
                            mm.then_inc(misc_full, 1)

                @block.scalar
                def _(act):
                    act.wait_ge(loaded, 16 * n_load)
                    act.activation(identb[:], ident[:], ACT.Copy).then_inc(identb_ready, 1)
                    act.sem_inc(b_exp, 1)
                    act.sem_inc(o_copied, 1)
                    if cs is None:
                        act.sem_inc(p_free[0], 1)
                        act.sem_inc(p_free[1], 1)
                    with act.Fori(0, NG) as hg:
                        with act.Fori(0, B) as b:
                            g = B * hg + b
                            if cs is None:
                                act.wait_ge(proj_mm, NPJ * g + 2)
                                act.activation(QT[:], pj[0][:], ACT.Identity, bias=bc[:, 0, ds(hg, 1)]) \
                                    .then_inc(qt_ready, 1)
                                act.wait_ge(proj_mm, NPJ * g + 3)
                                act.activation(KT[:], pj[1][:], ACT.Identity, bias=bc[:, 1, ds(hg, 1)]) \
                                    .then_inc(kt_ready, 1)
                                act.wait_ge(qt_ready, g + 1)
                                act.sem_inc(p_free[0], 1)
                                act.wait_ge(kt_ready, g + 1)
                                act.sem_inc(p_free[1], 1)
                            act.wait_ge(proj_mm, NPJ * g + NPJ + 1)
                            act.activation(VT[:], pj[0][:], ACT.Identity, bias=bc[:, 2, ds(hg, 1)]) \
                                .then_inc(vt_ready, 1)
                            act.wait_ge(vt_ready, g + 1)
                            act.sem_inc(p_free[0], 1)
                            act.wait_ge(misc_full, 3 * g + 2)
                            act.activation(VS[:].rearrange("p j h c -> p j (h c)"), misc[:], ACT.Copy) \
                                .then_inc(v_copied, 1)
                            act.wait_ge(os_ready, g + 1)
                            for kt in range(TB):
                                q0 = kt * P if causal else 0
                                for hp in range(2):
                                    act.wait_ge(b_mm, NU * g + 2 * kt + hp + 1)
                                    act.activation(EX[:, kt, 2 * hp:2 * hp + 2, q0:T], un[hp][:, :, q0:T], ACT.Exp,
                                                   scale=AD ** -0.5).then_inc(b_exp, 1)
                            act.wait_ge(misc_full, 3 * g + 4)
                            act.activation(AOT[:, ds(hg, 1), ds(b * T, T)],
                                           misc[0:AG * AD, :, :].rearrange("p j t -> p (j t)"), ACT.Copy) \
                                .then_inc(o_copied, 1)

                @block.vector
                def _(dve):
                    dve.wait_ge(loaded, 16 * n_load)
                    dve.wait_ge(mp_zero, 1)
                    dve.sem_inc(os_ready, 1)
                    if cs is not None:
                        dve.sem_inc(p_free[0], 1)
                        dve.sem_inc(p_free[1], 1)
                    with dve.Fori(0, NG) as hg:
                        with dve.Fori(0, B) as b:
                            g = B * hg + b
                            if cs is not None:
                                for n, (dst, ready) in enumerate(((QT, qt_ready), (KT, kt_ready))):
                                    dve.wait_ge(proj_mm, NPJ * g + 2 * n + 2)
                                    dve.scalar_tensor_tensor(RA[:], pj[0][:], bc[:, n, 0:1], cs[:, 0, :],
                                                             ALU.add, ALU.mult).then_inc(p_free[0], 1)
                                    dve.wait_ge(proj_mm, NPJ * g + 2 * n + 3)
                                    dve.tensor_tensor(RB[:], pj[1][:], cs[:, 1, :], ALU.mult).then_inc(p_free[1], 1)
                                    dve.wait_ge(p_free[0], 3 * g + n + 2)
                                    dve.wait_ge(p_free[1], 2 * g + n + 2)
                                    dve.tensor_tensor(dst[:], RA[:], RB[:], ALU.add).then_inc(ready, 1)
                                    dve.wait_ge(ready, g + 1)
                            for qt in range(TB):
                                nk = (qt + 1) * P if causal else T
                                for hp in range(2):
                                    u = 2 * qt + hp
                                    dve.wait_ge(a_mm, NU * g + u + 1)
                                    dve.tensor_reduce(MP[:, qt, 2 * hp:2 * hp + 2, ONE], un[u % 2][:, :, 0:nk],
                                                      AX.X, ALU.max, negate=True).then_inc(a_max, 1)
                            dve.wait_ge(misc_full, 3 * g + 3)
                            dve.tensor_tensor(QT[:], QT[:], misc[:].rearrange("p j t -> p (j t)"), ALU.add) \
                                .then_inc(shifted, 1)
                            dve.wait_ge(pv_mm, g + 1)
                            dve.reciprocal(RI[:], ob[:, :, :, ONE].rearrange("p j h -> p (j h)")) \
                                .then_inc(ri_ready, 1)
                            dve.wait_ge(ri_ready, g + 1)
                            dve.tensor_tensor(OS[:].rearrange("p j h c -> p (j h) c"),
                                              ob[:, :, :, 0:AD].rearrange("p j h c -> p (j h) c"),
                                              RI[:].unsqueeze(2).to_broadcast([P, TB * AG, AD]), ALU.mult) \
                                .then_inc(os_ready, 1)
        ot = s.sb("ot", [AG * AD, NG, T])
        bo = s.sb("bo", [P, D])
        yb = [s.ps(f"yb{i}", [P, 2, D]) for i in range(2)]
        bo_loaded = s.sem("bo_loaded")
        ot_ready = s.sem("ot_ready")
        y_mm = s.sem("y_mm")
        y_copied = s.sem("y_copied")
        with nc.Block() as block:
            @block.sync
            def _(sp):
                if out_bias is not None:
                    sp.dma_start(bo[:], out_bias.unsqueeze(0).to_broadcast([P, D])).then_inc(bo_loaded, 16)

            @block.scalar
            def _(act):
                with act.Fori(0, B) as b:
                    act.wait_ge(y_copied, 2 * b + 2)
                    act.activation(ot[:], AOT[:, :, ds(b * T, T)], ACT.Copy).then_inc(ot_ready, 1)

            @block.tensor
            def _(pe):
                with pe.Fori(0, B) as b:
                    pe.wait_ge(ot_ready, b + 1)
                    for j in range(TB):
                        if j % 2 == 0:
                            pe.wait_ge(y_copied, 2 * b + j // 2 + 1)
                        for g in range(NG):
                            mm = pe.matmul(yb[j // 2][:, j % 2, :], ot[:, g, j * P:(j + 1) * P], w["o"][:, g, :],
                                           start=(g == 0), stop=(g == NG - 1))
                        if j % 2:
                            mm.then_inc(y_mm, 1)

            @block.vector
            def _(dve):
                dve.sem_inc(y_copied, 2)
                if out_bias is not None:
                    dve.wait_ge(bo_loaded, 16)
                with dve.Fori(0, B) as b:
                    for f in range(2):
                        dve.wait_ge(y_mm, 2 * b + f + 1)
                        dst = Y[:, ds(TB * b + 2 * f, 2), :]
                        if out_bias is None:
                            dve.tensor_copy(dst, yb[f][:]).then_inc(y_copied, 1)
                        else:
                            dve.tensor_tensor(dst, yb[f][:], bo[:].unsqueeze(1).to_broadcast([P, 2, D]), ALU.add) \
                                .then_inc(y_copied, 1)



def stage_router(nc, XT, COMB, ident_d, gate_d, E, top, weight):
    with ExitStack() as stack:
        s = Space(nc, stack, "ro" + str(nc.next_id()))
        ident = s.sb("ident", [P, P])
        gate = s.sb("gate", [P, KC, E])
        lt = s.sb("lt", [E, T])
        LG = s.sb("LG", [P, NT, E])
        PR = s.sb("PR", [P, NT, E])
        EQ = s.sb("EQ", [P, NT, E])
        IO = s.sb("IO", [P, NT, E])
        KEY = s.sb("KEY", [P, NT, E])
        MX = s.sb("MX", [P, NT])
        SM = s.sb("SM", [P, NT])
        lo = s.ps("lo", [P, T])
        tp = s.ps("tp", [P, TB, P])
        loaded = s.sem("loaded")
        iota = s.sem("iota")
        pe_passed = s.sem("pe_passed")
        lt_mm = s.sem("lt_mm")
        lt_ready = s.sem("lt_ready")
        turned = s.sem("turned")
        lg_ready = s.sem("lg_ready")
        chain = s.sem("chain")
        less = s.sem("less")
        exps = s.sem("exps")
        bc = lambda ap: ap.unsqueeze(2).to_broadcast([P, NT, E])
        with nc.Block() as block:
            @block.sync
            def _(sp):
                sp.dma_start(ident[:], ident_d).then_inc(loaded, 16)
                sp.dma_start(gate[:], gate_d.rearrange("(c p) e -> p c e", p=P)).then_inc(loaded, 16)

            @block.tensor
            def _(pe):
                pe.wait_ge(loaded, 32)
                with pe.Fori(0, B) as b:
                    pe.wait_ge(lt_ready, b + 1)
                    for k in range(KC):
                        mm = pe.matmul(lo[0:E, :], gate[:, k, :], XT[:, k, ds(T * b, T)],
                                       start=(k == 0), stop=(k == KC - 1))
                    mm.then_inc(lt_mm, 1)
                    pe.wait_ge(lt_ready, b + 2)
                    pe.wait_ge(lg_ready, b + 1)
                    pe.sem_inc(pe_passed, 1)
                    for j in range(TB):
                        mm = pe.transpose(tp[:, j, 0:E], lt[:, j * P:(j + 1) * P], ident[0:E, 0:E])
                    mm.then_inc(turned, 1)

            @block.scalar
            def _(act):
                act.sem_inc(lt_ready, 1)
                act.sem_inc(lg_ready, 1)
                with act.Fori(0, B) as b:
                    act.wait_ge(lt_mm, b + 1)
                    act.activation(lt[:], lo[0:E, :], ACT.Copy).then_inc(lt_ready, 1)
                    act.wait_ge(turned, b + 1)
                    act.activation(LG[:, ds(TB * b, TB), :], tp[:, :, 0:E], ACT.Copy).then_inc(lg_ready, 1)
                act.wait_ge(less, 1)
                act.activation(PR[:], PR[:], ACT.Exp).then_inc(exps, 1)

            @block.gpsimd
            def _(pool):
                for e in range(E):
                    pool.memset(IO[:, :, e:e + 1], float(e)).then_inc(iota, 1)

            @block.vector
            def _(dve):
                c = Tally(chain)
                dve.wait_ge(iota, E)
                dve.wait_ge(lg_ready, B + 1)
                c.inc(dve.tensor_reduce(MX[:], LG[:], AX.X, ALU.max))
                c.wait(dve)
                dve.tensor_tensor(PR[:], LG[:], bc(MX[:]), ALU.subtract).then_inc(less, 1)
                for r in range(top):
                    if r:
                        c.inc(dve.tensor_reduce(MX[:], LG[:], AX.X, ALU.max))
                        c.wait(dve)
                    c.inc(dve.tensor_tensor(EQ[:], LG[:], bc(MX[:]), ALU.is_equal))
                    c.wait(dve)
                    c.inc(dve.scalar_tensor_tensor(KEY[:].rearrange("p t e -> p (t e)"),
                                                   EQ[:].rearrange("p t e -> p (t e)"), -64.0,
                                                   IO[:].rearrange("p t e -> p (t e)"), ALU.mult, ALU.add))
                    c.wait(dve)
                    c.inc(dve.tensor_reduce(SM[:], KEY[:], AX.X, ALU.min))
                    c.wait(dve)
                    hot = COMB if r == 0 else EQ
                    c.inc(dve.tensor_tensor(hot[:], KEY[:], bc(SM[:]), ALU.is_equal))
                    c.wait(dve)
                    if r + 1 < top:
                        c.inc(dve.scalar_tensor_tensor(LG[:].rearrange("p t e -> p (t e)"),
                                                       COMB[:].rearrange("p t e -> p (t e)"), -1e30,
                                                       LG[:].rearrange("p t e -> p (t e)"), ALU.mult, ALU.add))
                        c.wait(dve)
                    if r:
                        c.inc(dve.tensor_tensor(COMB[:], COMB[:], EQ[:], ALU.add))
                        c.wait(dve)
                dve.wait_ge(exps, 1)
                if weight == "softmax":
                    c.inc(dve.tensor_reduce(SM[:], PR[:], AX.X, ALU.add))
                    c.wait(dve)
                if weight != "one":
                    c.inc(dve.tensor_tensor(COMB[:], COMB[:], PR[:], ALU.mult))
                    c.wait(dve)
                    if weight == "renormed":
                        c.inc(dve.tensor_reduce(SM[:], COMB[:], AX.X, ALU.add))
                        c.wait(dve)
                    c.inc(dve.reciprocal(MX[:], SM[:]))
                    c.wait(dve)
                    c.inc(dve.tensor_tensor(COMB[:], COMB[:], bc(MX[:]), ALU.mult))
                    c.wait(dve)


def stage_experts(nc, XT, Y, COMB, E, F, func, w1_d, w3_d, w2_d, b1_d=None, b2_d=None, fresh=False,
                  resident=None):
    FC = F // P
    NS = min(E, 2)
    NC = FC
    gated = w3_d is not None
    with ExitStack() as stack:
        s = Space(nc, stack, "ex" + str(nc.next_id()))
        w1 = [s.sb(f"w1{i}", [P, KC, F]) for i in range(NS)] if resident is None else [resident[0]]
        w3 = [s.sb(f"w3{i}", [P, KC, F]) for i in range(NS)] if gated else None
        w2 = [s.sb(f"w2{i}", [P, FC, D]) for i in range(NS)] if resident is None else [resident[1]]
        b1 = [s.sb(f"b1{i}", [P, FC]) for i in range(NS)] if b1_d is not None else None
        b2 = [s.sb(f"b2{i}", [P, D]) for i in range(NS)] if b2_d is not None else None
        HT = s.sb("HT", [P, FC, T])
        GA = [s.sb(f"GA{i}", [P, T]) for i in range(2)] if gated else None
        YB = s.sb("YB", [P, TB, D])
        first = [s.ps(f"first{i}", [P, T]) for i in range(4)]
        yp = [s.ps(f"yp{i}", [P, 512]) for i in range(TB)]
        w_loaded = [s.sem(f"w_loaded{i}") for i in range(NS)]
        first_mm = s.sem("first_mm")
        ht_ready = s.sem("ht_ready")
        ga_ready = s.sem("ga_ready")
        y_mm = s.sem("y_mm")
        yb_ready = s.sem("yb_ready")
        y_ready = s.sem("y_ready")
        y_part = s.sem("y_part")
        zeroed = s.sem("zeroed")
        pe_passed = s.sem("pe_passed")
        act_passed = s.sem("act_passed")
        dve_passed = s.sem("dve_passed")
        n_dma = 2 * (resident is None) + gated + (b1 is not None) + (b2 is not None)
        ring = 2 if gated else 4
        with nc.Block() as block:
            @block.sync
            def _(sp):
                for e in range(E):
                    i = e % NS
                    if e >= NS:
                        sp.wait_ge(y_ready, B * (e - NS + 1) + 1)
                    if resident is None:
                        sp.dma_start(w1[i][:], w1_d[e].rearrange("(c p) f -> p c f", p=P)).then_inc(w_loaded[i], 16)
                    if gated:
                        sp.dma_start(w3[i][:], w3_d[e].rearrange("(c p) f -> p c f", p=P)).then_inc(w_loaded[i], 16)
                    if b1 is not None:
                        sp.dma_start(b1[i][:], b1_d[e]).then_inc(w_loaded[i], 16)
                    if resident is None:
                        sp.dma_start(w2[i][:], w2_d[e].rearrange("(c p) f -> p c f", p=P)).then_inc(w_loaded[i], 16)
                    if b2 is not None:
                        sp.dma_start(b2[i][:], b2_d[e].unsqueeze(0).to_broadcast([P, D])).then_inc(w_loaded[i], 16)

            @block.tensor
            def _(pe):
                with pe.Fori(0, E // NS) as i2:
                    for i in range(NS):
                        pe.wait_ge(w_loaded[i], 16 * n_dma * i2 + 16 * n_dma)
                        pe.sem_inc(pe_passed, 1)
                        with pe.Fori(0, B) as b:
                            g = B * (NS * i2 + i) + b

                            def layer1(f):
                                pe.wait_ge(ht_ready, NC * g + f + 1)
                                for v, w in enumerate((w1, w3) if gated else (w1,)):
                                    ps = first[2 * (f % 2) + v] if gated else first[f % 4]
                                    for k in range(KC):
                                        mm = pe.matmul(ps[:], w[i][:, k, f * P:(f + 1) * P], XT[:, k, ds(T * b, T)],
                                                       start=(k == 0), stop=(k == KC - 1))
                                mm.then_inc(first_mm, 1)

                            def layer2(f):
                                pe.wait_ge(ht_ready, NC * g + f + 1 + ring)
                                if f == 0:
                                    pe.wait_ge(y_ready, g + 1)
                                for j in range(TB):
                                    mm = pe.matmul(yp[j][:, 0:D], HT[:, f, j * P:(j + 1) * P], w2[i][:, f, :],
                                                   start=(f == 0), stop=(f == FC - 1))
                                return mm

                            layer1(0)
                            for f in range(1, FC):
                                layer1(f)
                                layer2(f - 1)
                            layer2(FC - 1).then_inc(y_mm, 1)

            @block.scalar
            def _(act):
                if not gated:
                    act.sem_inc(ht_ready, ring)
                with act.Fori(0, E // NS) as i2:
                    for i in range(NS):
                        act.wait_ge(w_loaded[i], 16 * n_dma * i2 + 16 * n_dma)
                        act.sem_inc(act_passed, 1)
                        with act.Fori(0, B) as b:
                            g = B * (NS * i2 + i) + b
                            for f in range(FC):
                                act.wait_ge(first_mm, FC * g + f + 1)
                                if gated:
                                    act.wait_ge(ht_ready, FC * g + f + 1)
                                    act.activation(GA[f % 2][:], first[2 * (f % 2)][:], func).then_inc(ga_ready, 1)
                                else:
                                    if f == 0:
                                        act.wait_ge(y_ready, g + 1)
                                    bias = b1[i][:, f:f + 1] if b1 is not None else 0.0
                                    act.activation(HT[:, f, :], first[f % 4][:], func, bias=bias).then_inc(ht_ready, 1)

            @block.vector
            def _(dve):
                dve.sem_inc(y_ready, 1)
                if gated:
                    dve.sem_inc(ht_ready, ring)
                if fresh:
                    dve.memset(Y[:], 0.0).then_inc(zeroed, 1)
                    dve.wait_ge(zeroed, 1)
                with dve.Fori(0, E // NS) as i2:
                    for i in range(NS):
                        dve.wait_ge(w_loaded[i], 16 * n_dma * i2 + 16 * n_dma)
                        dve.sem_inc(dve_passed, 1)
                        with dve.Fori(0, B) as b:
                            g = B * (NS * i2 + i) + b
                            if gated:
                                for f in range(FC):
                                    dve.wait_ge(ga_ready, FC * g + f + 1)
                                    dve.tensor_tensor(HT[:, f, :], GA[f % 2][:], first[2 * (f % 2) + 1][:], ALU.mult) \
                                        .then_inc(ht_ready, 1)
                            dve.wait_ge(y_mm, g + 1)
                            for j in range(TB):
                                src = yp[j][:, 0:D]
                                if b2 is not None:
                                    dve.tensor_tensor(YB[:, j, :], src, b2[i][:], ALU.add).then_inc(yb_ready, 1)
                            for j in range(TB):
                                src = yp[j][:, 0:D]
                                if b2 is not None:
                                    dve.wait_ge(yb_ready, TB * g + j + 1)
                                    src = YB[:, j, :]
                                dst = Y[:, ds(TB * b + j, 1), :]
                                if COMB is None:
                                    ins = dve.tensor_tensor(dst, src.unsqueeze(1), dst, ALU.add)
                                else:
                                    share = COMB[:, ds(TB * b + j, 1), ds(NS * i2 + i, 1)].rearrange("p a b -> p (a b)")
                                    ins = dve.scalar_tensor_tensor(dst, src.unsqueeze(1), share, dst, ALU.mult, ALU.add)
                                if j == TB - 1:
                                    ins.then_inc(y_ready, 1)
                                else:
                                    ins.then_inc(y_part, 1)
                            dve.wait_ge(y_ready, g + 2)
                            dve.wait_ge(y_part, (TB - 1) * g + TB - 1)



def stage_load(nc, name, pairs):
    with nc.semaphore(name) as loaded, nc.Block() as block:
        @block.sync
        def _(sp):
            for dst, src in pairs:
                sp.dma_start(dst, src).then_inc(loaded, 16)
            sp.wait_ge(loaded, 16 * len(pairs))


def stage_spectral(nc, W, qkv_d, u_qkv, sp_qkv, proj_d, u_proj, sp_proj):
    with ExitStack() as stack:
        s = Space(nc, stack, "sn")
        ones = s.sb("ones", [P, P])
        loaded = s.sem("loaded")
        ones_ready = s.sem("ones_ready")
        chain = s.sem("chain")
        mm_done = s.sem("mm_done")
        root = s.sem("root")
        parts = []
        for name, wd, u, sp_, n in (("qkv", qkv_d, u_qkv, sp_qkv, 3 * D), ("proj", proj_d, u_proj, sp_proj, D)):
            parts.append(dict(
                n=n, wd=wd, u=u, sp=sp_, w=s.sb("w" + name, [P, KC, n]), ub=s.sb("u" + name, [P, n]),
                pr=s.sb("pr" + name, [P, KC, n]), v=s.sb("v" + name, [P, KC]), sq=s.sb("sq" + name, [P, n // P]),
                r=s.sb("r" + name, [P, 1]), t=s.sb("t" + name, [P, 2]), u2=s.sb("u2" + name, [P, n // P]),
                c=s.sb("c" + name, [P, 1]), nrm=s.ps("nrm" + name, [P, 1]), col=s.ps("col" + name, [P, n // P])))
        with nc.Block() as block:
            @block.sync
            def _(sp):
                for p in parts:
                    sp.dma_start(p["w"][:], p["wd"].rearrange("(c p) n -> p c n", p=P)).then_inc(loaded, 16)
                    sp.dma_start(p["ub"][:], p["u"].unsqueeze(0).to_broadcast([P, p["n"]])).then_inc(loaded, 16)
                    sp.dma_start(p["c"][:], p["sp"].unsqueeze(0).to_broadcast([P, 1])).then_inc(loaded, 16)

            @block.vector
            def _(dve):
                c = Tally(chain)
                dve.memset(ones[:], 1.0).then_inc(ones_ready, 1)
                dve.wait_ge(loaded, 96)
                for k, p in enumerate(parts):
                    n = p["n"]
                    c.inc(dve.tensor_tensor(p["pr"][:], p["w"][:], p["ub"][:].unsqueeze(1).to_broadcast([P, KC, n]),
                                            ALU.mult))
                    c.wait(dve)
                    c.inc(dve.tensor_reduce(p["v"][:], p["pr"][:], AX.X, ALU.add))
                    c.wait(dve)
                    for src, width in ((p["v"], KC), (p["u2"], n // P)):
                        if width != KC or src is p["u2"]:
                            dve.wait_ge(mm_done, 3 * k + 2)
                            c.inc(dve.tensor_copy(src[:], p["col"][:]))
                            c.wait(dve)
                        c.inc(dve.tensor_tensor(p["sq"][:, 0:width], src[:], src[:], ALU.mult))
                        c.wait(dve)
                        c.inc(dve.tensor_reduce(p["r"][:], p["sq"][:, 0:width], AX.X, ALU.add))
                        p.setdefault("ready", []).append(c.n)
                        c.wait(dve)
                        if src is p["v"]:
                            dve.wait_ge(root, 2 * k + 1)
                            c.inc(dve.reciprocal(p["t"][:, 1:2], p["t"][:, 0:1]))
                            c.wait(dve)
                            c.inc(dve.tensor_scalar(p["v"][:], p["v"][:], p["t"][:, 1:2], None, ALU.mult))
                            p["v_ready"] = c.n
                            c.wait(dve)
                        else:
                            dve.wait_ge(root, 2 * k + 2)
                            c.inc(dve.reciprocal(p["t"][:, 1:2], p["t"][:, 0:1]))
                            c.wait(dve)
                            c.inc(dve.tensor_scalar(p["c"][:], p["c"][:], p["t"][:, 1:2], None, ALU.mult))
                            c.wait(dve)
                for m in ("q", "k", "v"):
                    c.inc(dve.tensor_scalar(W[m][:], W[m][:], parts[0]["c"][:], None, ALU.mult))
                c.inc(dve.tensor_scalar(W["o"][:], W["o"][:], parts[1]["c"][0:AG * AD, :], None, ALU.mult))

            @block.tensor
            def _(pe):
                pe.wait_ge(ones_ready, 1)
                for k, p in enumerate(parts):
                    pe.wait_ge(chain, p["ready"][0])
                    pe.matmul(p["nrm"][:], ones[:], p["r"][:], start=True, stop=True).then_inc(mm_done, 1)
                    pe.wait_ge(chain, p["v_ready"])
                    for m in range(p["n"] // P):
                        for q in range(KC):
                            mm = pe.matmul(p["col"][:, m:m + 1], p["w"][:, q, m * P:(m + 1) * P], p["v"][:, q:q + 1],
                                           start=(q == 0), stop=(q == KC - 1))
                    mm.then_inc(mm_done, 1)
                    pe.wait_ge(chain, p["ready"][1])
                    pe.matmul(p["nrm"][:], ones[:], p["r"][:], start=True, stop=True).then_inc(mm_done, 1)

            @block.scalar
            def _(act):
                for k, p in enumerate(parts):
                    for m in range(2):
                        act.wait_ge(mm_done, 3 * k + 1 + 2 * m)
                        act.activation(p["t"][:, 0:1], p["nrm"][:], ACT.Sqrt).then_inc(root, 1)


def stage_binary(nc, W):
    with ExitStack() as stack:
        s = Space(nc, stack, "bi")
        ones = s.sb("ones", [P, P])
        shapes = {"q": (P, KC, NG * P), "k": (P, KC, NG * P), "v": (P, KC, NG * P), "o": (AG * AD, NG, D)}
        view = {n: W[n][:].rearrange("p c g n -> p c (g n)") if n != "o" else W[n][:] for n in shapes}
        SG = {n: s.sb("sg" + n, list(sh)) for n, sh in shapes.items()}
        AB = {n: s.sb("ab" + n, list(sh)) for n, sh in shapes.items()}
        al = {n: s.ps("al" + n, [sh[0], sh[2]]) for n, sh in shapes.items()}
        ones_ready = s.sem("ones_ready")
        signs = s.sem("signs")
        sizes = s.sem("sizes")
        mm_done = s.sem("mm_done")
        chain = s.sem("chain")
        with nc.Block() as block:
            @block.scalar
            def _(act):
                for n in shapes:
                    act.activation(AB[n][:], view[n], ACT.Abs).then_inc(sizes, 1)
                    act.activation(SG[n][:], view[n], ACT.Sign).then_inc(signs, 1)

            @block.tensor
            def _(pe):
                pe.wait_ge(ones_ready, 1)
                for i, (n, (rows, chunks, width)) in enumerate(shapes.items()):
                    pe.wait_ge(sizes, i + 1)
                    for k in range(chunks):
                        mm = pe.matmul(al[n][:], ones[0:rows, 0:rows], AB[n][:, k, :],
                                       start=(k == 0), stop=(k == chunks - 1))
                    mm.then_inc(mm_done, 1)

            @block.vector
            def _(dve):
                dve.memset(ones[:], 1.0).then_inc(ones_ready, 1)
                c = Tally(chain)
                for i, (n, (rows, chunks, width)) in enumerate(shapes.items()):
                    dve.wait_ge(signs, i + 1)
                    c.inc(dve.tensor_tensor(SG[n][:], SG[n][:], view[n], ALU.subtract))
                    c.wait(dve)
                    c.inc(dve.tensor_tensor(view[n], view[n], SG[n][:], ALU.add))
                    c.wait(dve)
                    dve.wait_ge(mm_done, i + 1)
                    for k in range(chunks):
                        c.inc(dve.scalar_tensor_tensor(view[n][:, k, :], al[n][:], 1.0 / D, view[n][:, k, :],
                                                       ALU.mult, ALU.mult))


def stage_ternary(nc, tensors):
    with ExitStack() as stack:
        s = Space(nc, stack, "te")
        ones = s.sb("ones", [P, P])
        ones_ready = s.sem("ones_ready")
        chain = s.sem("chain")
        mm_done = s.sem("mm_done")
        sums = [s.sb(f"sum{i}", [P, 1]) for i in range(2)]
        thr = [s.sb(f"thr{i}", [P, 2]) for i in range(2)]
        low = [s.sb(f"low{i}", [P, 2048]) for i in range(2)]
        tot = [s.ps(f"tot{i}", [P, 1]) for i in range(2)]
        count = float(1024 * D)
        ready = []
        with nc.Block() as block:
            @block.vector
            def _(dve):
                dve.memset(ones[:], 1.0).then_inc(ones_ready, 1)
                c = Tally(chain)
                for i, w in enumerate(tensors):
                    c.inc(dve.tensor_reduce(sums[i][:], w, AX.XY, ALU.add, apply_absolute_value=True))
                    ready.append(c.n)
                for i, w in enumerate(tensors):
                    lo = low[i][:].rearrange("p (a b) -> p a b", a=w.shape[1])
                    dve.wait_ge(mm_done, i + 1)
                    for m, sign in enumerate((0.5, -0.5)):
                        c.inc(dve.tensor_scalar(thr[i][:, m:m + 1], tot[i][:], sign / count, sign * 1e-5,
                                                ALU.mult, ALU.add))
                    c.wait(dve)
                    c.inc(dve.tensor_scalar(lo, w, thr[i][:, 1:2], None, ALU.is_lt))
                    c.wait(dve)
                    c.inc(dve.scalar_tensor_tensor(w, w, thr[i][:, 0:1], lo, ALU.is_gt, ALU.subtract))

            @block.tensor
            def _(pe):
                pe.wait_ge(ones_ready, 1)
                for i in range(len(tensors)):
                    pe.wait_ge(chain, ready[i])
                    pe.matmul(tot[i][:], ones[:], sums[i][:], start=True, stop=True).then_inc(mm_done, 1)


def stage_conv(nc, XT, XC, taps_d):
    with ExitStack() as stack:
        s = Space(nc, stack, "cv")
        taps = s.sb("taps", [P, KC, 3])
        loaded = s.sem("loaded")
        summed = s.sem("summed")
        with nc.Block() as block:
            @block.sync
            def _(sp):
                sp.dma_start(taps[:], taps_d.rearrange("(c p) w -> p c w", p=P)).then_inc(loaded, 16)

            @block.vector
            def _(dve):
                c = Tally(summed)
                dve.wait_ge(loaded, 16)
                for k in range(KC):
                    x = XT[:, k, :].rearrange("p (b t) -> p b t", b=B)
                    y = XC[:, k, :].rearrange("p (b t) -> p b t", b=B)
                    c.inc(dve.tensor_scalar(y, x, taps[:, k, 2:3], None, ALU.mult))
                    for lag in (1, 2):
                        c.wait(dve)
                        c.inc(dve.scalar_tensor_tensor(y[:, :, lag:T], x[:, :, 0:T - lag],
                                                       taps[:, k, 2 - lag:3 - lag], y[:, :, lag:T],
                                                       ALU.mult, ALU.add))



def stage_linear(nc, XT, Y, ident_d, wqk_d, wv_d, wo_d, bqk_d, bv_d, bo_d):
    E1 = AD + 1
    with ExitStack() as stack:
        s = Space(nc, stack, "li")
        ident = s.sb("ident", [P, P])
        wqk = s.sb("wqk", [P, KC, 2 * D])
        wv = s.sb("wv", [P, KC, D])
        wo = s.sb("wo", [P, KC, D])
        bqk = s.sb("bqk", [P, 2 * D])
        bv = s.sb("bv", [P, D])
        bo = s.sb("bo", [P, D])
        XS = [s.sb(f"XS{i}", [P, KC, P]) for i in range(TB)]
        QK = [s.sb(f"QK{i}", [P, 2 * D]) for i in range(TB)]
        EX = [s.sb(f"EX{i}", [P, 2 * D]) for i in range(TB)]
        V1 = [s.sb(f"V1{i}", [P, AH, E1]) for i in range(TB)]
        KV = s.sb("KV", [P, AD, E1])
        PR = s.sb("PR", [P, AD, E1, AH])
        PQ = s.sb("PQ", [P, AH, E1, AD])
        QV = s.sb("QV", [P, AH, E1])
        RI = s.sb("RI", [P, AH])
        AT = [s.sb(f"AT{i}", [P, D]) for i in range(2)]
        ATT = [s.sb(f"ATT{i}", [P, KC, P]) for i in range(2)]
        pqk = [s.ps(f"pqk{i}", [P, 2 * D]) for i in range(2)]
        pv = [s.ps(f"pv{i}", [P, 512]) for i in range(2)]
        tp = [s.ps(f"tp{i}", [P, KC, 2 * P]) for i in range(2)]
        yo = [s.ps(f"yo{i}", [P, 512]) for i in range(2)]
        loaded = s.sem("loaded")
        ones_ready = s.sem("ones_ready")
        xs_ready = s.sem("xs_ready")
        qkv_mm = s.sem("qkv_mm")
        qk_added = s.sem("qk_added")
        v_ready = s.sem("v_ready")
        low_ready = s.sem("low_ready")
        exp_ready = s.sem("exp_ready")
        elu_ready = s.sem("elu_ready")
        kv_product = s.sem("kv_product")
        kv_ready = s.sem("kv_ready")
        chain = s.sem("chain")
        at_ready = s.sem("at_ready")
        turned = s.sem("turned")
        att_ready = s.sem("att_ready")
        o_mm = s.sem("o_mm")
        y_ready = s.sem("y_ready")
        dve_passed = s.sem("dve_passed")
        with nc.Block() as block:
            @block.sync
            def _(sp):
                sp.dma_start(ident[:], ident_d).then_inc(loaded, 16)
                for dst, src in ((wqk, wqk_d), (wv, wv_d), (wo, wo_d)):
                    sp.dma_start(dst[:], src.rearrange("(c p) n -> p c n", p=P)).then_inc(loaded, 16)
                for dst, src in ((bqk, bqk_d), (bv, bv_d), (bo, bo_d)):
                    sp.dma_start(dst[:], src.unsqueeze(0).to_broadcast([P, src.shape[0]])).then_inc(loaded, 16)

            @block.gpsimd
            def _(pool):
                for j in range(TB):
                    pool.memset(V1[j][:], 1.0).then_inc(ones_ready, 1)
                pool.sem_inc(kv_product, 1)
                with pool.Fori(0, B) as b:
                    for j in range(TB):
                        pool.wait_ge(qk_added, TB * b + j + 1)
                        pool.tensor_copy(XS[j][:], XT[:, :, ds(T * b + P * j, P)]).then_inc(xs_ready, 1)
                    for j in range(TB):
                        pool.wait_ge(elu_ready, TB * b + j + 1)
                        pool.wait_ge(v_ready, TB * b + j + 1 + TB)
                        pool.wait_ge(kv_ready, TB * b + j + 1)
                        k = QK[j][:, D:2 * D].rearrange("p (h d) -> p d h", h=AH)
                        v = V1[j][:].rearrange("p h e -> p e h")
                        pool.tensor_tensor(PR[:], k.unsqueeze(2).to_broadcast([P, AD, E1, AH]),
                                           v.unsqueeze(1).to_broadcast([P, AD, E1, AH]), ALU.mult) \
                            .then_inc(kv_product, 1)

            @block.tensor
            def _(pe):
                pe.wait_ge(loaded, 16 * 7)
                with pe.Fori(0, B) as b:
                    for j in range(TB):
                        f = j % 2
                        pe.wait_ge(xs_ready, TB * b + j + 1)
                        pe.wait_ge(qk_added, TB * b + j + 3)
                        pe.wait_ge(v_ready, TB * b + j + 3)
                        for k in range(KC):
                            pe.matmul(pqk[f][:], XS[j][:, k, :], wqk[:, k, :], start=(k == 0), stop=(k == KC - 1))
                        for k in range(KC):
                            mm = pe.matmul(pv[f][:, 0:D], XS[j][:, k, :], wv[:, k, :],
                                           start=(k == 0), stop=(k == KC - 1))
                        mm.then_inc(qkv_mm, 1)
                    for j in range(TB):
                        f = j % 2
                        pe.wait_ge(at_ready, TB * b + j + 1)
                        pe.wait_ge(att_ready, TB * b + j + 1)
                        for k in range(KC):
                            mm = pe.transpose(tp[f][:, k, 0:P], AT[f][:, k * P:(k + 1) * P], ident[:])
                        mm.then_inc(turned, 1)
                        pe.wait_ge(att_ready, TB * b + j + 3)
                        pe.wait_ge(y_ready, TB * b + j + 1)
                        for k in range(KC):
                            mm = pe.matmul(yo[f][:, 0:D], ATT[f][:, k, :], wo[:, k, :],
                                           start=(k == 0), stop=(k == KC - 1))
                        mm.then_inc(o_mm, 1)

            @block.scalar
            def _(act):
                act.sem_inc(att_ready, 2)
                with act.Fori(0, B) as b:
                    for j in range(TB):
                        act.wait_ge(low_ready, TB * b + j + 1)
                        act.activation(EX[j][:], EX[j][:], ACT.Exp).then_inc(exp_ready, 1)
                    for j in range(TB):
                        act.wait_ge(turned, TB * b + j + 1)
                        act.wait_ge(y_ready, TB * b + j + 1)
                        act.activation(ATT[j % 2][:], tp[j % 2][:, :, 0:P], ACT.Copy).then_inc(att_ready, 1)

            @block.vector
            def _(dve):
                dve.wait_ge(loaded, 16 * 7)
                dve.wait_ge(ones_ready, TB)
                dve.sem_inc(qk_added, TB)
                dve.sem_inc(v_ready, TB)
                dve.sem_inc(kv_ready, 1)
                dve.sem_inc(y_ready, 2)
                per = 4 * TB

                with dve.Fori(0, B) as b:
                    c = Tally(chain, per * b)
                    for j in range(TB):
                        n = TB * b + j
                        f = j % 2
                        dve.wait_ge(qkv_mm, n + 1)
                        dve.wait_ge(kv_product, TB * b + 1)
                        dve.tensor_tensor(QK[j][:], pqk[f][:], bqk[:], ALU.add).then_inc(qk_added, 1)
                        dve.tensor_tensor(V1[j][:, :, 0:AD], pv[f][:, 0:D].rearrange("p (h e) -> p h e", h=AH),
                                          bv[:].rearrange("p (h e) -> p h e", h=AH), ALU.add).then_inc(v_ready, 1)
                        dve.wait_ge(qk_added, n + 1 + TB)
                        dve.tensor_scalar(EX[j][:], QK[j][:], 0.0, None, ALU.min).then_inc(low_ready, 1)
                    for j in range(TB):
                        n = TB * b + j
                        dve.wait_ge(exp_ready, n + 1)
                        dve.scalar_tensor_tensor(QK[j][:], QK[j][:], 0.0, EX[j][:], ALU.max, ALU.add) \
                            .then_inc(elu_ready, 1)

                    def add_out(j):
                        dve.wait_ge(o_mm, TB * b + j + 1)
                        dve.tensor_tensor(Y[:, ds(TB * b + j, 1), :], yo[j % 2][:, 0:D].unsqueeze(1), bo[:].unsqueeze(1),
                                          ALU.add).then_inc(y_ready, 1)

                    for j in range(TB):
                        n = TB * b + j
                        dve.wait_ge(kv_product, n + 2)
                        dve.tensor_reduce(KV[:], PR[:], AX.X, ALU.add).then_inc(kv_ready, 1)
                        dve.wait_ge(kv_ready, n + 2)
                        q = QK[j][:, 0:D].rearrange("p (h d) -> p h d", h=AH)
                        c.inc(dve.tensor_tensor(PQ[:], q.unsqueeze(2).to_broadcast([P, AH, E1, AD]),
                                                KV[:].rearrange("p d e -> p e d").unsqueeze(1)
                                                .to_broadcast([P, AH, E1, AD]), ALU.mult))
                        c.wait(dve)
                        c.inc(dve.tensor_reduce(QV[:], PQ[:], AX.X, ALU.add))
                        c.wait(dve)
                        c.inc(dve.reciprocal(RI[:], QV[:, :, AD]))
                        c.wait(dve)
                        dve.wait_ge(att_ready, n + 1)
                        c.inc(dve.tensor_tensor(AT[j % 2][:].rearrange("p (h e) -> p h e", h=AH), QV[:, :, 0:AD],
                                                RI[:].unsqueeze(2).to_broadcast([P, AH, AD]), ALU.mult))
                        c.wait(dve)
                        dve.sem_inc(at_ready, 1)
                        if j:
                            add_out(j - 1)
                    add_out(TB - 1)



def tower(nc, a, out):
    ident = a["ident"]
    RETIRED.clear()
    with ExitStack() as whole:
        def buf(stack, name, shape, dt=F32):
            return stack.enter_context(nc.sbuf_tensor(name, shape, dt))

        def attention_weights(stack, prefix, names):
            w = {n: buf(stack, f"{prefix}_{n}", [P, KC, NG, P]) for n in names}
            w["o"] = buf(stack, f"{prefix}_o", [AG * AD, NG, D])
            return w, [(w[n][:], a[f"{prefix}_{n}"]) for n in w]

        H = buf(whole, "H", [P, NT, D])
        Y = buf(whole, "Y", [P, NT, D])
        XT = buf(whole, "XT", [P, KC, B * T])

        stage_tokens(nc, H, a["xk"], a["wsT"], a["wtok"])
        stage_rows(nc, H, None, XT, ident)
        with ExitStack() as st:
            OUT = buf(st, "OUT", [P, T, HN])
            with ExitStack() as cell:
                KN = buf(cell, "KN", [P, TL, D])
                QR = buf(cell, "QR", [P, TL, D])
                V = buf(cell, "V", [P, HN, T])
                BT = buf(cell, "BT", [P, HN, T])
                stage_cell_inputs(nc, XT, KN, QR, V, BT, a["w_in"], a["w_kq"], a["w_vb"], a["b_beta"])
                stage_cell(nc, KN, QR, V, BT, OUT, ident)
            stage_cell_out(nc, OUT, Y, a["w_out"])
        stage_rows(nc, H, Y, XT, ident, post="ln", second="rms", w=a["g1"])
        with ExitStack() as st:
            w, pairs = attention_weights(st, "a0", ("q", "k", "v", "qr", "kr"))
            stage_load(nc, "a0_loaded", pairs)
            stage_attention(nc, XT, Y, ident, w, a["no_bias"], True, a["rope"])
        stage_rows(nc, H, Y, XT, ident, post="add", second="rms", w=a["g2"])
        with ExitStack() as st:
            COMB = buf(st, "COMB0", [P, NT, 4])
            stage_router(nc, XT, COMB, ident, a["gate0"], 4, 2, "renormed")
            stage_experts(nc, XT, Y, COMB, 4, 768, ACT.Silu, a["e0_w1"], a["e0_w3"], a["e0_w2"])
        stage_rows(nc, H, Y, XT, ident, post="ln")

        with ExitStack() as st:
            w, pairs = attention_weights(st, "a1", ("q", "k", "v"))
            stage_load(nc, "a1_loaded", pairs)
            stage_spectral(nc, w, a["w_qkv"], a["u_qkv"], a["sp_qkv"], a["w_proj"], a["u_proj"], a["sp_proj"])
            stage_attention(nc, XT, Y, ident, w, a["no_bias"], True)
        stage_rows(nc, H, Y, XT, ident, post="ln")
        with ExitStack() as st:
            COMB = buf(st, "COMB1", [P, NT, 8])
            stage_router(nc, XT, COMB, ident, a["gate1"], 8, 1, "softmax")
            stage_experts(nc, XT, Y, COMB, 8, 1024, ACT.Relu, a["e1_w1"], None, a["e1_w2"], a["e1_b1"], a["e1_b2"],
                          fresh=True)
        stage_rows(nc, H, Y, XT, ident, post="ln")

        with ExitStack() as st:
            w, pairs = attention_weights(st, "a2", ("q", "k", "v"))
            stage_load(nc, "a2_loaded", pairs)
            stage_binary(nc, w)
            stage_attention(nc, XT, Y, ident, w, a["a2_bias"], False, out_bias=a["a2_bo"])
        stage_rows(nc, H, Y, XT, ident, post="ln", second="ln", w=a["c_ln1_w"], b=a["c_ln1_b"])
        with ExitStack() as st:
            XC = buf(st, "XC", [P, KC, B * T])
            stage_conv(nc, XT, XC, a["taps"])
            w, pairs = attention_weights(st, "a3", ("q", "k", "v", "qr", "kr"))
            stage_load(nc, "a3_loaded", pairs)
            stage_attention(nc, XC, Y, ident, w, a["no_bias"], True, a["rope"])
        stage_rows(nc, H, Y, XT, ident, post="add", second="ln", w=a["c_ln2_w"], b=a["c_ln2_b"])
        with ExitStack() as st:
            COMB = buf(st, "COMB2", [P, NT, 4])
            stage_router(nc, XT, COMB, ident, a["gate2"], 4, 1, "one")
            stage_experts(nc, XT, Y, COMB, 4, 1024, ACT.Silu, a["e2_w1"], a["e2_w3"], a["e2_w2"])
        stage_rows(nc, H, Y, XT, ident, post="ln", second="ln", w=a["d_ln1_w"], b=a["d_ln1_b"])

        stage_linear(nc, XT, Y, ident, a["l_wqk"], a["l_wv"], a["l_wo"], a["l_bqk"], a["l_bv"], a["l_bo"])
        stage_rows(nc, H, Y, XT, ident, post="add", second="ln", w=a["d_ln2_w"], b=a["d_ln2_b"])
        stage_experts(nc, XT, Y, None, 1, 1024, ACT.Gelu, a["fc_w"], None, a["fp_w"], a["fc_b"], a["fp_b"])
        stage_rows(nc, H, Y, XT, ident, post="ln")
        with ExitStack() as st:
            w1 = buf(st, "t_w1", [P, KC, 1024])
            w2 = buf(st, "t_w2", [P, 8, D])
            stage_load(nc, "t_loaded", [(w1[:], a["t_w1"]), (w2[:], a["t_w2"])])
            stage_ternary(nc, [w1[:], w2[:]])
            stage_experts(nc, XT, Y, None, 1, 1024, ACT.Relu, None, None, None, a["t_b1"], a["t_b2"], fresh=True,
                          resident=(w1, w2))
        stage_rows(nc, H, Y, None, ident, post="ln", out=out)



def layout(i):
    def rows(w):
        o = np.zeros((D, AH, Q4), np.float32)
        o[:, :, :AD] = w.reshape(D, AH, AD)
        return o.reshape(KC, P, NG, P).transpose(1, 0, 2, 3)

    def turned(w):
        return w.reshape(D, AH, 2, AD // 2)[:, :, ::-1, :].reshape(D, D)

    def bias(*bs):
        o = np.zeros((3, AH, Q4), np.float32)
        for n, b in enumerate(bs):
            o[n, :, :AD] = b.reshape(AH, AD)
        o[1:, :, ONE] = 1
        return o.reshape(3, NG, P).transpose(2, 0, 1)

    def out_rows(w):
        return w.reshape(NG, AG * AD, D).transpose(1, 0, 2)

    def expert_bias(b):
        return b.reshape(b.shape[0], -1, P).transpose(0, 2, 1)

    freq = 1.0 / 10000.0 ** (np.arange(0, AD, 2, dtype=np.float32) / AD)
    angle = freq.astype(np.float32)[:, None] * np.arange(T, dtype=np.float32)[None, :]
    rope = np.zeros((2, AG, Q4, T), np.float32)
    for half, sign in ((0, -1), (1, 1)):
        rows_of = slice(half * AD // 2, (half + 1) * AD // 2)
        rope[0, :, rows_of] = np.cos(angle)
        rope[1, :, rows_of] = sign * np.sin(angle)
    rope[0, :, ONE] = 1
    vb = np.stack([i["L0_attn_W_v"].reshape(HN, HD, D), i["L0_attn_W_beta"].reshape(HN, HD, D)], 1)
    kv_heads = lambda w: np.repeat(w.reshape(D, NG, AD), AG, axis=1).reshape(D, D)
    a = {
        "ident": np.eye(P, dtype=np.float32),
        "xk": i["x"].reshape(B * T, D, 4).transpose(2, 1, 0).reshape(4 * KC, P, B * T),
        "wsT": i["L0_tok_weighted_sum"].T.reshape(KC, P, D),
        "wtok": i["L0_tok_weight"].T,
        "w_in": i["L0_attn_W_in"].T.reshape(KC, P, D),
        "w_kq": np.concatenate([i["L0_attn_W_k"].T, i["L0_attn_W_q"].T], 1).reshape(KC, P, 2 * D),
        "w_vb": vb.reshape(HN, 2 * HD, KC, P).transpose(0, 3, 2, 1),
        "b_beta": np.tile(i["L0_attn_b_beta"].T, (B, 1)),
        "w_out": np.tile(i["L0_attn_W_out"].T.reshape(HN, HD, D).transpose(1, 0, 2), (B, 1, 1)),
        "g1": i["L0_ffn_g1"], "g2": i["L0_ffn_g2"],
        "rope": rope.reshape(2, P, T).transpose(1, 0, 2),
        "no_bias": bias(),
        "a0_q": rows(i["L0_ffn_wq"]), "a0_qr": rows(turned(i["L0_ffn_wq"])),
        "a0_k": rows(kv_heads(i["L0_ffn_wk"])), "a0_kr": rows(turned(kv_heads(i["L0_ffn_wk"]))),
        "a0_v": rows(kv_heads(i["L0_ffn_wv"])), "a0_o": out_rows(i["L0_ffn_wo"]),
        "gate0": i["L0_ffn_gate"],
        "e0_w1": i["L0_ffn_w1"], "e0_w3": i["L0_ffn_w3"], "e0_w2": i["L0_ffn_w2"],
        "w_qkv": i["L1_attn_W_qkv"], "u_qkv": i["L1_attn_u_qkv"], "sp_qkv": i["L1_attn_sigma_qkv"],
        "w_proj": i["L1_attn_W_proj"], "u_proj": i["L1_attn_u_proj"], "sp_proj": i["L1_attn_sigma_proj"],
        "a1_q": rows(i["L1_attn_W_qkv"][:, 0:D]), "a1_k": rows(i["L1_attn_W_qkv"][:, D:2 * D]),
        "a1_v": rows(i["L1_attn_W_qkv"][:, 2 * D:]), "a1_o": out_rows(i["L1_attn_W_proj"]),
        "gate1": i["L1_ffn_gate_w"].T,
        "e1_w1": i["L1_ffn_w1"], "e1_w2": i["L1_ffn_w2"], "e1_b1": expert_bias(i["L1_ffn_b1"]),
        "e1_b2": i["L1_ffn_b2"],
        "a2_q": rows(i["L2_attn_Wq"].T), "a2_k": rows(i["L2_attn_Wk"].T), "a2_v": rows(i["L2_attn_Wv"].T),
        "a2_o": out_rows(i["L2_attn_Wp"].T), "a2_bo": i["L2_attn_bp"],
        "a2_bias": bias(i["L2_attn_bq"], i["L2_attn_bk"], i["L2_attn_bv"]),
        "c_ln1_w": i["L2_ffn_ln1_w"], "c_ln1_b": i["L2_ffn_ln1_b"],
        "c_ln2_w": i["L2_ffn_ln2_w"], "c_ln2_b": i["L2_ffn_ln2_b"],
        "taps": i["L2_ffn_conv_w"][:, 0, :],
        "a3_q": rows(i["L2_ffn_attn_w"][:, 0:D]), "a3_qr": rows(turned(i["L2_ffn_attn_w"][:, 0:D])),
        "a3_k": rows(i["L2_ffn_attn_w"][:, D:2 * D]), "a3_kr": rows(turned(i["L2_ffn_attn_w"][:, D:2 * D])),
        "a3_v": rows(i["L2_ffn_attn_w"][:, 2 * D:]), "a3_o": out_rows(i["L2_ffn_proj_w"]),
        "gate2": i["L2_ffn_router_w"],
        "e2_w1": i["L2_ffn_expert_wv"][:, :, 0:1024], "e2_w3": i["L2_ffn_expert_wv"][:, :, 1024:],
        "e2_w2": i["L2_ffn_expert_proj"],
        "d_ln1_w": i["L3_attn_ln1_w"], "d_ln1_b": i["L3_attn_ln1_b"],
        "d_ln2_w": i["L3_attn_ln2_w"], "d_ln2_b": i["L3_attn_ln2_b"],
        "l_wqk": np.concatenate([i["L3_attn_q_w"].T, i["L3_attn_k_w"].T], 1),
        "l_wv": i["L3_attn_v_w"].T, "l_wo": i["L3_attn_o_w"].T,
        "l_bqk": np.concatenate([i["L3_attn_q_b"], i["L3_attn_k_b"]]),
        "l_bv": i["L3_attn_v_b"], "l_bo": i["L3_attn_o_b"],
        "fc_w": i["L3_attn_fc_w"].T[None], "fp_w": i["L3_attn_proj_w"].T[None],
        "fc_b": expert_bias(i["L3_attn_fc_b"][None]), "fp_b": i["L3_attn_proj_b"][None],
        "t_w1": i["L3_ffn_W1"].T.reshape(KC, P, 1024).transpose(1, 0, 2),
        "t_w2": i["L3_ffn_W2"].T.reshape(8, P, D).transpose(1, 0, 2),
        "t_b1": expert_bias(i["L3_ffn_b1"][None]), "t_b2": i["L3_ffn_b2"][None],
    }
    return {n: np.ascontiguousarray(v) for n, v in a.items()}


def kernel(**inputs):
    import concourse.bacc as _bacc
    from concourse.bass_utils import run_bass_kernel_spmd as _run

    nc = _bacc.Bacc("TRN2", target_bir_lowering=False, num_devices=1)
    arrays = layout({n: np.asarray(v) for n, v in inputs.items()})
    aps = {n: nc.dram_tensor("in_" + n, v.shape, mybir.dt.from_np(v.dtype), kind="ExternalInput").ap()
           for n, v in arrays.items()}
    out = nc.dram_tensor("out", (B, T, D), F32, kind="ExternalOutput").ap()
    tower(nc, aps, out)
    r = _run(nc, [{"in_" + n: v for n, v in arrays.items()}], core_ids=[0])
    return r.results[0]["out"]
```

```python
from contextlib import ExitStack

import numpy as np
import concourse.bass as bass
from concourse import mybir
from concourse.bass import ds

F32 = mybir.dt.float32
BF16 = mybir.dt.bfloat16
ALU = mybir.AluOpType
ACT = mybir.ActivationFunctionType
AX = mybir.AxisListType

P = 128
B, T, D = 4, 512, 256
KC = D // P
NT = B * T // P
TB = T // P
Q4 = 32


RETIRED = []
CLEAR_AT = 100


class Space:

    def __init__(self, nc, stack, name):
        self.nc, self.stack, self.name = nc, stack, name
        if len(RETIRED) > CLEAR_AT:
            nc.clear_and_free_semaphores(list(RETIRED))
            RETIRED.clear()
            nc.all_engine_barrier()

    def sb(self, name, shape, dt=F32):
        return self.stack.enter_context(self.nc.sbuf_tensor(f"{self.name}_{name}", shape, dt))

    def ps(self, name, shape, dt=F32):
        return self.stack.enter_context(self.nc.psum_tensor(f"{self.name}_{name}", shape, dt))

    def sem(self, name):
        made = self.nc.alloc_semaphore(name=f"{self.name}_{name}")
        self.stack.callback(RETIRED.append, made)
        return made


class Tally:

    def __init__(self, sem, base=0):
        self.sem, self.base, self.n = sem, base, 0

    def inc(self, ins):
        ins.then_inc(self.sem, 1)
        self.n += 1
        return self.n

    def wait(self, eng, n=None):
        eng.wait_ge(self.sem, self.base + (self.n if n is None else n))



def stage_tokens(nc, H, xk, wsT, wtok):
    NX = 4 * KC
    with ExitStack() as stack:
        s = Space(nc, stack, "tok")
        xg = [s.sb(f"xg{i}", [P, NX, T]) for i in range(2)]
        ws = s.sb("ws", [P, KC, D])
        wd = s.sb("wd", [P, 4, D])
        w2 = s.sb("w2", [P, NX, D])
        out = [s.ps(f"out{i}", [P, 2, 2, D]) for i in range(2)]
        w_loaded = s.sem("w_loaded")
        x_loaded = [s.sem(f"x_loaded{i}") for i in range(2)]
        w_ready = s.sem("w_ready")
        mm_done = s.sem("mm_done")
        out_free = s.sem("out_free")
        with nc.Block() as block:
            @block.sync
            def _(sp):
                sp.dma_start(ws[:], wsT.rearrange("c p o -> p c o")).then_inc(w_loaded, 16)
                sp.dma_start(wd[:], wtok.unsqueeze(0).to_broadcast([P, 4, D])).then_inc(w_loaded, 16)
                for b in range(B):
                    if b >= 2:
                        sp.wait_ge(mm_done, 2 * (b - 1))
                    sp.dma_start(xg[b % 2][:], xk[:, :, b * T:(b + 1) * T].rearrange("c p t -> p c t")) \
                        .then_inc(x_loaded[b % 2], 16)

            @block.vector
            def _(dve):
                dve.wait_ge(w_loaded, 32)
                for d in range(4):
                    dve.tensor_tensor(w2[:, KC * d:KC * d + KC, :], ws[:],
                                      wd[:, d:d + 1, :].to_broadcast([P, KC, D]), ALU.mult) \
                        .then_inc(w_ready, 1)

            @block.tensor
            def _(pe):
                pe.wait_ge(w_ready, 4)
                with pe.Fori(0, 2) as i:
                    for half in range(2):
                        pe.wait_ge(x_loaded[half], 16 * i + 16)
                        pe.wait_ge(out_free, 4 * i + 2 * half + 2)
                        for j in range(TB):
                            for c in range(NX):
                                mm = pe.matmul(out[half][:, j // 2, j % 2, :], xg[half][:, c, j * P:(j + 1) * P],
                                               w2[:, c, :], start=(c == 0), stop=(c == NX - 1))
                            if j % 2:
                                mm.then_inc(mm_done, 1)

            @block.scalar
            def _(act):
                act.sem_inc(out_free, 4)
                with act.Fori(0, 2) as i:
                    for half in range(2):
                        for u in range(2):
                            act.wait_ge(mm_done, 4 * i + 2 * half + u + 1)
                            act.activation(H[:, ds(8 * i + 4 * half + 2 * u, 2), :], out[half][:, u, :, :],
                                           ACT.Copy).then_inc(out_free, 1)



def stage_rows(nc, H, Y, XT, ident_d, post=None, second=None, w=None, b=None, out=None):
    with ExitStack() as stack:
        s = Space(nc, stack, "rows" + str(nc.next_id()))
        R = s.sb("R", [P, TB, D])
        S = s.sb("S", [P, TB, D])
        XN = s.sb("XN", [P, TB, D]) if second else R
        stats = s.sb("stats", [P, TB, 6])
        mv = s.sb("mv", [P, TB, 2])
        ms = s.sb("ms", [P, TB])
        sd = s.sb("sd", [P, TB])
        rstd = s.sb("rstd", [P, TB])
        epsc = s.sb("epsc", [P, 2])
        wb = s.sb("wb", [P, 2, D]) if w is not None else None
        ident = s.sb("ident", [P, P])
        tp = [s.ps(f"tp{i}", [P, KC, T]) for i in range(2)] if XT is not None else None
        w_loaded = s.sem("w_loaded")
        chain = s.sem("chain")
        stats_seen = s.sem("stats_seen")
        var_ready = s.sem("var_ready")
        sd_ready = s.sem("sd_ready")
        r_ready = s.sem("r_ready")
        r_copied = s.sem("r_copied")
        xn_ready = s.sem("xn_ready")
        turned = s.sem("turned")
        xt_copied = s.sem("xt_copied")
        stored = s.sem("stored")
        n_w = 1 + (w is not None) + (b is not None)
        norms = ([("ln", 1e-5)] if post == "ln" else []) + \
            ([(second, 1e-5 if second == "ln" else 1.1920928955078125e-07)] if second else [])
        NV = len(norms)
        keep = H if post == "ln" else Y if post == "add" else None
        with nc.Block() as block:
            @block.sync
            def _(sp):
                sp.dma_start(ident[:], ident_d).then_inc(w_loaded, 16)
                if w is not None:
                    sp.dma_start(wb[:, 0, :], w.unsqueeze(0).to_broadcast([P, D])).then_inc(w_loaded, 16)
                if b is not None:
                    sp.dma_start(wb[:, 1, :], b.unsqueeze(0).to_broadcast([P, D])).then_inc(w_loaded, 16)
                if out is not None:
                    for i in range(B):
                        sp.wait_ge(r_ready, i + 1)
                        sp.dma_start(out[i].rearrange("(j p) d -> p j d", p=P), R[:]).then_inc(stored, 16)
                    sp.wait_ge(stored, 16 * B)

            @block.vector
            def _(dve):
                for k, (_, eps) in enumerate(norms):
                    dve.memset(epsc[:, k:k + 1], eps).then_inc(chain, 1)
                dve.wait_ge(w_loaded, 16 * n_w)
                per = 0
                per += 1 if post else 0
                for kind, _ in norms:
                    per += 2 * TB + 1 + TB + (2 if kind == "rms" else 0)
                if w is not None:
                    per += 1 + (b is not None)
                with dve.Fori(0, B) as i:
                    c = Tally(chain, per * i + NV)

                    def norm(k, kind, src, dst):
                        for j in range(TB):
                            c.inc(dve.bn_stats(stats[:, j, :], src[:, j, :]))
                        c.wait(dve)
                        dve.sem_inc(stats_seen, 1)
                        for j in range(TB):
                            last = dve.bn_aggr(mv[:, j, :], stats[:, j, :])
                            c.inc(last)
                        if kind == "rms":
                            c.wait(dve)
                            c.inc(dve.tensor_tensor(ms[:], mv[:, :, 0], mv[:, :, 0], ALU.mult))
                            c.wait(dve)
                            c.inc(dve.tensor_tensor(ms[:], ms[:], mv[:, :, 1], ALU.add))
                        c.wait(dve)
                        dve.sem_inc(var_ready, 1)
                        dve.wait_ge(sd_ready, NV * i + k + 1)
                        c.inc(dve.reciprocal(rstd[:], sd[:]))
                        c.wait(dve)
                        for j in range(TB):
                            if kind == "rms":
                                c.inc(dve.tensor_scalar(dst[:, j, :], src[:, j, :], rstd[:, j:j + 1], None, ALU.mult))
                            else:
                                c.inc(dve.tensor_scalar(dst[:, j, :], src[:, j, :], mv[:, j, 0:1], rstd[:, j:j + 1],
                                                        ALU.subtract, ALU.mult))
                        c.wait(dve)

                    if XT is not None and not second:
                        dve.wait_ge(turned, i + 1)
                    if post:
                        if post == "add" or not norms:
                            dst = R
                        else:
                            dst = S
                        if keep is not None:
                            dve.wait_ge(r_copied, i + 1)
                        c.inc(dve.tensor_tensor(dst[:], H[:, ds(TB * i, TB), :], Y[:, ds(TB * i, TB), :], ALU.add))
                        c.wait(dve)
                        if post == "ln":
                            if out is not None:
                                dve.wait_ge(stored, 16 * i)
                            norm(0, "ln", S, R)
                        dve.sem_inc(r_ready, 1)
                    else:
                        dve.tensor_copy(R[:], H[:, ds(TB * i, TB), :]).then_inc(r_ready, 1)
                        dve.wait_ge(r_ready, i + 1)
                    if second:
                        dve.wait_ge(turned, i + 1)
                        norm(NV - 1, second, R, XN)
                        if w is not None:
                            c.inc(dve.tensor_tensor(XN[:], XN[:], wb[:, 0:1, :].to_broadcast([P, TB, D]), ALU.mult))
                            c.wait(dve)
                        if b is not None:
                            c.inc(dve.tensor_tensor(XN[:], XN[:], wb[:, 1:2, :].to_broadcast([P, TB, D]), ALU.add))
                            c.wait(dve)
                    dve.sem_inc(xn_ready, 1)

            @block.scalar
            def _(act):
                if NV:
                    act.wait_ge(chain, NV)
                if keep is not None:
                    act.sem_inc(r_copied, 1)
                act.sem_inc(xt_copied, 2)
                with act.Fori(0, B) as i:
                    for k, (kind, _) in enumerate(norms):
                        act.wait_ge(var_ready, NV * i + k + 1)
                        src = ms[:] if kind == "rms" else mv[:, :, 1]
                        act.activation(sd[:], src, ACT.Sqrt, bias=epsc[:, k:k + 1]).then_inc(sd_ready, 1)
                    if keep is not None:
                        act.wait_ge(r_ready, i + 1)
                        act.activation(keep[:, ds(TB * i, TB), :], R[:], ACT.Copy).then_inc(r_copied, 1)
                    if XT is not None:
                        act.wait_ge(turned, i + 2)
                        for k in range(KC):
                            act.activation(XT[:, k, ds(T * i, T)], tp[0][:, k, :], ACT.Copy).then_inc(xt_copied, 1)

            @block.tensor
            def _(pe):
                if XT is None:
                    return
                pe.wait_ge(w_loaded, 16 * n_w)
                pe.sem_inc(turned, 1)
                with pe.Fori(0, B) as i:
                    pe.wait_ge(xn_ready, i + 1)
                    pe.wait_ge(xt_copied, KC * i + KC)
                    for j in range(TB):
                        for k in range(KC):
                            last = pe.transpose(tp[0][:, k, j * P:(j + 1) * P], XN[:, j, k * P:(k + 1) * P], ident[:])
                    last.then_inc(turned, 1)



HN, HD = 8, 32
TL = 16
TH = T // TL


def stage_cell_inputs(nc, XT, KN, QR, V, BT, w_in, w_kq, w_vb, b_beta):
    with ExitStack() as stack:
        s = Space(nc, stack, "ci")
        XP = s.sb("XP", [P, KC, B * T])
        wi = s.sb("wi", [P, KC, D])
        wkq = s.sb("wkq", [P, KC, 2 * D])
        wvb = s.sb("wvb", [P, HN, KC, 2 * HD])
        wh = [s.sb(f"wh{i}", [P, KC, 2 * HD]) for i in range(2)]
        bb = s.sb("bb", [P, HN])
        xs = [s.sb(f"xs{i}", [P, KC, P]) for i in range(4)]
        sq = [s.sb(f"sq{i}", [P, D]) for i in range(4)]
        ss = s.sb("ss", [P, TL * HN])
        nrm = s.sb("nrm", [P, TL * HN])
        bank = [s.ps(f"bank{i}", [P, 512]) for i in range(8)]
        loaded = s.sem("loaded")
        xp_mm = s.sem("xp_mm")
        xp_ready = s.sem("xp_ready")
        xs_ready = s.sem("xs_ready")
        kq_mm = s.sem("kq_mm")
        k_copied = s.sem("k_copied")
        q_copied = s.sem("q_copied")
        sq_ready = s.sem("sq_ready")
        ss_ready = s.sem("ss_ready")
        nrm_ready = s.sem("nrm_ready")
        inv = s.sem("inv")
        wh_ready = s.sem("wh_ready")
        vb_mm = s.sem("vb_mm")
        vb_copied = s.sem("vb_copied")
        with nc.Block() as block:
            @block.sync
            def _(sp):
                sp.dma_start(wi[:], w_in.rearrange("c p o -> p c o")).then_inc(loaded, 16)
                sp.dma_start(wkq[:], w_kq.rearrange("c p o -> p c o")).then_inc(loaded, 16)
                sp.dma_start(wvb[:], w_vb.rearrange("h p c o -> p h c o")).then_inc(loaded, 16)
                sp.dma_start(bb[:], b_beta).then_inc(loaded, 16)

            @block.tensor
            def _(pe):
                pe.wait_ge(loaded, 64)
                with pe.Fori(0, B) as b:
                    for e in range(KC):
                        pe.wait_ge(xp_ready, KC * b + e + 1)
                        for k in range(KC):
                            mm = pe.matmul(bank[e][:], wi[:, k, e * P:(e + 1) * P], XT[:, k, ds(b * T, T)],
                                           start=(k == 0), stop=(k == KC - 1))
                        mm.then_inc(xp_mm, 1)
                with pe.Fori(0, TL // 4) as i:
                    for u in range(4):
                        pe.wait_ge(xs_ready, 4 * i + u + 1)
                        pe.wait_ge(k_copied, 4 * i + u + 1)
                        pe.wait_ge(q_copied, 4 * i + u + 1)
                        pe.wait_ge(sq_ready, 4 * i + u + 1)
                        for k in range(KC):
                            mm = pe.matmul(bank[2 + u][:], xs[u][:, k, :], wkq[:, k, :],
                                           start=(k == 0), stop=(k == KC - 1))
                        mm.then_inc(kq_mm, 1)
                with pe.Fori(0, HN // 2) as i:
                    for u in range(2):
                        pe.wait_ge(wh_ready, 2 * i + u + 1)
                        for ty in range(2):
                            pe.wait_ge(vb_copied, 4 * i + 2 * u + ty + 1)
                            for b in range(B):
                                for k in range(KC):
                                    mm = pe.matmul(bank[2 * ty + u][Q4 * b:Q4 * b + Q4, :],
                                                   wh[u][:, k, ty * HD:(ty + 1) * HD], XP[:, k, b * T:(b + 1) * T],
                                                   start=(k == 0), stop=(k == KC - 1))
                            mm.then_inc(vb_mm, 1)

            @block.scalar
            def _(act):
                act.sem_inc(xp_ready, 2)
                with act.Fori(0, B) as b:
                    for e in range(KC):
                        act.wait_ge(xp_mm, KC * b + e + 1)
                        act.activation(XP[:, e, ds(b * T, T)], bank[e][:], ACT.Silu).then_inc(xp_ready, 1)
                act.sem_inc(q_copied, 4)
                act.sem_inc(sq_ready, 4)
                with act.Fori(0, TL // 4) as i:
                    for u in range(4):
                        act.wait_ge(kq_mm, 4 * i + u + 1)
                        act.wait_ge(ss_ready, 4 * i + u + 1)
                        act.activation(sq[u][:], bank[2 + u][:, 0:D], ACT.Square).then_inc(sq_ready, 1)
                        act.activation(QR[:, ds(4 * i + u, 1), :], bank[2 + u][:, D:2 * D], ACT.Copy) \
                            .then_inc(q_copied, 1)
                act.wait_ge(ss_ready, 4 + TL)
                act.activation(nrm[:], ss[:], ACT.Sqrt).then_inc(nrm_ready, 1)
                act.sem_inc(vb_copied, 4)
                with act.Fori(0, HN // 2) as i:
                    for u in range(2):
                        act.wait_ge(vb_mm, 4 * i + 2 * u + 1)
                        act.activation(V[:, ds(2 * i + u, 1), :], bank[u][:], ACT.Copy).then_inc(vb_copied, 1)
                        act.wait_ge(vb_mm, 4 * i + 2 * u + 2)
                        act.activation(BT[:, ds(2 * i + u, 1), :], bank[2 + u][:], ACT.Sigmoid,
                                       bias=bb[:, ds(2 * i + u, 1)]).then_inc(vb_copied, 1)

            @block.vector
            def _(dve):
                dve.sem_inc(k_copied, 4)
                dve.sem_inc(ss_ready, 4)
                dve.wait_ge(xp_ready, 2 + KC * B)
                xpv = XP[:].rearrange("p k (n l) -> p k n l", l=TL)
                with dve.Fori(0, TL // 4) as i:
                    for u in range(4):
                        dve.wait_ge(sq_ready, 4 * i + u + 1)
                        dve.tensor_copy(xs[u][:], xpv[:, :, :, ds(4 * i + u, 1)]).then_inc(xs_ready, 1)
                    for u in range(4):
                        dve.wait_ge(q_copied, 4 * i + u + 5)
                        dve.tensor_copy(KN[:, ds(4 * i + u, 1), :], bank[2 + u][:, 0:D]).then_inc(k_copied, 1)
                        dve.wait_ge(sq_ready, 4 * i + u + 5)
                        dve.tensor_reduce(ss[:, ds(HN * (4 * i + u), HN)],
                                          sq[u][:].rearrange("p (h j) -> p h j", h=HN), AX.X, ALU.add) \
                            .then_inc(ss_ready, 1)
                dve.wait_ge(loaded, 64)
                dve.wait_ge(k_copied, 4 + TL)
                dve.wait_ge(nrm_ready, 1)
                dve.tensor_scalar(nrm[:], nrm[:], 1e-6, None, ALU.add).then_inc(inv, 1)
                dve.wait_ge(inv, 1)
                dve.reciprocal(ss[:], nrm[:]).then_inc(inv, 1)
                dve.wait_ge(inv, 2)
                knv = KN[:].rearrange("p l (h j) -> p (l h) j", h=HN)
                dve.tensor_tensor(knv, knv, ss[:].unsqueeze(2).to_broadcast([P, TL * HN, HD]), ALU.mult) \
                    .then_inc(inv, 1)

            @block.gpsimd
            def _(pool):
                pool.wait_ge(loaded, 64)
                with pool.Fori(0, HN // 2) as i:
                    for u in range(2):
                        if u == 0:
                            pool.wait_ge(vb_copied, 4 * i + 1)
                        pool.wait_ge(vb_copied, 4 * i + 2 * u + 1)
                        pool.wait_ge(vb_copied, 4 * i + 2 * u + 2)
                        pool.tensor_copy(wh[u][:], wvb[:, ds(2 * i + u, 1), :, :]).then_inc(wh_ready, 1)


def stage_cell(nc, KN, QR, V, BT, OUT, ident_d):
    NCH = 2
    CH = HN // NCH
    CW = CH * HD
    with ExitStack() as stack:
        s = Space(nc, stack, "cell")
        ident = s.sb("ident", [P, P])
        sel = s.sb("sel", [P, P])
        S = [s.sb(f"S{i}", [P, NCH, CW]) for i in range(2)]
        T1 = s.sb("T1", [P, NCH, CW])
        T2 = s.sb("T2", [P, NCH, CW])
        T3 = s.sb("T3", [P, NCH, CW])
        BS = s.sb("BS", [P, NCH, CW])
        R = s.sb("R", [P, NCH, CH])
        DL = s.sb("DL", [P, NCH, CH])
        QB = [s.sb(f"QB{i}", [P, 2, NCH, CW]) for i in range(2)]
        SQ = s.sb("SQ", [P, TL, NCH, CW])
        kb = [s.ps(f"kb{i}", [P, 2, NCH, CW]) for i in range(4)]
        qb = [s.ps(f"qb{i}", [P, 2, NCH, CW]) for i in range(2)]
        loaded = s.sem("loaded")
        sel_ready = s.sem("sel_ready")
        kb_ready = s.sem("kb_ready")
        qb_ready = s.sem("qb_ready")
        qb_copied = s.sem("qb_copied")
        sk_done = s.sem("sk_done")
        r_done = s.sem("r_done")
        delta_done = s.sem("delta_done")
        outer_done = s.sem("outer_done")
        sum_done = s.sem("sum_done")
        state_ready = s.sem("state_ready")
        bs_ready = s.sem("bs_ready")
        sq_done = s.sem("sq_done")
        out_done = s.sem("out_done")
        NP = TL // 2
        h4 = lambda ap: ap.rearrange("p (h j) -> p h j", h=CH)
        with nc.Block() as block:
            @block.sync
            def _(sp):
                sp.dma_start(ident[:], ident_d).then_inc(loaded, 16)

            @block.tensor
            def _(pe):
                with pe.Fori(0, TH) as i:
                    pe.wait_ge(sel_ready, i + 1)
                    for pp in range(NP):
                        pe.wait_ge(outer_done, 4 * (NP * i + pp) + 4)
                        pe.matmul(kb[pp % 4][:], sel[:], KN[:, 2 * pp:2 * pp + 2, :],
                                  start=True, stop=True).then_inc(kb_ready, 1)
                        pe.wait_ge(qb_copied, 2 * (NP * i + pp) + 2)
                        pe.matmul(qb[pp % 2][:], sel[:], QR[:, 2 * pp:2 * pp + 2, :],
                                  start=True, stop=True).then_inc(qb_ready, 1)

            @block.vector
            def _(dve):
                dve.memset(S[1][:], 0.0).then_inc(state_ready, 2)
                dve.sem_inc(outer_done, 16)
                dve.sem_inc(out_done, NP)
                with dve.Fori(0, TH) as i:
                    def reduce_out(pp):
                        dve.wait_ge(sq_done, 2 * TL * i + 8 + 4 * pp + 4)
                        dve.tensor_reduce(OUT[:, ds(TL * i + 2 * pp, 2), :],
                                          SQ[:, 2 * pp:2 * pp + 2, :, :].rearrange("p t c (h j) -> p t (c h) j", h=CH),
                                          AX.X, ALU.add).then_inc(out_done, 1)

                    for t in range(TL):
                        if t % 2 == 0:
                            dve.wait_ge(kb_ready, NP * i + t // 2 + 1)
                        kt = kb[(t // 2) % 4]
                        for c in range(NCH):
                            n = 2 * TL * i + 2 * t + c + 1
                            dve.wait_ge(state_ready, n)
                            dve.tensor_tensor(T1[:, c, :], S[(t + 1) % 2][:, c, :], kt[:, t % 2, c, :], ALU.mult) \
                                .then_inc(sk_done, 1)
                            dve.wait_ge(sk_done, n)
                            dve.tensor_reduce(R[:, c, :], h4(T1[:, c, :]), AX.X, ALU.add).then_inc(r_done, 1)
                            dve.wait_ge(r_done, n)
                            dve.tensor_tensor(DL[:, c, :], V[:, c * CH:(c + 1) * CH, ds(TL * i + t, 1)],
                                              R[:, c, :], ALU.subtract).then_inc(delta_done, 1)
                            dve.wait_ge(delta_done, n)
                            dve.tensor_tensor(h4(T2[:, c, :]), DL[:, c, :].unsqueeze(2).to_broadcast([P, CH, HD]),
                                              h4(kt[:, t % 2, c, :]), ALU.mult).then_inc(outer_done, 1)
                            dve.wait_ge(outer_done, n + 16)
                            dve.wait_ge(bs_ready, n)
                            dve.tensor_tensor(T3[:, c, :], T2[:, c, :], BS[:, c, :], ALU.add).then_inc(sum_done, 1)
                        if t % 2 == 1 and t >= 3:
                            reduce_out((t - 3) // 2)
                    reduce_out(NP - 1)

            @block.scalar
            def _(act):
                act.wait_ge(loaded, 16)
                act.sem_inc(qb_copied, 4)
                rows = ident[:].rearrange("p (b t) -> p b t", b=B)
                with act.Fori(0, TH) as i:
                    def copy_queries(pp, c):
                        act.wait_ge(qb_ready, NP * i + pp + 1)
                        act.wait_ge(sq_done, 2 * TL * i + 4 * pp + 4)
                        act.activation(QB[pp % 2][:, :, c, :], qb[pp % 2][:, :, c, :], ACT.Copy) \
                            .then_inc(qb_copied, 1)

                    act.wait_ge(qb_copied, 2 * NP * i + 4)
                    act.activation(sel[:].rearrange("p (b t) -> p b t", b=B),
                                   rows[:, :, ds(i, 1)].to_broadcast([P, B, Q4]), ACT.Copy).then_inc(sel_ready, 1)
                    copy_queries(0, 0)
                    copy_queries(0, 1)
                    for t in range(TL):
                        for c in range(NCH):
                            n = 2 * TL * i + 2 * t + c + 1
                            act.wait_ge(sum_done, n)
                            act.wait_ge(sq_done, n + 4)
                            act.activation(S[t % 2][:, c, :], T3[:, c, :], ACT.Tanh).then_inc(state_ready, 1)
                            if t % 2 == 1 and t < TL - 1:
                                copy_queries(t // 2 + 1, c)

            @block.gpsimd
            def _(pool):
                pool.sem_inc(sq_done, 8)
                with pool.Fori(0, TH) as i:
                    def query(t, c):
                        if t % 2 == 0:
                            pool.wait_ge(qb_copied, 2 * (NP * i + t // 2) + 4 + 2)
                            pool.wait_ge(out_done, NP * i + t // 2 + 1)
                        pool.tensor_tensor(SQ[:, t, c, :], S[t % 2][:, c, :], QB[(t // 2) % 2][:, t % 2, c, :],
                                           ALU.mult).then_inc(sq_done, 1)

                    for t in range(TL):
                        for c in range(NCH):
                            n = 2 * TL * i + 2 * t + c + 1
                            pool.wait_ge(state_ready, n)
                            pool.wait_ge(outer_done, n + 14)
                            pool.tensor_tensor(h4(BS[:, c, :]), h4(S[(t + 1) % 2][:, c, :]),
                                               BT[:, c * CH:(c + 1) * CH, ds(TL * i + t, 1)].to_broadcast([P, CH, HD]),
                                               ALU.mult).then_inc(bs_ready, 1)
                            if t:
                                query(t - 1, c)
                    for c in range(NCH):
                        pool.wait_ge(state_ready, 2 * TL * i + 2 * TL + c + 1)
                        query(TL - 1, c)


def stage_cell_out(nc, OUT, Y, w_out):
    with ExitStack() as stack:
        s = Space(nc, stack, "co")
        wo = s.sb("wo", [P, HN, D])
        si = s.sb("si", [P, HN, P])
        cc = s.sb("cc", [P, HN, P])
        y = [s.ps(f"y{i}", [P, 512]) for i in range(B)]
        loaded = s.sem("loaded")
        si_ready = s.sem("si_ready")
        cc_ready = s.sem("cc_ready")
        mm_done = s.sem("mm_done")
        copied = s.sem("copied")
        with nc.Block() as block:
            @block.sync
            def _(sp):
                sp.dma_start(wo[:], w_out).then_inc(loaded, 16)

            @block.scalar
            def _(act):
                act.sem_inc(copied, B)
                with act.Fori(0, TB) as j:
                    act.wait_ge(cc_ready, j + 1)
                    act.activation(si[:], OUT[:, ds(P * j, P), :].rearrange("p t h -> p h t"), ACT.Silu) \
                        .then_inc(si_ready, 1)
                    for b in range(B):
                        act.wait_ge(mm_done, B * j + b + 1)
                        act.activation(Y[:, ds(j + TB * b, 1), :], y[b][:, 0:D], ACT.Copy).then_inc(copied, 1)

            @block.vector
            def _(dve):
                dve.sem_inc(cc_ready, 1)
                with dve.Fori(0, TB) as j:
                    dve.wait_ge(si_ready, j + 1)
                    dve.wait_ge(copied, B * j + B)
                    dve.tensor_tensor(cc[:], si[:], OUT[:, ds(P * j, P), :].rearrange("p t h -> p h t"), ALU.mult) \
                        .then_inc(cc_ready, 1)

            @block.tensor
            def _(pe):
                pe.wait_ge(loaded, 16)
                with pe.Fori(0, TB) as j:
                    pe.wait_ge(cc_ready, j + 2)
                    pe.wait_ge(copied, B * j + B)
                    for b in range(B):
                        q = slice(Q4 * b, Q4 * b + Q4)
                        for h in range(HN):
                            mm = pe.matmul(y[b][:, 0:D], cc[q, h, :], wo[q, h, :], start=(h == 0), stop=(h == HN - 1))
                        mm.then_inc(mm_done, 1)



AH = 16
AD = D // AH
AG = 4
NG = AH // AG
NP = 3
Q_PARTS = (range(0, 3), range(0, 2), range(0, 1))
K_PARTS = (0, 1, 2)
QK_ROWS = AD * sum(len(run) for run in Q_PARTS)
QK_LOADS = 2 * len(Q_PARTS)
MAX_ROWS = slice(QK_ROWS, QK_ROWS + NP)


def stage_heads(nc, X, V, split_d, w, bias_cols, v_bias, rope):
    turned = rope is not None
    with ExitStack() as stack:
        s = Space(nc, stack, "hd" + str(nc.next_id()))
        bc = s.sb("bc", [P, 4])
        bv = s.sb("bv", [P, D])
        cs = s.sb("cs", [P, 2, T]) if turned else None
        XS = s.sb("XS", [P, KC, T])
        RA = [s.sb(f"RA{i}", [P, T]) for i in range(2)]
        RB = [s.sb(f"RB{i}", [P, T]) for i in range(2)]
        F = [s.sb(f"F{i}", [P, T]) for i in range(2)]
        R = [s.sb(f"R{i}", [P, T]) for i in range(2)]
        parts = [s.sb(f"parts{i}", [P, NP, T], BF16) for i in range(2)]
        pj = [[s.ps(f"pj{i}{m}", [P, T]) for m in range(2)] for i in range(2)]
        vb = [s.ps(f"vb{i}", [P, 2, D]) for i in range(2)]
        loaded = s.sem("loaded")
        xs_ready = s.sem("xs_ready")
        p_mm = s.sem("p_mm")
        p_free = s.sem("p_free")
        turn = s.sem("turn")
        f_ready = s.sem("f_ready")
        high_ready = s.sem("high_ready")
        rest_ready = s.sem("rest_ready")
        mid_ready = s.sem("mid_ready")
        low_ready = s.sem("low_ready")
        stored = [s.sem(f"stored{i}") for i in range(2)]
        passed = s.sem("passed")
        parts_free = s.sem("parts_free")
        v_mm = s.sem("v_mm")
        v_copied = s.sem("v_copied")
        n_load = 2 + turned
        tiles = [(n, half) for n in range(2) for half in range(2)]
        with nc.Block() as block:
            @block.sync
            def _(sp):
                sp.dma_start(bc[:], bias_cols).then_inc(loaded, 16)
                sp.dma_start(bv[:], v_bias.unsqueeze(0).to_broadcast([P, D])).then_inc(loaded, 16)
                if turned:
                    sp.dma_start(cs[:], rope).then_inc(loaded, 16)
                sp.sem_inc(parts_free, 2)
                with sp.Fori(0, B) as b:
                    for i, (n, half) in enumerate(tiles):
                        sp.wait_ge(low_ready, 4 * b + i + 1)
                        for c in range(NP):
                            sp.dma_start(split_d[n][ds(b, 1), half, c, :, :, :].rearrange("o d h t -> (o h) d t"),
                                         parts[i % 2][:, c, :]).then_inc(stored[i % 2], 16)
                        if i:
                            sp.wait_ge(stored[(i - 1) % 2], 16 * NP * (2 * b + (i + 1) // 2))
                            sp.sem_inc(parts_free, 1)
                    sp.wait_ge(stored[1], 16 * NP * (2 * b + 2))
                    sp.sem_inc(parts_free, 1)

            @block.tensor
            def _(pe):
                pe.sem_inc(v_mm, 2)
                with pe.Fori(0, B) as b:
                    for i, (n, half) in enumerate(tiles):
                        pe.wait_ge(p_free, 4 * b + i + 1)
                        for m in range(1 + turned):
                            wm = w["qk"[n] + ("r" if m else "")]
                            for k in range(KC):
                                mm = pe.matmul(pj[i % 2][m][:], wm[:, k, half * P:(half + 1) * P],
                                               X[:, k, ds(b * T, T)], start=(k == 0), stop=(k == KC - 1))
                            mm.then_inc(p_mm, 1)
                    pe.wait_ge(xs_ready, b + 1)
                    for j in range(TB):
                        if j % 2 == 0:
                            pe.wait_ge(v_copied, 2 * b + j // 2 + 1)
                        for k in range(KC):
                            mm = pe.matmul(vb[j // 2][:, j % 2, :], XS[:, k, j * P:(j + 1) * P], w["v"][:, k, :],
                                           start=(k == 0), stop=(k == KC - 1))
                        if j % 2:
                            mm.then_inc(v_mm, 1)

            @block.gpsimd
            def _(pool):
                with pool.Fori(0, B) as b:
                    pool.wait_ge(v_mm, 2 * b + 2)
                    pool.sem_inc(passed, 1)
                    pool.tensor_copy(XS[:], X[:, :, ds(b * T, T)]).then_inc(xs_ready, 1)
                    for i in range(4):
                        f = i % 2
                        if turned:
                            pool.wait_ge(turn, 2 * (4 * b + i) + 2)
                            pool.wait_ge(rest_ready, 4 * b + i + 1)
                            pool.tensor_tensor(F[f][:], RA[f][:], RB[f][:], ALU.add).then_inc(f_ready, 1)
                        pool.wait_ge(mid_ready, 4 * b + i + 1)
                        pool.tensor_tensor(parts[f][:, 2, :], R[f][:], parts[f][:, 1, :], ALU.subtract) \
                            .then_inc(low_ready, 1)

            @block.scalar
            def _(act):
                act.wait_ge(loaded, 16 * n_load)
                if not turned:
                    act.sem_inc(p_free, 2)
                with act.Fori(0, B) as b:
                    for i in range(4):
                        f = i % 2
                        if not turned:
                            act.wait_ge(p_mm, 4 * b + i + 1)
                            act.wait_ge(rest_ready, 4 * b + i + 1)
                            act.activation(F[f][:], pj[f][0][:], ACT.Identity, bias=bc[:, i:i + 1]) \
                                .then_inc(f_ready, 1)
                        act.wait_ge(f_ready, 4 * b + i + 1)
                        if not turned:
                            act.sem_inc(p_free, 1)
                        act.wait_ge(parts_free, 4 * b + i + 1)
                        act.activation(parts[f][:, 0, :], F[f][:], ACT.Copy).then_inc(high_ready, 1)
                        act.wait_ge(rest_ready, 4 * b + i + 3)
                        act.activation(parts[f][:, 1, :], R[f][:], ACT.Copy).then_inc(mid_ready, 1)

            @block.vector
            def _(dve):
                dve.wait_ge(loaded, 16 * n_load)
                dve.sem_inc(rest_ready, 2)
                dve.sem_inc(v_copied, 2)
                if turned:
                    dve.sem_inc(p_free, 2)
                with dve.Fori(0, B) as b:
                    for i in range(4):
                        f = i % 2
                        if turned:
                            dve.wait_ge(p_mm, 2 * (4 * b + i) + 2)
                            dve.tensor_tensor(RA[f][:], pj[f][0][:], cs[:, 0, :], ALU.mult).then_inc(turn, 1)
                            dve.tensor_tensor(RB[f][:], pj[f][1][:], cs[:, 1, :], ALU.mult).then_inc(turn, 1)
                            dve.wait_ge(turn, 2 * (4 * b + i) + 2)
                            dve.sem_inc(p_free, 1)
                        dve.wait_ge(high_ready, 4 * b + i + 1)
                        dve.tensor_tensor(R[f][:], F[f][:], parts[f][:, 0, :], ALU.subtract) \
                            .then_inc(rest_ready, 1)
                    for f in range(2):
                        dve.wait_ge(v_mm, 2 * b + f + 3)
                        dve.tensor_tensor(V[:, ds(TB * b + 2 * f, 2), :], vb[f][:],
                                          bv[:].unsqueeze(1).to_broadcast([P, 2, D]), ALU.add) \
                            .then_inc(v_copied, 1)


def stage_softmax(nc, V, AO, split_d, ident_d, causal):
    if causal:
        a_steps = [(0, range(0, 4)), (1, range(0, 2)), (1, range(2, 4))]
        a_steps += [(qt, range(h, h + 1)) for qt in (2, 3) for h in range(AG)]
        b_steps = [(0, range(0, 2)), (0, range(2, 4)), (1, range(0, 2)), (1, range(2, 4)),
                   (2, range(0, 4)), (3, range(0, 4))]
    else:
        a_steps = [(qt, range(h, h + 1)) for qt in range(TB) for h in range(AG)]
        b_steps = [(kt, range(h, h + 2)) for kt in range(TB) for h in (0, 2)]
    NA, NB = len(a_steps), len(b_steps)
    TAIL = 4
    b_upto = [max(i for i, st in enumerate(b_steps) if st[0] == kt) + 1 for kt in range(TB)]
    nk = [(qt + 1) * P if causal else T for qt in range(TB)]
    q0 = [kt * P if causal else 0 for kt in range(TB)]
    pitch = [T, T, T // 2, T // 4] if causal else [T] * TB
    with ExitStack() as stack:
        s = Space(nc, stack, "sm" + str(nc.next_id()))
        ident = s.sb("ident", [P, P])
        identb = s.sb("identb", [P, P], BF16)
        maska = s.sb("maska", [P, AG, P], BF16)
        maskb = s.sb("maskb", [P, AG, P], BF16)
        QS = [s.sb(f"QS{i}", [P, AG, T], BF16) for i in range(4)]
        KS = [s.sb(f"KS{i}", [P, AG, T], BF16) for i in range(4)]
        VG = [s.sb(f"VG{i}", [P, TB, AG, Q4]) for i in range(2)]
        MX = [s.sb(f"MX{i}", [P, TB, AG]) for i in range(2)]
        MR = s.sb("MR", [P, TB, AG])
        MQ = s.sb("MQ", [P, TB, AG])
        MP = s.sb("MP", [P, TB, NP, AG], BF16)
        MT = [s.sb(f"MT{i}", [AG * NP, T], BF16) for i in range(2)]
        EX = s.sb("EX", [P, TB, AG, T])
        at = [s.ps(f"at{i}", [P, T]) for i in range(2)]
        bt = [s.ps(f"bt{i}", [P, 2 * T]) for i in range(2)]
        pv = s.ps("pv", [P, T])
        mt = s.ps("mt", [P, TB, P], BF16)
        loaded = s.sem("loaded")
        identb_ready = s.sem("identb_ready")
        drawn = s.sem("drawn")
        passed = s.sem("passed")
        qk_loaded = [s.sem(f"qk_loaded{i}") for i in range(4)]
        max_loaded = [s.sem(f"max_loaded{i}") for i in range(4)]
        a_mm = s.sem("a_mm")
        a_max = s.sem("a_max")
        b_mm = s.sem("b_mm")
        b_exp = s.sem("b_exp")
        split_step = s.sem("split_step")
        max_split = s.sem("max_split")
        max_turned = s.sem("max_turned")
        mt_ready = s.sem("mt_ready")
        v_ready = s.sem("v_ready")
        pv_mm = s.sem("pv_mm")
        ao_ready = s.sem("ao_ready")

        def after(b, hg, n):
            b2, g2 = b + (hg + n) // NG, (hg + n) % NG
            return None if isinstance(b2, int) and b2 >= B else (b2, g2)

        def units(eng, turn):
            with eng.Fori(0, B - 1) as b:
                for hg in range(NG):
                    turn(b, hg)
            for hg in range(NG):
                turn(B - 1, hg)

        drawn_all = []
        with nc.Block() as block:
            @block.sync
            def _(sp):
                def load(b, hg):
                    sp.wait_ge(b_mm, NB * (NG * b + hg + 1))
                    row = 0
                    for q_run, k_part in zip(Q_PARTS, K_PARTS):
                        rows = slice(row, row + AD * len(q_run))
                        heads = slice(hg % 2 * AG, (hg % 2 + 1) * AG)
                        q, k = (split_d[n][ds(b, 1), hg // 2, :, :, heads, :] for n in range(2))
                        sp.dma_start(QS[hg][rows, :, :],
                                     q[:, q_run.start:q_run.stop].rearrange("o c d h t -> (o c d) (h t)")) \
                            .then_inc(qk_loaded[hg], 16)
                        sp.dma_start(KS[hg][rows, :, :],
                                     k[:, k_part].rearrange("o d h t -> o d (h t)")
                                     .to_broadcast([len(q_run), AD, AG * T])).then_inc(qk_loaded[hg], 16)
                        row = rows.stop

                def maxima(b, hg):
                    sp.wait_ge(mt_ready, NG * b + hg + 2)
                    sp.dma_start(QS[hg][MAX_ROWS, :, :], MT[hg % 2][:]).then_inc(max_loaded[hg], 16)

                def turn(b, hg):
                    if after(b, hg, 2):
                        load(*after(b, hg, 2))
                    maxima(b, hg)

                sp.dma_start(ident[:], ident_d).then_inc(loaded, 16)
                load(0, 0)
                load(0, 1)
                units(sp, turn)

            @block.gpsimd
            def _(pool):
                c = Tally(drawn)
                for i in range(4):
                    c.inc(pool.memset(KS[i][MAX_ROWS, :, :], 1.0))
                c.wait(pool)
                for i in range(2):
                    c.inc(pool.memset(VG[i][:], 0.0))
                    c.wait(pool)
                    c.inc(pool.memset(VG[i][:, :, :, AD:AD + 2], 1.0))
                if causal:
                    for mask, sign in ((maska, 1), (maskb, -1)):
                        c.inc(pool.memset(mask[:], 0.0))
                        c.wait(pool)
                        c.inc(pool.affine_select(out=mask[:], in_=mask[:], compare_op=ALU.is_ge, fill=-1e30,
                                                 base=0, pattern=[[0, AG], [-sign, P]],
                                                 channel_multiplier=sign))
                drawn_all.append(c.n)

                def split(b, hg):
                    u, m = NG * b + hg, MX[hg % 2]
                    pool.wait_ge(a_max, NA * (u + 1))
                    if not (isinstance(u, int) and u == 0):
                        pool.wait_ge(max_turned, u)
                    pool.sem_inc(passed, 1)
                    pool.tensor_copy(MP[:, :, 0, :], m[:]).then_inc(split_step, 1)
                    pool.wait_ge(split_step, 4 * u + 1)
                    pool.tensor_tensor(MR[:], m[:], MP[:, :, 0, :], ALU.subtract).then_inc(split_step, 1)
                    pool.wait_ge(split_step, 4 * u + 2)
                    pool.sem_inc(passed, 1)
                    pool.tensor_copy(MP[:, :, 1, :], MR[:]).then_inc(split_step, 1)
                    pool.wait_ge(split_step, 4 * u + 3)
                    pool.tensor_tensor(MP[:, :, 2, :], MR[:], MP[:, :, 1, :], ALU.subtract) \
                        .then_inc(split_step, 1)
                    pool.wait_ge(split_step, 4 * u + 4)
                    pool.sem_inc(max_split, 1)

                def values(b, hg):
                    if not (isinstance(b, int) and NG * b + hg == 0):
                        pool.wait_ge(pv_mm, TB * (NG * b + hg))
                        pool.sem_inc(passed, 1)
                    pool.tensor_copy(VG[hg % 2][:, :, :, 0:AD],
                                     V[:, ds(TB * b, TB), hg * AG * AD:(hg + 1) * AG * AD]
                                     .rearrange("p j (h d) -> p j h d", h=AG)).then_inc(v_ready, 1)

                def turn(b, hg):
                    if after(b, hg, 1):
                        values(*after(b, hg, 1))
                        split(*after(b, hg, 1))

                pool.sem_inc(max_split, 2)
                values(0, 0)
                split(0, 0)
                units(pool, turn)

            @block.tensor
            def _(pe):
                def first_pass(b, hg, i):
                    index = NA * (NG * b + hg) + i
                    qt, heads = a_steps[i]
                    bank = at[(NA * hg + i) % 2]
                    if not (isinstance(index, int) and index < 2):
                        pe.wait_ge(a_max, index - 1)
                    n = nk[qt]
                    for k, h in enumerate(heads):
                        mm = pe.matmul(bank[:, k * n:(k + 1) * n], QS[hg][0:QK_ROWS, h, qt * P:(qt + 1) * P],
                                       KS[hg][0:QK_ROWS, h, 0:n], start=(k == 0), stop=not causal)
                    if causal:
                        at_end = bank[:, 0:len(heads) * n].rearrange("p (h k) -> p h k", k=n)[:, :, n - P:n]
                        mm = pe.matmul(at_end, identb[:], maska[:, 0:len(heads), :], start=False, stop=True)
                    mm.then_inc(a_mm, 1)

                def second_pass(b, hg, i):
                    kt, heads = b_steps[i]
                    bank = bt[i % 2]
                    pe.wait_ge(b_exp, NB * (NG * b + hg) + i + 1)
                    n, w = T - q0[kt], pitch[kt]
                    for k, h in enumerate(heads):
                        mm = pe.matmul(bank[:, k * w:k * w + n], KS[hg][0:MAX_ROWS.stop, h, kt * P:(kt + 1) * P],
                                       QS[hg][0:MAX_ROWS.stop, h, q0[kt]:T],
                                       start=(k % (T // w) == 0), stop=not causal)
                    if causal:
                        per = T // w
                        for k in range(0, len(heads), per):
                            first = bank[:, k * w:(k + per) * w].rearrange("p (h q) -> p h q", q=w)[:, :, 0:P]
                            mm = pe.matmul(first, identb[:], maskb[:, 0:per, :], start=False, stop=True)
                    mm.then_inc(b_mm, 1)

                def turn_maxima(b, hg):
                    u = NG * b + hg
                    pe.wait_ge(max_split, u + 3)
                    pe.wait_ge(mt_ready, u + 1)
                    for qt in range(TB):
                        mm = pe.transpose(mt[0:AG * NP, qt, :], MP[:, qt, :, :].rearrange("p c h -> p (c h)"),
                                          identb[:])
                    mm.then_inc(max_turned, 1)

                def weigh(b, hg, kt):
                    u = NG * b + hg
                    if kt == 0:
                        pe.wait_ge(v_ready, u + 1)
                        pe.wait_ge(ao_ready, u + 1)
                    pe.wait_ge(b_exp, NB * u + b_upto[kt] + 2)
                    for h in range(AG):
                        mm = pe.matmul(pv[h * Q4:(h + 1) * Q4, q0[kt]:T], VG[hg % 2][:, kt, h, :],
                                       EX[:, kt, h, q0[kt]:T], start=(kt == 0), stop=(kt == TB - 1))
                    mm.then_inc(pv_mm, 1)

                def turn(b, hg):
                    ahead = after(b, hg, 2)
                    if ahead:
                        pe.wait_ge(qk_loaded[ahead[1]], 16 * QK_LOADS * (ahead[0] + 1))
                    pe.wait_ge(max_loaded[hg], 16 * (b + 1))
                    done = weighed = 0
                    for i in range(NB):
                        second_pass(b, hg, i)
                        if i == NB // 2 and after(b, hg, 1):
                            turn_maxima(*after(b, hg, 1))
                        upto = (i + 1) * (NA - TAIL) // NB
                        if ahead:
                            for k in range(done, upto):
                                first_pass(*ahead, k)
                        done = upto
                        if i == b_upto[weighed] + 1:
                            weigh(b, hg, weighed)
                            weighed += 1
                    for k in range(done, NA):
                        if k == NA - TAIL // 2:
                            for kt in range(weighed, TB):
                                weigh(b, hg, kt)
                        if ahead:
                            first_pass(*ahead, k)

                pe.wait_ge(loaded, 16)
                pe.wait_ge(identb_ready, 1)
                pe.wait_ge(drawn, drawn_all[0])
                pe.sem_inc(b_mm, 4 * NB)
                pe.sem_inc(pv_mm, TB)
                for hg in range(2):
                    pe.wait_ge(qk_loaded[hg], 16 * QK_LOADS)
                    for i in range(NA):
                        first_pass(0, hg, i)
                turn_maxima(0, 0)
                units(pe, turn)

            @block.scalar
            def _(act):
                def take_maxima(b, hg):
                    act.wait_ge(max_turned, NG * b + hg + 1)
                    act.activation(MT[hg % 2][:], mt[0:AG * NP, :, :].rearrange("p j t -> p (j t)"), ACT.Copy) \
                        .then_inc(mt_ready, 1)

                def turn(b, hg):
                    u = NG * b + hg
                    for i, (kt, heads) in enumerate(b_steps):
                        act.wait_ge(b_mm, NB * (u + 4) + i + 1)
                        if i == 0 or b_steps[i - 1][0] != kt:
                            act.wait_ge(pv_mm, TB * u + kt + 1)
                        w = pitch[kt]
                        src = bt[i % 2][:, 0:len(heads) * w].rearrange("p (h q) -> p h q", q=w)
                        act.activation(EX[:, kt, heads[0]:heads[-1] + 1, q0[kt]:T], src[:, :, 0:T - q0[kt]],
                                       ACT.Exp, scale=AD ** -0.5).then_inc(b_exp, 1)
                        if i == NB // 2 + 1 and after(b, hg, 1):
                            take_maxima(*after(b, hg, 1))

                act.wait_ge(loaded, 16)
                act.activation(identb[:], ident[:], ACT.Copy).then_inc(identb_ready, 1)
                act.sem_inc(b_exp, 2)
                act.sem_inc(mt_ready, 1)
                take_maxima(0, 0)
                units(act, turn)

            @block.vector
            def _(dve):
                def maxima(b, hg, i):
                    qt, heads = a_steps[i]
                    dve.wait_ge(a_mm, NA * (NG * b + hg) + i + 1)
                    n = nk[qt]
                    dve.tensor_reduce(MX[hg % 2][:, qt, heads[0]:heads[-1] + 1],
                                      at[(NA * hg + i) % 2][:, 0:len(heads) * n]
                                      .rearrange("p (h k) -> p h k", k=n),
                                      AX.X, ALU.max, negate=True).then_inc(a_max, 1)

                def copy_out(b, hg):
                    u = NG * b + hg
                    dve.wait_ge(pv_mm, TB * (u + 2))
                    dve.tensor_copy(AO[:, hg, ds(b * T, T)], pv[:]).then_inc(ao_ready, 1)

                def turn(b, hg):
                    ahead = after(b, hg, 2)
                    if ahead:
                        dve.wait_ge(max_split, NG * ahead[0] + ahead[1] + 1)
                    for i in range(NA):
                        if i == NA - TAIL // 2:
                            copy_out(b, hg)
                        if ahead:
                            maxima(*ahead, i)

                for hg in range(2):
                    for i in range(NA):
                        maxima(0, hg, i)
                dve.sem_inc(ao_ready, 1)
                units(dve, turn)


def stage_heads_out(nc, AO, Y, wo, out_bias):
    HT = T // 2
    with ExitStack() as stack:
        s = Space(nc, stack, "ho" + str(nc.next_id()))
        sel = s.sb("sel", [P, P])
        SU = s.sb("SU", [P, NG * B * T // Q4])
        RC = s.sb("RC", [P, NG * B * T // Q4])
        ot = [s.sb(f"ot{i}", [P, NG, HT]) for i in range(2)]
        rb = [s.ps(f"rb{i}", [P, NG, HT]) for i in range(2)]
        yb = [s.ps(f"yb{i}", [P, 2, D]) for i in range(2)]
        bo_loaded = s.sem("bo_loaded")
        sums_taken = s.sem("sums_taken")
        inverted = s.sem("inverted")
        sums_back = s.sem("sums_back")
        drawn = s.sem("drawn")
        spread = s.sem("spread")
        ot_ready = s.sem("ot_ready")
        y_mm = s.sem("y_mm")
        y_copied = s.sem("y_copied")
        with nc.Block() as block:
            @block.sync
            def _(sp):
                for h in range(AG):
                    row = slice(h * Q4 + AD, h * Q4 + AD + 1)
                    sp.dma_start(SU[h * Q4:(h + 1) * Q4, :], AO[row, :, :]).then_inc(sums_taken, 16)
                if out_bias is not None:
                    sp.dma_start(wo[AD + 1:AD + 2, 0, :], out_bias.unsqueeze(0)).then_inc(bo_loaded, 16)
                sp.wait_ge(inverted, 1)
                for h in range(AG):
                    row = slice(h * Q4 + AD, h * Q4 + AD + 1)
                    sp.dma_start(AO[row, :, :], RC[h * Q4:(h + 1) * Q4, :]).then_inc(sums_back, 16)

            @block.gpsimd
            def _(pool):
                c = Tally(drawn)
                for h in range(AG):
                    cols = sel[:, h * Q4:(h + 1) * Q4]
                    c.inc(pool.memset(cols, 1.0))
                    c.wait(pool)
                    c.inc(pool.affine_select(out=cols, in_=cols, compare_op=ALU.is_equal, fill=0.0,
                                             base=-(h * Q4 + AD), pattern=[[0, Q4]], channel_multiplier=1))

            @block.tensor
            def _(pe):
                def invert(b, f):
                    pe.wait_ge(ot_ready, 2 * b + f + 1)
                    for g in range(NG):
                        mm = pe.matmul(rb[f][:, g, :], sel[:], AO[:, g, ds(b * T + f * HT, HT)],
                                       start=True, stop=True)
                    mm.then_inc(spread, 1)

                pe.wait_ge(drawn, 2 * AG)
                pe.wait_ge(sums_back, 16 * AG)
                if out_bias is not None:
                    pe.wait_ge(bo_loaded, 16)
                with pe.Fori(0, B) as b:
                    invert(b, 0)
                    invert(b, 1)
                    for f in range(2):
                        pe.wait_ge(ot_ready, 2 * b + f + 3)
                        pe.wait_ge(y_copied, 2 * b + f + 1)
                        for j in range(2):
                            for g in range(NG):
                                mm = pe.matmul(yb[f][:, j, :], ot[f][:, g, j * P:(j + 1) * P], wo[:, g, :],
                                               start=(g == 0), stop=(g == NG - 1))
                        mm.then_inc(y_mm, 1)

            @block.vector
            def _(dve):
                dve.wait_ge(sums_taken, 16 * AG)
                dve.reciprocal(RC[:], SU[:]).then_inc(inverted, 1)
                dve.sem_inc(ot_ready, 2)
                with dve.Fori(0, B) as b:
                    for f in range(2):
                        dve.wait_ge(spread, 2 * b + f + 1)
                        dve.wait_ge(y_copied, 2 * b + f + 1)
                        dve.tensor_tensor(ot[f][:], AO[:, :, ds(b * T + f * HT, HT)], rb[f][:], ALU.mult) \
                            .then_inc(ot_ready, 1)

            @block.scalar
            def _(act):
                act.sem_inc(y_copied, 2)
                with act.Fori(0, B) as b:
                    for f in range(2):
                        act.wait_ge(y_mm, 2 * b + f + 1)
                        act.activation(Y[:, ds(TB * b + 2 * f, 2), :], yb[f][:], ACT.Copy).then_inc(y_copied, 1)


def stage_attention(nc, X, Y, ident_d, split_d, w, bias_cols, v_bias, causal, rope=None, out_bias=None):
    with ExitStack() as stack:
        s = Space(nc, stack, "at" + str(nc.next_id()))
        AO = s.sb("AO", [P, NG, B * T])
        with ExitStack() as inner:
            V = Space(nc, inner, s.name + "v").sb("V", [P, NT, D])
            stage_heads(nc, X, V, split_d, w, bias_cols, v_bias, rope)
            stage_softmax(nc, V, AO, split_d, ident_d, causal)
        stage_heads_out(nc, AO, Y, w["o"], out_bias)



def stage_router(nc, XT, COMB, ident_d, gate_d, E, top, weight):
    with ExitStack() as stack:
        s = Space(nc, stack, "ro" + str(nc.next_id()))
        ident = s.sb("ident", [P, P])
        gate = s.sb("gate", [P, KC, E])
        lt = s.sb("lt", [E, T])
        LG = s.sb("LG", [P, NT, E])
        PR = s.sb("PR", [P, NT, E])
        EQ = s.sb("EQ", [P, NT, E])
        IO = s.sb("IO", [P, NT, E])
        KEY = s.sb("KEY", [P, NT, E])
        MX = s.sb("MX", [P, NT])
        SM = s.sb("SM", [P, NT])
        lo = s.ps("lo", [P, T])
        tp = s.ps("tp", [P, TB, P])
        loaded = s.sem("loaded")
        iota = s.sem("iota")
        pe_passed = s.sem("pe_passed")
        lt_mm = s.sem("lt_mm")
        lt_ready = s.sem("lt_ready")
        turned = s.sem("turned")
        lg_ready = s.sem("lg_ready")
        chain = s.sem("chain")
        less = s.sem("less")
        exps = s.sem("exps")
        bc = lambda ap: ap.unsqueeze(2).to_broadcast([P, NT, E])
        with nc.Block() as block:
            @block.sync
            def _(sp):
                sp.dma_start(ident[:], ident_d).then_inc(loaded, 16)
                sp.dma_start(gate[:], gate_d.rearrange("(c p) e -> p c e", p=P)).then_inc(loaded, 16)

            @block.tensor
            def _(pe):
                pe.wait_ge(loaded, 32)
                with pe.Fori(0, B) as b:
                    pe.wait_ge(lt_ready, b + 1)
                    for k in range(KC):
                        mm = pe.matmul(lo[0:E, :], gate[:, k, :], XT[:, k, ds(T * b, T)],
                                       start=(k == 0), stop=(k == KC - 1))
                    mm.then_inc(lt_mm, 1)
                    pe.wait_ge(lt_ready, b + 2)
                    pe.wait_ge(lg_ready, b + 1)
                    pe.sem_inc(pe_passed, 1)
                    for j in range(TB):
                        mm = pe.transpose(tp[:, j, 0:E], lt[:, j * P:(j + 1) * P], ident[0:E, 0:E])
                    mm.then_inc(turned, 1)

            @block.scalar
            def _(act):
                act.sem_inc(lt_ready, 1)
                act.sem_inc(lg_ready, 1)
                with act.Fori(0, B) as b:
                    act.wait_ge(lt_mm, b + 1)
                    act.activation(lt[:], lo[0:E, :], ACT.Copy).then_inc(lt_ready, 1)
                    act.wait_ge(turned, b + 1)
                    act.activation(LG[:, ds(TB * b, TB), :], tp[:, :, 0:E], ACT.Copy).then_inc(lg_ready, 1)
                act.wait_ge(less, 1)
                act.activation(PR[:], PR[:], ACT.Exp).then_inc(exps, 1)

            @block.gpsimd
            def _(pool):
                for e in range(E):
                    pool.memset(IO[:, :, e:e + 1], float(e)).then_inc(iota, 1)

            @block.vector
            def _(dve):
                c = Tally(chain)
                dve.wait_ge(iota, E)
                dve.wait_ge(lg_ready, B + 1)
                c.inc(dve.tensor_reduce(MX[:], LG[:], AX.X, ALU.max))
                c.wait(dve)
                dve.tensor_tensor(PR[:], LG[:], bc(MX[:]), ALU.subtract).then_inc(less, 1)
                for r in range(top):
                    if r:
                        c.inc(dve.tensor_reduce(MX[:], LG[:], AX.X, ALU.max))
                        c.wait(dve)
                    c.inc(dve.tensor_tensor(EQ[:], LG[:], bc(MX[:]), ALU.is_equal))
                    c.wait(dve)
                    c.inc(dve.scalar_tensor_tensor(KEY[:].rearrange("p t e -> p (t e)"),
                                                   EQ[:].rearrange("p t e -> p (t e)"), -64.0,
                                                   IO[:].rearrange("p t e -> p (t e)"), ALU.mult, ALU.add))
                    c.wait(dve)
                    c.inc(dve.tensor_reduce(SM[:], KEY[:], AX.X, ALU.min))
                    c.wait(dve)
                    hot = COMB if r == 0 else EQ
                    c.inc(dve.tensor_tensor(hot[:], KEY[:], bc(SM[:]), ALU.is_equal))
                    c.wait(dve)
                    if r + 1 < top:
                        c.inc(dve.scalar_tensor_tensor(LG[:].rearrange("p t e -> p (t e)"),
                                                       COMB[:].rearrange("p t e -> p (t e)"), -1e30,
                                                       LG[:].rearrange("p t e -> p (t e)"), ALU.mult, ALU.add))
                        c.wait(dve)
                    if r:
                        c.inc(dve.tensor_tensor(COMB[:], COMB[:], EQ[:], ALU.add))
                        c.wait(dve)
                dve.wait_ge(exps, 1)
                if weight == "softmax":
                    c.inc(dve.tensor_reduce(SM[:], PR[:], AX.X, ALU.add))
                    c.wait(dve)
                if weight != "one":
                    c.inc(dve.tensor_tensor(COMB[:], COMB[:], PR[:], ALU.mult))
                    c.wait(dve)
                    if weight == "renormed":
                        c.inc(dve.tensor_reduce(SM[:], COMB[:], AX.X, ALU.add))
                        c.wait(dve)
                    c.inc(dve.reciprocal(MX[:], SM[:]))
                    c.wait(dve)
                    c.inc(dve.tensor_tensor(COMB[:], COMB[:], bc(MX[:]), ALU.mult))
                    c.wait(dve)


def stage_experts(nc, XT, Y, COMB, E, F, func, w1_d, w3_d, w2_d, b1_d=None, b2_d=None, fresh=False,
                  resident=None):
    FC = F // P
    NS = min(E, 2)
    NC = FC
    gated = w3_d is not None
    with ExitStack() as stack:
        s = Space(nc, stack, "ex" + str(nc.next_id()))
        w1 = [s.sb(f"w1{i}", [P, KC, F]) for i in range(NS)] if resident is None else [resident[0]]
        w3 = [s.sb(f"w3{i}", [P, KC, F]) for i in range(NS)] if gated else None
        w2 = [s.sb(f"w2{i}", [P, FC, D]) for i in range(NS)] if resident is None else [resident[1]]
        b1 = [s.sb(f"b1{i}", [P, FC]) for i in range(NS)] if b1_d is not None else None
        b2 = [s.sb(f"b2{i}", [P, D]) for i in range(NS)] if b2_d is not None else None
        HT = s.sb("HT", [P, FC, T])
        GA = [s.sb(f"GA{i}", [P, T]) for i in range(2)] if gated else None
        YB = s.sb("YB", [P, TB, D])
        first = [s.ps(f"first{i}", [P, T]) for i in range(4)]
        yp = [s.ps(f"yp{i}", [P, 512]) for i in range(TB)]
        w_loaded = [s.sem(f"w_loaded{i}") for i in range(NS)]
        first_mm = s.sem("first_mm")
        ht_ready = s.sem("ht_ready")
        ga_ready = s.sem("ga_ready")
        y_mm = s.sem("y_mm")
        yb_ready = s.sem("yb_ready")
        y_ready = s.sem("y_ready")
        y_part = s.sem("y_part")
        zeroed = s.sem("zeroed")
        pe_passed = s.sem("pe_passed")
        act_passed = s.sem("act_passed")
        dve_passed = s.sem("dve_passed")
        n_dma = 2 * (resident is None) + gated + (b1 is not None) + (b2 is not None)
        ring = 2 if gated else 4
        with nc.Block() as block:
            @block.sync
            def _(sp):
                for e in range(E):
                    i = e % NS
                    if e >= NS:
                        sp.wait_ge(y_ready, B * (e - NS + 1) + 1)
                    if resident is None:
                        sp.dma_start(w1[i][:], w1_d[e].rearrange("(c p) f -> p c f", p=P)).then_inc(w_loaded[i], 16)
                    if gated:
                        sp.dma_start(w3[i][:], w3_d[e].rearrange("(c p) f -> p c f", p=P)).then_inc(w_loaded[i], 16)
                    if b1 is not None:
                        sp.dma_start(b1[i][:], b1_d[e]).then_inc(w_loaded[i], 16)
                    if resident is None:
                        sp.dma_start(w2[i][:], w2_d[e].rearrange("(c p) f -> p c f", p=P)).then_inc(w_loaded[i], 16)
                    if b2 is not None:
                        sp.dma_start(b2[i][:], b2_d[e].unsqueeze(0).to_broadcast([P, D])).then_inc(w_loaded[i], 16)

            @block.tensor
            def _(pe):
                with pe.Fori(0, E // NS) as i2:
                    for i in range(NS):
                        pe.wait_ge(w_loaded[i], 16 * n_dma * i2 + 16 * n_dma)
                        pe.sem_inc(pe_passed, 1)
                        with pe.Fori(0, B) as b:
                            g = B * (NS * i2 + i) + b

                            def layer1(f):
                                pe.wait_ge(ht_ready, NC * g + f + 1)
                                for v, w in enumerate((w1, w3) if gated else (w1,)):
                                    ps = first[2 * (f % 2) + v] if gated else first[f % 4]
                                    for k in range(KC):
                                        mm = pe.matmul(ps[:], w[i][:, k, f * P:(f + 1) * P], XT[:, k, ds(T * b, T)],
                                                       start=(k == 0), stop=(k == KC - 1))
                                mm.then_inc(first_mm, 1)

                            def layer2(f):
                                pe.wait_ge(ht_ready, NC * g + f + 1 + ring)
                                if f == 0:
                                    pe.wait_ge(y_ready, g + 1)
                                for j in range(TB):
                                    mm = pe.matmul(yp[j][:, 0:D], HT[:, f, j * P:(j + 1) * P], w2[i][:, f, :],
                                                   start=(f == 0), stop=(f == FC - 1))
                                return mm

                            layer1(0)
                            for f in range(1, FC):
                                layer1(f)
                                layer2(f - 1)
                            layer2(FC - 1).then_inc(y_mm, 1)

            @block.scalar
            def _(act):
                if not gated:
                    act.sem_inc(ht_ready, ring)
                with act.Fori(0, E // NS) as i2:
                    for i in range(NS):
                        act.wait_ge(w_loaded[i], 16 * n_dma * i2 + 16 * n_dma)
                        act.sem_inc(act_passed, 1)
                        with act.Fori(0, B) as b:
                            g = B * (NS * i2 + i) + b
                            for f in range(FC):
                                act.wait_ge(first_mm, FC * g + f + 1)
                                if gated:
                                    act.wait_ge(ht_ready, FC * g + f + 1)
                                    act.activation(GA[f % 2][:], first[2 * (f % 2)][:], func).then_inc(ga_ready, 1)
                                else:
                                    if f == 0:
                                        act.wait_ge(y_ready, g + 1)
                                    bias = b1[i][:, f:f + 1] if b1 is not None else 0.0
                                    act.activation(HT[:, f, :], first[f % 4][:], func, bias=bias).then_inc(ht_ready, 1)

            @block.vector
            def _(dve):
                dve.sem_inc(y_ready, 1)
                if gated:
                    dve.sem_inc(ht_ready, ring)
                if fresh:
                    dve.memset(Y[:], 0.0).then_inc(zeroed, 1)
                    dve.wait_ge(zeroed, 1)
                with dve.Fori(0, E // NS) as i2:
                    for i in range(NS):
                        dve.wait_ge(w_loaded[i], 16 * n_dma * i2 + 16 * n_dma)
                        dve.sem_inc(dve_passed, 1)
                        with dve.Fori(0, B) as b:
                            g = B * (NS * i2 + i) + b
                            if gated:
                                for f in range(FC):
                                    dve.wait_ge(ga_ready, FC * g + f + 1)
                                    dve.tensor_tensor(HT[:, f, :], GA[f % 2][:], first[2 * (f % 2) + 1][:], ALU.mult) \
                                        .then_inc(ht_ready, 1)
                            dve.wait_ge(y_mm, g + 1)
                            for j in range(TB):
                                src = yp[j][:, 0:D]
                                if b2 is not None:
                                    dve.tensor_tensor(YB[:, j, :], src, b2[i][:], ALU.add).then_inc(yb_ready, 1)
                            for j in range(TB):
                                src = yp[j][:, 0:D]
                                if b2 is not None:
                                    dve.wait_ge(yb_ready, TB * g + j + 1)
                                    src = YB[:, j, :]
                                dst = Y[:, ds(TB * b + j, 1), :]
                                if COMB is None:
                                    ins = dve.tensor_tensor(dst, src.unsqueeze(1), dst, ALU.add)
                                else:
                                    share = COMB[:, ds(TB * b + j, 1), ds(NS * i2 + i, 1)].rearrange("p a b -> p (a b)")
                                    ins = dve.scalar_tensor_tensor(dst, src.unsqueeze(1), share, dst, ALU.mult, ALU.add)
                                if j == TB - 1:
                                    ins.then_inc(y_ready, 1)
                                else:
                                    ins.then_inc(y_part, 1)
                            dve.wait_ge(y_ready, g + 2)
                            dve.wait_ge(y_part, (TB - 1) * g + TB - 1)



def stage_load(nc, name, pairs):
    with nc.semaphore(name) as loaded, nc.Block() as block:
        @block.sync
        def _(sp):
            for dst, src in pairs:
                sp.dma_start(dst, src).then_inc(loaded, 16)
            sp.wait_ge(loaded, 16 * len(pairs))


def stage_spectral(nc, W, qkv_d, u_qkv, sp_qkv, proj_d, u_proj, sp_proj):
    with ExitStack() as stack:
        s = Space(nc, stack, "sn")
        ones = s.sb("ones", [P, P])
        loaded = s.sem("loaded")
        ones_ready = s.sem("ones_ready")
        chain = s.sem("chain")
        mm_done = s.sem("mm_done")
        root = s.sem("root")
        parts = []
        for name, wd, u, sp_, n in (("qkv", qkv_d, u_qkv, sp_qkv, 3 * D), ("proj", proj_d, u_proj, sp_proj, D)):
            parts.append(dict(
                n=n, wd=wd, u=u, sp=sp_, w=s.sb("w" + name, [P, KC, n]), ub=s.sb("u" + name, [P, n]),
                pr=s.sb("pr" + name, [P, KC, n]), v=s.sb("v" + name, [P, KC]), sq=s.sb("sq" + name, [P, n // P]),
                r=s.sb("r" + name, [P, 1]), t=s.sb("t" + name, [P, 2]), u2=s.sb("u2" + name, [P, n // P]),
                c=s.sb("c" + name, [P, 1]), nrm=s.ps("nrm" + name, [P, 1]), col=s.ps("col" + name, [P, n // P])))
        with nc.Block() as block:
            @block.sync
            def _(sp):
                for p in parts:
                    sp.dma_start(p["w"][:], p["wd"].rearrange("(c p) n -> p c n", p=P)).then_inc(loaded, 16)
                    sp.dma_start(p["ub"][:], p["u"].unsqueeze(0).to_broadcast([P, p["n"]])).then_inc(loaded, 16)
                    sp.dma_start(p["c"][:], p["sp"].unsqueeze(0).to_broadcast([P, 1])).then_inc(loaded, 16)

            @block.vector
            def _(dve):
                c = Tally(chain)
                dve.memset(ones[:], 1.0).then_inc(ones_ready, 1)
                dve.wait_ge(loaded, 96)
                for k, p in enumerate(parts):
                    n = p["n"]
                    c.inc(dve.tensor_tensor(p["pr"][:], p["w"][:], p["ub"][:].unsqueeze(1).to_broadcast([P, KC, n]),
                                            ALU.mult))
                    c.wait(dve)
                    c.inc(dve.tensor_reduce(p["v"][:], p["pr"][:], AX.X, ALU.add))
                    c.wait(dve)
                    for src, width in ((p["v"], KC), (p["u2"], n // P)):
                        if width != KC or src is p["u2"]:
                            dve.wait_ge(mm_done, 3 * k + 2)
                            c.inc(dve.tensor_copy(src[:], p["col"][:]))
                            c.wait(dve)
                        c.inc(dve.tensor_tensor(p["sq"][:, 0:width], src[:], src[:], ALU.mult))
                        c.wait(dve)
                        c.inc(dve.tensor_reduce(p["r"][:], p["sq"][:, 0:width], AX.X, ALU.add))
                        p.setdefault("ready", []).append(c.n)
                        c.wait(dve)
                        if src is p["v"]:
                            dve.wait_ge(root, 2 * k + 1)
                            c.inc(dve.reciprocal(p["t"][:, 1:2], p["t"][:, 0:1]))
                            c.wait(dve)
                            c.inc(dve.tensor_scalar(p["v"][:], p["v"][:], p["t"][:, 1:2], None, ALU.mult))
                            p["v_ready"] = c.n
                            c.wait(dve)
                        else:
                            dve.wait_ge(root, 2 * k + 2)
                            c.inc(dve.reciprocal(p["t"][:, 1:2], p["t"][:, 0:1]))
                            c.wait(dve)
                            c.inc(dve.tensor_scalar(p["c"][:], p["c"][:], p["t"][:, 1:2], None, ALU.mult))
                            c.wait(dve)
                for m in ("q", "k", "v"):
                    c.inc(dve.tensor_scalar(W[m][:], W[m][:], parts[0]["c"][:], None, ALU.mult))
                c.inc(dve.tensor_scalar(W["o"][:], W["o"][:], parts[1]["c"][:], None, ALU.mult))

            @block.tensor
            def _(pe):
                pe.wait_ge(ones_ready, 1)
                for k, p in enumerate(parts):
                    pe.wait_ge(chain, p["ready"][0])
                    pe.matmul(p["nrm"][:], ones[:], p["r"][:], start=True, stop=True).then_inc(mm_done, 1)
                    pe.wait_ge(chain, p["v_ready"])
                    for m in range(p["n"] // P):
                        for q in range(KC):
                            mm = pe.matmul(p["col"][:, m:m + 1], p["w"][:, q, m * P:(m + 1) * P], p["v"][:, q:q + 1],
                                           start=(q == 0), stop=(q == KC - 1))
                    mm.then_inc(mm_done, 1)
                    pe.wait_ge(chain, p["ready"][1])
                    pe.matmul(p["nrm"][:], ones[:], p["r"][:], start=True, stop=True).then_inc(mm_done, 1)

            @block.scalar
            def _(act):
                for k, p in enumerate(parts):
                    for m in range(2):
                        act.wait_ge(mm_done, 3 * k + 1 + 2 * m)
                        act.activation(p["t"][:, 0:1], p["nrm"][:], ACT.Sqrt).then_inc(root, 1)


def stage_binary(nc, W):
    with ExitStack() as stack:
        s = Space(nc, stack, "bi")
        ones = s.sb("ones", [P, P])
        shapes = {"q": (P, KC, D), "k": (P, KC, D), "v": (P, KC, D), "o": (P, NG, D)}
        view = {n: W[n][:] for n in shapes}
        SG = {n: s.sb("sg" + n, list(sh)) for n, sh in shapes.items()}
        AB = {n: s.sb("ab" + n, list(sh)) for n, sh in shapes.items()}
        al = {n: s.ps("al" + n, [sh[0], sh[2]]) for n, sh in shapes.items()}
        ones_ready = s.sem("ones_ready")
        signs = s.sem("signs")
        sizes = s.sem("sizes")
        mm_done = s.sem("mm_done")
        chain = s.sem("chain")
        with nc.Block() as block:
            @block.scalar
            def _(act):
                for n in shapes:
                    act.activation(AB[n][:], view[n], ACT.Abs).then_inc(sizes, 1)
                    act.activation(SG[n][:], view[n], ACT.Sign).then_inc(signs, 1)

            @block.tensor
            def _(pe):
                pe.wait_ge(ones_ready, 1)
                for i, (n, (rows, chunks, width)) in enumerate(shapes.items()):
                    pe.wait_ge(sizes, i + 1)
                    for k in range(chunks):
                        mm = pe.matmul(al[n][:], ones[0:rows, 0:rows], AB[n][:, k, :],
                                       start=(k == 0), stop=(k == chunks - 1))
                    mm.then_inc(mm_done, 1)

            @block.vector
            def _(dve):
                dve.memset(ones[:], 1.0).then_inc(ones_ready, 1)
                c = Tally(chain)
                for i, (n, (rows, chunks, width)) in enumerate(shapes.items()):
                    dve.wait_ge(signs, i + 1)
                    c.inc(dve.tensor_tensor(SG[n][:], SG[n][:], view[n], ALU.subtract))
                    c.wait(dve)
                    c.inc(dve.tensor_tensor(view[n], view[n], SG[n][:], ALU.add))
                    c.wait(dve)
                    dve.wait_ge(mm_done, i + 1)
                    for k in range(chunks):
                        c.inc(dve.scalar_tensor_tensor(view[n][:, k, :], al[n][:], 1.0 / D, view[n][:, k, :],
                                                       ALU.mult, ALU.mult))


def stage_ternary(nc, tensors):
    with ExitStack() as stack:
        s = Space(nc, stack, "te")
        ones = s.sb("ones", [P, P])
        ones_ready = s.sem("ones_ready")
        chain = s.sem("chain")
        mm_done = s.sem("mm_done")
        sums = [s.sb(f"sum{i}", [P, 1]) for i in range(2)]
        thr = [s.sb(f"thr{i}", [P, 2]) for i in range(2)]
        low = [s.sb(f"low{i}", [P, 2048]) for i in range(2)]
        tot = [s.ps(f"tot{i}", [P, 1]) for i in range(2)]
        count = float(1024 * D)
        ready = []
        with nc.Block() as block:
            @block.vector
            def _(dve):
                dve.memset(ones[:], 1.0).then_inc(ones_ready, 1)
                c = Tally(chain)
                for i, w in enumerate(tensors):
                    c.inc(dve.tensor_reduce(sums[i][:], w, AX.XY, ALU.add, apply_absolute_value=True))
                    ready.append(c.n)
                for i, w in enumerate(tensors):
                    lo = low[i][:].rearrange("p (a b) -> p a b", a=w.shape[1])
                    dve.wait_ge(mm_done, i + 1)
                    for m, sign in enumerate((0.5, -0.5)):
                        c.inc(dve.tensor_scalar(thr[i][:, m:m + 1], tot[i][:], sign / count, sign * 1e-5,
                                                ALU.mult, ALU.add))
                    c.wait(dve)
                    c.inc(dve.tensor_scalar(lo, w, thr[i][:, 1:2], None, ALU.is_lt))
                    c.wait(dve)
                    c.inc(dve.scalar_tensor_tensor(w, w, thr[i][:, 0:1], lo, ALU.is_gt, ALU.subtract))

            @block.tensor
            def _(pe):
                pe.wait_ge(ones_ready, 1)
                for i in range(len(tensors)):
                    pe.wait_ge(chain, ready[i])
                    pe.matmul(tot[i][:], ones[:], sums[i][:], start=True, stop=True).then_inc(mm_done, 1)


def stage_conv(nc, XT, XC, taps_d):
    with ExitStack() as stack:
        s = Space(nc, stack, "cv")
        taps = s.sb("taps", [P, KC, 3])
        loaded = s.sem("loaded")
        summed = s.sem("summed")
        with nc.Block() as block:
            @block.sync
            def _(sp):
                sp.dma_start(taps[:], taps_d.rearrange("(c p) w -> p c w", p=P)).then_inc(loaded, 16)

            @block.vector
            def _(dve):
                c = Tally(summed)
                dve.wait_ge(loaded, 16)
                for k in range(KC):
                    x = XT[:, k, :].rearrange("p (b t) -> p b t", b=B)
                    y = XC[:, k, :].rearrange("p (b t) -> p b t", b=B)
                    c.inc(dve.tensor_scalar(y, x, taps[:, k, 2:3], None, ALU.mult))
                    for lag in (1, 2):
                        c.wait(dve)
                        c.inc(dve.scalar_tensor_tensor(y[:, :, lag:T], x[:, :, 0:T - lag],
                                                       taps[:, k, 2 - lag:3 - lag], y[:, :, lag:T],
                                                       ALU.mult, ALU.add))



def stage_linear(nc, XT, Y, ident_d, wqk_d, wv_d, wo_d, bqk_d, bv_d, bo_d):
    E1 = AD + 1
    with ExitStack() as stack:
        s = Space(nc, stack, "li")
        ident = s.sb("ident", [P, P])
        wqk = s.sb("wqk", [P, KC, 2 * D])
        wv = s.sb("wv", [P, KC, D])
        wo = s.sb("wo", [P, KC, D])
        bqk = s.sb("bqk", [P, 2 * D])
        bv = s.sb("bv", [P, D])
        bo = s.sb("bo", [P, D])
        XS = [s.sb(f"XS{i}", [P, KC, P]) for i in range(TB)]
        QK = [s.sb(f"QK{i}", [P, 2 * D]) for i in range(TB)]
        EX = [s.sb(f"EX{i}", [P, 2 * D]) for i in range(TB)]
        V1 = [s.sb(f"V1{i}", [P, AH, E1]) for i in range(TB)]
        KV = s.sb("KV", [P, AD, E1])
        PR = s.sb("PR", [P, AD, E1, AH])
        PQ = s.sb("PQ", [P, AH, E1, AD])
        QV = s.sb("QV", [P, AH, E1])
        RI = s.sb("RI", [P, AH])
        AT = [s.sb(f"AT{i}", [P, D]) for i in range(2)]
        ATT = [s.sb(f"ATT{i}", [P, KC, P]) for i in range(2)]
        pqk = [s.ps(f"pqk{i}", [P, 2 * D]) for i in range(2)]
        pv = [s.ps(f"pv{i}", [P, 512]) for i in range(2)]
        tp = [s.ps(f"tp{i}", [P, KC, 2 * P]) for i in range(2)]
        yo = [s.ps(f"yo{i}", [P, 512]) for i in range(2)]
        loaded = s.sem("loaded")
        ones_ready = s.sem("ones_ready")
        xs_ready = s.sem("xs_ready")
        qkv_mm = s.sem("qkv_mm")
        qk_added = s.sem("qk_added")
        v_ready = s.sem("v_ready")
        low_ready = s.sem("low_ready")
        exp_ready = s.sem("exp_ready")
        elu_ready = s.sem("elu_ready")
        kv_product = s.sem("kv_product")
        kv_ready = s.sem("kv_ready")
        chain = s.sem("chain")
        at_ready = s.sem("at_ready")
        turned = s.sem("turned")
        att_ready = s.sem("att_ready")
        o_mm = s.sem("o_mm")
        y_ready = s.sem("y_ready")
        dve_passed = s.sem("dve_passed")
        with nc.Block() as block:
            @block.sync
            def _(sp):
                sp.dma_start(ident[:], ident_d).then_inc(loaded, 16)
                for dst, src in ((wqk, wqk_d), (wv, wv_d), (wo, wo_d)):
                    sp.dma_start(dst[:], src.rearrange("(c p) n -> p c n", p=P)).then_inc(loaded, 16)
                for dst, src in ((bqk, bqk_d), (bv, bv_d), (bo, bo_d)):
                    sp.dma_start(dst[:], src.unsqueeze(0).to_broadcast([P, src.shape[0]])).then_inc(loaded, 16)

            @block.gpsimd
            def _(pool):
                for j in range(TB):
                    pool.memset(V1[j][:], 1.0).then_inc(ones_ready, 1)
                pool.sem_inc(kv_product, 1)
                with pool.Fori(0, B) as b:
                    for j in range(TB):
                        pool.wait_ge(qk_added, TB * b + j + 1)
                        pool.tensor_copy(XS[j][:], XT[:, :, ds(T * b + P * j, P)]).then_inc(xs_ready, 1)
                    for j in range(TB):
                        pool.wait_ge(elu_ready, TB * b + j + 1)
                        pool.wait_ge(v_ready, TB * b + j + 1 + TB)
                        pool.wait_ge(kv_ready, TB * b + j + 1)
                        k = QK[j][:, D:2 * D].rearrange("p (h d) -> p d h", h=AH)
                        v = V1[j][:].rearrange("p h e -> p e h")
                        pool.tensor_tensor(PR[:], k.unsqueeze(2).to_broadcast([P, AD, E1, AH]),
                                           v.unsqueeze(1).to_broadcast([P, AD, E1, AH]), ALU.mult) \
                            .then_inc(kv_product, 1)

            @block.tensor
            def _(pe):
                pe.wait_ge(loaded, 16 * 7)
                with pe.Fori(0, B) as b:
                    for j in range(TB):
                        f = j % 2
                        pe.wait_ge(xs_ready, TB * b + j + 1)
                        pe.wait_ge(qk_added, TB * b + j + 3)
                        pe.wait_ge(v_ready, TB * b + j + 3)
                        for k in range(KC):
                            pe.matmul(pqk[f][:], XS[j][:, k, :], wqk[:, k, :], start=(k == 0), stop=(k == KC - 1))
                        for k in range(KC):
                            mm = pe.matmul(pv[f][:, 0:D], XS[j][:, k, :], wv[:, k, :],
                                           start=(k == 0), stop=(k == KC - 1))
                        mm.then_inc(qkv_mm, 1)
                    for j in range(TB):
                        f = j % 2
                        pe.wait_ge(at_ready, TB * b + j + 1)
                        pe.wait_ge(att_ready, TB * b + j + 1)
                        for k in range(KC):
                            mm = pe.transpose(tp[f][:, k, 0:P], AT[f][:, k * P:(k + 1) * P], ident[:])
                        mm.then_inc(turned, 1)
                        pe.wait_ge(att_ready, TB * b + j + 3)
                        pe.wait_ge(y_ready, TB * b + j + 1)
                        for k in range(KC):
                            mm = pe.matmul(yo[f][:, 0:D], ATT[f][:, k, :], wo[:, k, :],
                                           start=(k == 0), stop=(k == KC - 1))
                        mm.then_inc(o_mm, 1)

            @block.scalar
            def _(act):
                act.sem_inc(att_ready, 2)
                with act.Fori(0, B) as b:
                    for j in range(TB):
                        act.wait_ge(low_ready, TB * b + j + 1)
                        act.activation(EX[j][:], EX[j][:], ACT.Exp).then_inc(exp_ready, 1)
                    for j in range(TB):
                        act.wait_ge(turned, TB * b + j + 1)
                        act.wait_ge(y_ready, TB * b + j + 1)
                        act.activation(ATT[j % 2][:], tp[j % 2][:, :, 0:P], ACT.Copy).then_inc(att_ready, 1)

            @block.vector
            def _(dve):
                dve.wait_ge(loaded, 16 * 7)
                dve.wait_ge(ones_ready, TB)
                dve.sem_inc(qk_added, TB)
                dve.sem_inc(v_ready, TB)
                dve.sem_inc(kv_ready, 1)
                dve.sem_inc(y_ready, 2)
                per = 4 * TB

                with dve.Fori(0, B) as b:
                    c = Tally(chain, per * b)
                    for j in range(TB):
                        n = TB * b + j
                        f = j % 2
                        dve.wait_ge(qkv_mm, n + 1)
                        dve.wait_ge(kv_product, TB * b + 1)
                        dve.tensor_tensor(QK[j][:], pqk[f][:], bqk[:], ALU.add).then_inc(qk_added, 1)
                        dve.tensor_tensor(V1[j][:, :, 0:AD], pv[f][:, 0:D].rearrange("p (h e) -> p h e", h=AH),
                                          bv[:].rearrange("p (h e) -> p h e", h=AH), ALU.add).then_inc(v_ready, 1)
                        dve.wait_ge(qk_added, n + 1 + TB)
                        dve.tensor_scalar(EX[j][:], QK[j][:], 0.0, None, ALU.min).then_inc(low_ready, 1)
                    for j in range(TB):
                        n = TB * b + j
                        dve.wait_ge(exp_ready, n + 1)
                        dve.scalar_tensor_tensor(QK[j][:], QK[j][:], 0.0, EX[j][:], ALU.max, ALU.add) \
                            .then_inc(elu_ready, 1)

                    def add_out(j):
                        dve.wait_ge(o_mm, TB * b + j + 1)
                        dve.tensor_tensor(Y[:, ds(TB * b + j, 1), :], yo[j % 2][:, 0:D].unsqueeze(1), bo[:].unsqueeze(1),
                                          ALU.add).then_inc(y_ready, 1)

                    for j in range(TB):
                        n = TB * b + j
                        dve.wait_ge(kv_product, n + 2)
                        dve.tensor_reduce(KV[:], PR[:], AX.X, ALU.add).then_inc(kv_ready, 1)
                        dve.wait_ge(kv_ready, n + 2)
                        q = QK[j][:, 0:D].rearrange("p (h d) -> p h d", h=AH)
                        c.inc(dve.tensor_tensor(PQ[:], q.unsqueeze(2).to_broadcast([P, AH, E1, AD]),
                                                KV[:].rearrange("p d e -> p e d").unsqueeze(1)
                                                .to_broadcast([P, AH, E1, AD]), ALU.mult))
                        c.wait(dve)
                        c.inc(dve.tensor_reduce(QV[:], PQ[:], AX.X, ALU.add))
                        c.wait(dve)
                        c.inc(dve.reciprocal(RI[:], QV[:, :, AD]))
                        c.wait(dve)
                        dve.wait_ge(att_ready, n + 1)
                        c.inc(dve.tensor_tensor(AT[j % 2][:].rearrange("p (h e) -> p h e", h=AH), QV[:, :, 0:AD],
                                                RI[:].unsqueeze(2).to_broadcast([P, AH, AD]), ALU.mult))
                        c.wait(dve)
                        dve.sem_inc(at_ready, 1)
                        if j:
                            add_out(j - 1)
                    add_out(TB - 1)



def tower(nc, a, out):
    ident = a["ident"]
    RETIRED.clear()
    split_d = [nc.dram_tensor(f"split_{n}", (B, 2, NP, AD, AH // 2, T), BF16, kind="Internal").ap() for n in ("q", "k")]
    with ExitStack() as whole:
        def buf(stack, name, shape, dt=F32):
            return stack.enter_context(nc.sbuf_tensor(name, shape, dt))

        def attention_weights(stack, prefix, names):
            w = {n: buf(stack, f"{prefix}_{n}", [P, KC, D]) for n in names}
            w["o"] = buf(stack, f"{prefix}_o", [P, NG, D])
            return w, [(w[n][:], a[f"{prefix}_{n}"]) for n in w]

        H = buf(whole, "H", [P, NT, D])
        Y = buf(whole, "Y", [P, NT, D])
        XT = buf(whole, "XT", [P, KC, B * T])

        stage_tokens(nc, H, a["xk"], a["wsT"], a["wtok"])
        stage_rows(nc, H, None, XT, ident)
        with ExitStack() as st:
            OUT = buf(st, "OUT", [P, T, HN])
            with ExitStack() as cell:
                KN = buf(cell, "KN", [P, TL, D])
                QR = buf(cell, "QR", [P, TL, D])
                V = buf(cell, "V", [P, HN, T])
                BT = buf(cell, "BT", [P, HN, T])
                stage_cell_inputs(nc, XT, KN, QR, V, BT, a["w_in"], a["w_kq"], a["w_vb"], a["b_beta"])
                stage_cell(nc, KN, QR, V, BT, OUT, ident)
            stage_cell_out(nc, OUT, Y, a["w_out"])
        stage_rows(nc, H, Y, XT, ident, post="ln", second="rms", w=a["g1"])
        with ExitStack() as st:
            w, pairs = attention_weights(st, "a0", ("q", "k", "v", "qr", "kr"))
            stage_load(nc, "a0_loaded", pairs)
            stage_attention(nc, XT, Y, ident, split_d, w, a["no_bias"], a["no_v_bias"], True, a["rope"])
        stage_rows(nc, H, Y, XT, ident, post="add", second="rms", w=a["g2"])
        with ExitStack() as st:
            COMB = buf(st, "COMB0", [P, NT, 4])
            stage_router(nc, XT, COMB, ident, a["gate0"], 4, 2, "renormed")
            stage_experts(nc, XT, Y, COMB, 4, 768, ACT.Silu, a["e0_w1"], a["e0_w3"], a["e0_w2"])
        stage_rows(nc, H, Y, XT, ident, post="ln")

        with ExitStack() as st:
            w, pairs = attention_weights(st, "a1", ("q", "k", "v"))
            stage_load(nc, "a1_loaded", pairs)
            stage_spectral(nc, w, a["w_qkv"], a["u_qkv"], a["sp_qkv"], a["w_proj"], a["u_proj"], a["sp_proj"])
            stage_attention(nc, XT, Y, ident, split_d, w, a["no_bias"], a["no_v_bias"], True)
        stage_rows(nc, H, Y, XT, ident, post="ln")
        with ExitStack() as st:
            COMB = buf(st, "COMB1", [P, NT, 8])
            stage_router(nc, XT, COMB, ident, a["gate1"], 8, 1, "softmax")
            stage_experts(nc, XT, Y, COMB, 8, 1024, ACT.Relu, a["e1_w1"], None, a["e1_w2"], a["e1_b1"], a["e1_b2"],
                          fresh=True)
        stage_rows(nc, H, Y, XT, ident, post="ln")

        with ExitStack() as st:
            w, pairs = attention_weights(st, "a2", ("q", "k", "v"))
            stage_load(nc, "a2_loaded", pairs)
            stage_binary(nc, w)
            stage_attention(nc, XT, Y, ident, split_d, w, a["a2_bias"], a["a2_bv"], False, out_bias=a["a2_bo"])
        stage_rows(nc, H, Y, XT, ident, post="ln", second="ln", w=a["c_ln1_w"], b=a["c_ln1_b"])
        with ExitStack() as st:
            XC = buf(st, "XC", [P, KC, B * T])
            stage_conv(nc, XT, XC, a["taps"])
            w, pairs = attention_weights(st, "a3", ("q", "k", "v", "qr", "kr"))
            stage_load(nc, "a3_loaded", pairs)
            stage_attention(nc, XC, Y, ident, split_d, w, a["no_bias"], a["no_v_bias"], True, a["rope"])
        stage_rows(nc, H, Y, XT, ident, post="add", second="ln", w=a["c_ln2_w"], b=a["c_ln2_b"])
        with ExitStack() as st:
            COMB = buf(st, "COMB2", [P, NT, 4])
            stage_router(nc, XT, COMB, ident, a["gate2"], 4, 1, "one")
            stage_experts(nc, XT, Y, COMB, 4, 1024, ACT.Silu, a["e2_w1"], a["e2_w3"], a["e2_w2"])
        stage_rows(nc, H, Y, XT, ident, post="ln", second="ln", w=a["d_ln1_w"], b=a["d_ln1_b"])

        stage_linear(nc, XT, Y, ident, a["l_wqk"], a["l_wv"], a["l_wo"], a["l_bqk"], a["l_bv"], a["l_bo"])
        stage_rows(nc, H, Y, XT, ident, post="add", second="ln", w=a["d_ln2_w"], b=a["d_ln2_b"])
        stage_experts(nc, XT, Y, None, 1, 1024, ACT.Gelu, a["fc_w"], None, a["fp_w"], a["fc_b"], a["fp_b"])
        stage_rows(nc, H, Y, XT, ident, post="ln")
        with ExitStack() as st:
            w1 = buf(st, "t_w1", [P, KC, 1024])
            w2 = buf(st, "t_w2", [P, 8, D])
            stage_load(nc, "t_loaded", [(w1[:], a["t_w1"]), (w2[:], a["t_w2"])])
            stage_ternary(nc, [w1[:], w2[:]])
            stage_experts(nc, XT, Y, None, 1, 1024, ACT.Relu, None, None, None, a["t_b1"], a["t_b2"], fresh=True,
                          resident=(w1, w2))
        stage_rows(nc, H, Y, None, ident, post="ln", out=out)



def layout(i):
    def rows(w):
        return w.reshape(KC, P, D).transpose(1, 0, 2)

    def turned(w):
        return w.reshape(D, AH, 2, AD // 2)[:, :, ::-1, :].reshape(D, D)

    def bias(*bs):
        return np.stack(bs).reshape(4, P).T

    def out_rows(w):
        o = np.zeros((NG, AG, Q4, D), np.float32)
        o[:, :, :AD] = w.reshape(NG, AG, AD, D)
        return o.reshape(NG, P, D).transpose(1, 0, 2)

    def expert_bias(b):
        return b.reshape(b.shape[0], -1, P).transpose(0, 2, 1)

    freq = 1.0 / 10000.0 ** (np.arange(0, AD, 2, dtype=np.float32) / AD)
    angle = freq.astype(np.float32)[:, None] * np.arange(T, dtype=np.float32)[None, :]
    rope = np.zeros((2, P // AD, AD, T), np.float32)
    for half, sign in ((0, -1), (1, 1)):
        rows_of = slice(half * AD // 2, (half + 1) * AD // 2)
        rope[0, :, rows_of] = np.cos(angle)
        rope[1, :, rows_of] = sign * np.sin(angle)
    vb = np.stack([i["L0_attn_W_v"].reshape(HN, HD, D), i["L0_attn_W_beta"].reshape(HN, HD, D)], 1)
    kv_heads = lambda w: np.repeat(w.reshape(D, NG, AD), AG, axis=1).reshape(D, D)
    a = {
        "ident": np.eye(P, dtype=np.float32),
        "xk": i["x"].reshape(B * T, D, 4).transpose(2, 1, 0).reshape(4 * KC, P, B * T),
        "wsT": i["L0_tok_weighted_sum"].T.reshape(KC, P, D),
        "wtok": i["L0_tok_weight"].T,
        "w_in": i["L0_attn_W_in"].T.reshape(KC, P, D),
        "w_kq": np.concatenate([i["L0_attn_W_k"].T, i["L0_attn_W_q"].T], 1).reshape(KC, P, 2 * D),
        "w_vb": vb.reshape(HN, 2 * HD, KC, P).transpose(0, 3, 2, 1),
        "b_beta": np.tile(i["L0_attn_b_beta"].T, (B, 1)),
        "w_out": np.tile(i["L0_attn_W_out"].T.reshape(HN, HD, D).transpose(1, 0, 2), (B, 1, 1)),
        "g1": i["L0_ffn_g1"], "g2": i["L0_ffn_g2"],
        "rope": rope.reshape(2, P, T).transpose(1, 0, 2),
        "no_bias": np.zeros((P, 4), np.float32), "no_v_bias": np.zeros(D, np.float32),
        "a0_q": rows(i["L0_ffn_wq"]), "a0_qr": rows(turned(i["L0_ffn_wq"])),
        "a0_k": rows(kv_heads(i["L0_ffn_wk"])), "a0_kr": rows(turned(kv_heads(i["L0_ffn_wk"]))),
        "a0_v": rows(kv_heads(i["L0_ffn_wv"])), "a0_o": out_rows(i["L0_ffn_wo"]),
        "gate0": i["L0_ffn_gate"],
        "e0_w1": i["L0_ffn_w1"], "e0_w3": i["L0_ffn_w3"], "e0_w2": i["L0_ffn_w2"],
        "w_qkv": i["L1_attn_W_qkv"], "u_qkv": i["L1_attn_u_qkv"], "sp_qkv": i["L1_attn_sigma_qkv"],
        "w_proj": i["L1_attn_W_proj"], "u_proj": i["L1_attn_u_proj"], "sp_proj": i["L1_attn_sigma_proj"],
        "a1_q": rows(i["L1_attn_W_qkv"][:, 0:D]), "a1_k": rows(i["L1_attn_W_qkv"][:, D:2 * D]),
        "a1_v": rows(i["L1_attn_W_qkv"][:, 2 * D:]), "a1_o": out_rows(i["L1_attn_W_proj"]),
        "gate1": i["L1_ffn_gate_w"].T,
        "e1_w1": i["L1_ffn_w1"], "e1_w2": i["L1_ffn_w2"], "e1_b1": expert_bias(i["L1_ffn_b1"]),
        "e1_b2": i["L1_ffn_b2"],
        "a2_q": rows(i["L2_attn_Wq"].T), "a2_k": rows(i["L2_attn_Wk"].T), "a2_v": rows(i["L2_attn_Wv"].T),
        "a2_o": out_rows(i["L2_attn_Wp"].T), "a2_bo": i["L2_attn_bp"],
        "a2_bias": bias(i["L2_attn_bq"], i["L2_attn_bk"]), "a2_bv": i["L2_attn_bv"],
        "c_ln1_w": i["L2_ffn_ln1_w"], "c_ln1_b": i["L2_ffn_ln1_b"],
        "c_ln2_w": i["L2_ffn_ln2_w"], "c_ln2_b": i["L2_ffn_ln2_b"],
        "taps": i["L2_ffn_conv_w"][:, 0, :],
        "a3_q": rows(i["L2_ffn_attn_w"][:, 0:D]), "a3_qr": rows(turned(i["L2_ffn_attn_w"][:, 0:D])),
        "a3_k": rows(i["L2_ffn_attn_w"][:, D:2 * D]), "a3_kr": rows(turned(i["L2_ffn_attn_w"][:, D:2 * D])),
        "a3_v": rows(i["L2_ffn_attn_w"][:, 2 * D:]), "a3_o": out_rows(i["L2_ffn_proj_w"]),
        "gate2": i["L2_ffn_router_w"],
        "e2_w1": i["L2_ffn_expert_wv"][:, :, 0:1024], "e2_w3": i["L2_ffn_expert_wv"][:, :, 1024:],
        "e2_w2": i["L2_ffn_expert_proj"],
        "d_ln1_w": i["L3_attn_ln1_w"], "d_ln1_b": i["L3_attn_ln1_b"],
        "d_ln2_w": i["L3_attn_ln2_w"], "d_ln2_b": i["L3_attn_ln2_b"],
        "l_wqk": np.concatenate([i["L3_attn_q_w"].T, i["L3_attn_k_w"].T], 1),
        "l_wv": i["L3_attn_v_w"].T, "l_wo": i["L3_attn_o_w"].T,
        "l_bqk": np.concatenate([i["L3_attn_q_b"], i["L3_attn_k_b"]]),
        "l_bv": i["L3_attn_v_b"], "l_bo": i["L3_attn_o_b"],
        "fc_w": i["L3_attn_fc_w"].T[None], "fp_w": i["L3_attn_proj_w"].T[None],
        "fc_b": expert_bias(i["L3_attn_fc_b"][None]), "fp_b": i["L3_attn_proj_b"][None],
        "t_w1": i["L3_ffn_W1"].T.reshape(KC, P, 1024).transpose(1, 0, 2),
        "t_w2": i["L3_ffn_W2"].T.reshape(8, P, D).transpose(1, 0, 2),
        "t_b1": expert_bias(i["L3_ffn_b1"][None]), "t_b2": i["L3_ffn_b2"][None],
    }
    return {n: np.ascontiguousarray(v) for n, v in a.items()}


def kernel(**inputs):
    import concourse.bacc as _bacc
    from concourse.bass_utils import run_bass_kernel_spmd as _run

    nc = _bacc.Bacc("TRN2", target_bir_lowering=False, num_devices=1)
    arrays = layout({n: np.asarray(v) for n, v in inputs.items()})
    aps = {n: nc.dram_tensor("in_" + n, v.shape, mybir.dt.from_np(v.dtype), kind="ExternalInput").ap()
           for n, v in arrays.items()}
    out = nc.dram_tensor("out", (B, T, D), F32, kind="ExternalOutput").ap()
    tower(nc, aps, out)
    r = _run(nc, [{"in_" + n: v for n, v in arrays.items()}], core_ids=[0])
    return r.results[0]["out"]
```

```python
from contextlib import ExitStack

import numpy as np
import concourse.bass as bass
from concourse import mybir
from concourse.bass import ds

F32 = mybir.dt.float32
BF16 = mybir.dt.bfloat16
ALU = mybir.AluOpType
ACT = mybir.ActivationFunctionType
AX = mybir.AxisListType

P = 128
B, T, D = 4, 512, 256
KC = D // P
NT = B * T // P
TB = T // P
Q4 = 32


RETIRED = []
CLEAR_AT = 100




class Space:

    def __init__(self, nc, stack, name):
        self.nc, self.stack, self.name = nc, stack, name
        if len(RETIRED) > CLEAR_AT:
            nc.clear_and_free_semaphores(list(RETIRED))
            RETIRED.clear()
            nc.all_engine_barrier()

    def sb(self, name, shape, dt=F32):
        return self.stack.enter_context(self.nc.sbuf_tensor(f"{self.name}_{name}", shape, dt))

    def ps(self, name, shape, dt=F32):
        return self.stack.enter_context(self.nc.psum_tensor(f"{self.name}_{name}", shape, dt))

    def sem(self, name):
        made = self.nc.alloc_semaphore(name=f"{self.name}_{name}")
        self.stack.callback(RETIRED.append, made)
        return made


class Tally:

    def __init__(self, sem, base=0):
        self.sem, self.base, self.n = sem, base, 0

    def inc(self, ins):
        ins.then_inc(self.sem, 1)
        self.n += 1
        return self.n

    def wait(self, eng, n=None):
        eng.wait_ge(self.sem, self.base + (self.n if n is None else n))



def stage_tokens(nc, H, xk, wsT, wtok):
    NX = 4 * KC
    with ExitStack() as stack:
        s = Space(nc, stack, "tok")
        xg = [s.sb(f"xg{i}", [P, NX, T]) for i in range(2)]
        ws = s.sb("ws", [P, KC, D])
        wd = s.sb("wd", [P, 4, D])
        w2 = s.sb("w2", [P, NX, D])
        out = [s.ps(f"out{i}", [P, 2, 2, D]) for i in range(2)]
        w_loaded = s.sem("w_loaded")
        x_loaded = [s.sem(f"x_loaded{i}") for i in range(2)]
        w_ready = s.sem("w_ready")
        mm_done = s.sem("mm_done")
        out_free = s.sem("out_free")
        with nc.Block() as block:
            @block.sync
            def _(sp):
                sp.dma_start(ws[:], wsT.rearrange("c p o -> p c o")).then_inc(w_loaded, 16)
                sp.dma_start(wd[:], wtok.unsqueeze(0).to_broadcast([P, 4, D])).then_inc(w_loaded, 16)
                for b in range(B):
                    if b >= 2:
                        sp.wait_ge(mm_done, 2 * (b - 1))
                    sp.dma_start(xg[b % 2][:], xk[:, :, b * T:(b + 1) * T].rearrange("c p t -> p c t")) \
                        .then_inc(x_loaded[b % 2], 16)

            @block.vector
            def _(dve):
                dve.wait_ge(w_loaded, 32)
                for d in range(4):
                    dve.tensor_tensor(w2[:, KC * d:KC * d + KC, :], ws[:],
                                      wd[:, d:d + 1, :].to_broadcast([P, KC, D]), ALU.mult) \
                        .then_inc(w_ready, 1)

            @block.tensor
            def _(pe):
                pe.wait_ge(w_ready, 4)
                with pe.Fori(0, 2) as i:
                    for half in range(2):
                        pe.wait_ge(x_loaded[half], 16 * i + 16)
                        pe.wait_ge(out_free, 4 * i + 2 * half + 2)
                        for j in range(TB):
                            for c in range(NX):
                                mm = pe.matmul(out[half][:, j // 2, j % 2, :], xg[half][:, c, j * P:(j + 1) * P],
                                               w2[:, c, :], start=(c == 0), stop=(c == NX - 1))
                            if j % 2:
                                mm.then_inc(mm_done, 1)

            @block.scalar
            def _(act):
                act.sem_inc(out_free, 4)
                with act.Fori(0, 2) as i:
                    for half in range(2):
                        for u in range(2):
                            act.wait_ge(mm_done, 4 * i + 2 * half + u + 1)
                            act.activation(H[:, ds(8 * i + 4 * half + 2 * u, 2), :], out[half][:, u, :, :],
                                           ACT.Copy).then_inc(out_free, 1)



def stage_rows(nc, H, Y, XT, ident_d, post=None, second=None, w=None, b=None, out=None, rows=None):
    with ExitStack() as stack:
        s = Space(nc, stack, "rows" + str(nc.next_id()))
        R = [s.sb(f"R{i}", [P, TB, D]) for i in range(2)]
        S = [s.sb(f"S{i}", [P, TB, D]) for i in range(2)]
        XN = [s.sb(f"XN{i}", [P, TB, D]) for i in range(2)] if second else R
        stats = s.sb("stats", [P, TB, 6])
        mv = s.sb("mv", [P, TB, 2])
        ms = s.sb("ms", [P, TB])
        sd = s.sb("sd", [P, TB])
        rstd = s.sb("rstd", [P, TB])
        epsc = s.sb("epsc", [P, 2])
        wb = s.sb("wb", [P, 2, KC]) if w is not None else None
        ident = s.sb("ident", [P, P])
        tp = [s.ps(f"tp{i}", [P, KC, T]) for i in range(2)] if XT is not None else None
        w_loaded = s.sem("w_loaded")
        chain = s.sem("chain")
        stats_seen = s.sem("stats_seen")
        var_ready = s.sem("var_ready")
        sd_ready = s.sem("sd_ready")
        r_ready = s.sem("r_ready")
        r_copied = s.sem("r_copied")
        xn_ready = s.sem("xn_ready")
        turned = s.sem("turned")
        xt_copied = s.sem("xt_copied")
        stored = s.sem("stored")
        out_free = s.sem("out_free")
        rows_copied = s.sem("rows_copied")
        passed = s.sem("passed")
        n_w = 1 + (w is not None) + (b is not None)
        norms = ([("ln", 1e-5)] if post == "ln" else []) + \
            ([(second, 1e-5 if second == "ln" else 1.1920928955078125e-07)] if second else [])
        NV = len(norms)
        keep = H if post == "ln" else Y if post == "add" else None
        with nc.Block() as block:
            @block.sync
            def _(sp):
                sp.dma_start(ident[:], ident_d).then_inc(w_loaded, 16)
                if w is not None:
                    sp.dma_start(wb[:, 0, :], w).then_inc(w_loaded, 16)
                if b is not None:
                    sp.dma_start(wb[:, 1, :], b).then_inc(w_loaded, 16)
                if out is not None:
                    sp.sem_inc(out_free, 2)
                    for i in range(B):
                        sp.wait_ge(r_ready, i + 1)
                        sp.dma_start(out[i].rearrange("(j p) d -> p j d", p=P), R[i % 2][:]).then_inc(stored, 16)
                        sp.wait_ge(stored, 16 * (i + 1))
                        sp.sem_inc(out_free, 1)

            @block.vector
            def _(dve):
                for k, (_, eps) in enumerate(norms):
                    dve.memset(epsc[:, k:k + 1], eps).then_inc(chain, 1)
                dve.wait_ge(w_loaded, 16 * n_w)
                per = 0
                per += 1 if post else 0
                for kind, _ in norms:
                    per += 2 * TB + 1 + TB + (2 if kind == "rms" else 0)
                def rows_of(i, f):
                    c = Tally(chain, per * i + NV)

                    def norm(k, kind, src, dst, free):
                        for j in range(TB):
                            c.inc(dve.bn_stats(stats[:, j, :], src[:, j, :]))
                        c.wait(dve)
                        dve.sem_inc(stats_seen, 1)
                        for j in range(TB):
                            last = dve.bn_aggr(mv[:, j, :], stats[:, j, :])
                            c.inc(last)
                        if kind == "rms":
                            c.wait(dve)
                            c.inc(dve.tensor_tensor(ms[:], mv[:, :, 0], mv[:, :, 0], ALU.mult))
                            c.wait(dve)
                            c.inc(dve.tensor_tensor(ms[:], ms[:], mv[:, :, 1], ALU.add))
                        c.wait(dve)
                        dve.sem_inc(var_ready, 1)
                        dve.wait_ge(sd_ready, NV * i + k + 1)
                        c.inc(dve.reciprocal(rstd[:], sd[:]))
                        c.wait(dve)
                        free()
                        for j in range(TB):
                            if kind == "rms":
                                c.inc(dve.tensor_scalar(dst[:, j, :], src[:, j, :], rstd[:, j:j + 1], None, ALU.mult))
                            else:
                                c.inc(dve.tensor_scalar(dst[:, j, :], src[:, j, :], mv[:, j, 0:1], rstd[:, j:j + 1],
                                                        ALU.subtract, ALU.mult))
                        c.wait(dve)

                    def r_free():
                        if XT is not None and not second:
                            dve.wait_ge(turned, i + 1)
                        if keep is not None:
                            dve.wait_ge(r_copied, i + 1)
                        if out is not None:
                            dve.wait_ge(out_free, i + 1)

                    def xn_free():
                        dve.wait_ge(turned, i + 1)
                        if rows is not None:
                            dve.wait_ge(rows_copied, i + 1)

                    if post:
                        plain = post == "add" or not norms
                        dst = R[f] if plain else S[f]
                        if plain:
                            r_free()
                        c.inc(dve.tensor_tensor(dst[:], H[:, ds(TB * i, TB), :], Y[:, ds(TB * i, TB), :], ALU.add))
                        c.wait(dve)
                        if post == "ln":
                            norm(0, "ln", S[f], R[f], r_free)
                        dve.sem_inc(r_ready, 1)
                    else:
                        r_free()
                        dve.tensor_copy(R[f][:], H[:, ds(TB * i, TB), :]).then_inc(r_ready, 1)
                        dve.wait_ge(r_ready, i + 1)
                    if second:
                        norm(NV - 1, second, R[f], XN[f], xn_free)
                    dve.sem_inc(xn_ready, 1)

                with dve.Fori(0, B // 2) as i2:
                    for f in range(2):
                        rows_of(2 * i2 + f, f)

            @block.scalar
            def _(act):
                act.wait_ge(w_loaded, 16 * n_w)
                if NV:
                    act.wait_ge(chain, NV)
                if keep is not None:
                    act.sem_inc(r_copied, 2)
                act.sem_inc(xt_copied, 2 * KC)

                def roots(i):
                    for k, (kind, _) in enumerate(norms):
                        act.wait_ge(var_ready, NV * i + k + 1)
                        src = ms[:] if kind == "rms" else mv[:, :, 1]
                        act.activation(sd[:], src, ACT.Sqrt, bias=epsc[:, k:k + 1]).then_inc(sd_ready, 1)

                def keep_rows(i, f):
                    if keep is not None:
                        act.wait_ge(r_ready, i + 1)
                        act.activation(keep[:, ds(TB * i, TB), :], R[f][:], ACT.Copy).then_inc(r_copied, 1)

                def take_turned(i, f):
                    if XT is not None:
                        act.wait_ge(turned, i + 3)
                        for k in range(KC):
                            affine = {} if w is None else {"scale": wb[:, 0, k:k + 1]}
                            if b is not None:
                                affine["bias"] = wb[:, 1, k:k + 1]
                            act.activation(XT[:, k, ds(T * i, T)], tp[f][:, k, :], ACT.Identity, **affine) \
                                .then_inc(xt_copied, 1)

                for i in range(B):
                    roots(i)
                    if i:
                        take_turned(i - 1, (i - 1) % 2)
                    keep_rows(i, i % 2)
                take_turned(B - 1, (B - 1) % 2)

            @block.gpsimd
            def _(pool):
                if rows is None:
                    return
                pool.sem_inc(rows_copied, 2)
                with pool.Fori(0, B // 2) as i2:
                    for f in range(2):
                        pool.wait_ge(xn_ready, 2 * i2 + f + 1)
                        pool.sem_inc(passed, 1)
                        pool.tensor_copy(rows[:, ds(TB * (2 * i2 + f), TB), :], XN[f][:]).then_inc(rows_copied, 1)

            @block.tensor
            def _(pe):
                if XT is None:
                    return
                pe.wait_ge(w_loaded, 16 * n_w)
                pe.sem_inc(turned, 2)
                with pe.Fori(0, B // 2) as i2:
                    for f in range(2):
                        i = 2 * i2 + f
                        pe.wait_ge(xn_ready, i + 1)
                        pe.wait_ge(xt_copied, KC * i + KC)
                        for j in range(TB):
                            for k in range(KC):
                                last = pe.transpose(tp[f][:, k, j * P:(j + 1) * P], XN[f][:, j, k * P:(k + 1) * P],
                                                    ident[:])
                        last.then_inc(turned, 1)



HN, HD = 8, 32
TL = 16
TH = T // TL


def stage_cell_inputs(nc, XT, KN, QR, V, BT, w_in, w_kq, w_vb, b_beta):
    with ExitStack() as stack:
        s = Space(nc, stack, "ci")
        XP = s.sb("XP", [P, KC, B * T])
        wi = s.sb("wi", [P, KC, D])
        wkq = s.sb("wkq", [P, KC, 2 * D])
        wvb = s.sb("wvb", [P, HN, KC, 2 * HD])
        wh = [s.sb(f"wh{i}", [P, KC, 2 * HD]) for i in range(2)]
        bb = s.sb("bb", [P, HN])
        xs = [s.sb(f"xs{i}", [P, KC, P]) for i in range(4)]
        sq = [s.sb(f"sq{i}", [P, D]) for i in range(4)]
        ss = s.sb("ss", [P, TL * HN])
        nrm = s.sb("nrm", [P, TL * HN])
        bank = [s.ps(f"bank{i}", [P, 512]) for i in range(8)]
        loaded = s.sem("loaded")
        xp_mm = s.sem("xp_mm")
        xp_ready = s.sem("xp_ready")
        xs_ready = s.sem("xs_ready")
        kq_mm = s.sem("kq_mm")
        k_copied = s.sem("k_copied")
        q_copied = s.sem("q_copied")
        sq_ready = s.sem("sq_ready")
        ss_ready = s.sem("ss_ready")
        nrm_ready = s.sem("nrm_ready")
        inv = s.sem("inv")
        wh_ready = s.sem("wh_ready")
        vb_mm = s.sem("vb_mm")
        vb_copied = s.sem("vb_copied")
        with nc.Block() as block:
            @block.sync
            def _(sp):
                sp.dma_start(wi[:], w_in.rearrange("c p o -> p c o")).then_inc(loaded, 16)
                sp.dma_start(wkq[:], w_kq.rearrange("c p o -> p c o")).then_inc(loaded, 16)
                sp.dma_start(wvb[:], w_vb.rearrange("h p c o -> p h c o")).then_inc(loaded, 16)
                sp.dma_start(bb[:], b_beta).then_inc(loaded, 16)

            @block.tensor
            def _(pe):
                pe.wait_ge(loaded, 64)
                with pe.Fori(0, B) as b:
                    for e in range(KC):
                        pe.wait_ge(xp_ready, KC * b + e + 1)
                        for k in range(KC):
                            mm = pe.matmul(bank[e][:], wi[:, k, e * P:(e + 1) * P], XT[:, k, ds(b * T, T)],
                                           start=(k == 0), stop=(k == KC - 1))
                        mm.then_inc(xp_mm, 1)
                with pe.Fori(0, TL // 4) as i:
                    for u in range(4):
                        pe.wait_ge(xs_ready, 4 * i + u + 1)
                        pe.wait_ge(k_copied, 4 * i + u + 1)
                        pe.wait_ge(q_copied, 4 * i + u + 1)
                        pe.wait_ge(sq_ready, 4 * i + u + 1)
                        for k in range(KC):
                            mm = pe.matmul(bank[2 + u][:], xs[u][:, k, :], wkq[:, k, :],
                                           start=(k == 0), stop=(k == KC - 1))
                        mm.then_inc(kq_mm, 1)
                with pe.Fori(0, HN // 2) as i:
                    for u in range(2):
                        pe.wait_ge(wh_ready, 2 * i + u + 1)
                        for ty in range(2):
                            pe.wait_ge(vb_copied, 4 * i + 2 * u + ty + 1)
                            for b in range(B):
                                for k in range(KC):
                                    mm = pe.matmul(bank[2 * ty + u][Q4 * b:Q4 * b + Q4, :],
                                                   wh[u][:, k, ty * HD:(ty + 1) * HD], XP[:, k, b * T:(b + 1) * T],
                                                   start=(k == 0), stop=(k == KC - 1))
                            mm.then_inc(vb_mm, 1)

            @block.scalar
            def _(act):
                act.sem_inc(xp_ready, 2)
                with act.Fori(0, B) as b:
                    for e in range(KC):
                        act.wait_ge(xp_mm, KC * b + e + 1)
                        act.activation(XP[:, e, ds(b * T, T)], bank[e][:], ACT.Silu).then_inc(xp_ready, 1)
                act.sem_inc(q_copied, 4)
                act.sem_inc(sq_ready, 4)
                with act.Fori(0, TL // 4) as i:
                    for u in range(4):
                        act.wait_ge(kq_mm, 4 * i + u + 1)
                        act.wait_ge(ss_ready, 4 * i + u + 1)
                        act.activation(sq[u][:], bank[2 + u][:, 0:D], ACT.Square).then_inc(sq_ready, 1)
                        act.activation(QR[:, ds(4 * i + u, 1), :], bank[2 + u][:, D:2 * D], ACT.Copy) \
                            .then_inc(q_copied, 1)
                act.wait_ge(ss_ready, 4 + TL)
                act.activation(nrm[:], ss[:], ACT.Sqrt).then_inc(nrm_ready, 1)
                act.sem_inc(vb_copied, 4)
                with act.Fori(0, HN // 2) as i:
                    for u in range(2):
                        act.wait_ge(vb_mm, 4 * i + 2 * u + 1)
                        act.activation(V[:, ds(2 * i + u, 1), :], bank[u][:], ACT.Copy).then_inc(vb_copied, 1)
                        act.wait_ge(vb_mm, 4 * i + 2 * u + 2)
                        act.activation(BT[:, ds(2 * i + u, 1), :], bank[2 + u][:], ACT.Sigmoid,
                                       bias=bb[:, ds(2 * i + u, 1)]).then_inc(vb_copied, 1)

            @block.vector
            def _(dve):
                dve.sem_inc(k_copied, 4)
                dve.sem_inc(ss_ready, 4)
                dve.wait_ge(xp_ready, 2 + KC * B)
                xpv = XP[:].rearrange("p k (n l) -> p k n l", l=TL)
                with dve.Fori(0, TL // 4) as i:
                    for u in range(4):
                        dve.wait_ge(sq_ready, 4 * i + u + 1)
                        dve.tensor_copy(xs[u][:], xpv[:, :, :, ds(4 * i + u, 1)]).then_inc(xs_ready, 1)
                    for u in range(4):
                        dve.wait_ge(q_copied, 4 * i + u + 5)
                        dve.tensor_copy(KN[:, ds(4 * i + u, 1), :], bank[2 + u][:, 0:D]).then_inc(k_copied, 1)
                        dve.wait_ge(sq_ready, 4 * i + u + 5)
                        dve.tensor_reduce(ss[:, ds(HN * (4 * i + u), HN)],
                                          sq[u][:].rearrange("p (h j) -> p h j", h=HN), AX.X, ALU.add) \
                            .then_inc(ss_ready, 1)
                dve.wait_ge(loaded, 64)
                dve.wait_ge(k_copied, 4 + TL)
                dve.wait_ge(nrm_ready, 1)
                dve.tensor_scalar(nrm[:], nrm[:], 1e-6, None, ALU.add).then_inc(inv, 1)
                dve.wait_ge(inv, 1)
                dve.reciprocal(ss[:], nrm[:]).then_inc(inv, 1)
                dve.wait_ge(inv, 2)
                knv = KN[:].rearrange("p l (h j) -> p (l h) j", h=HN)
                dve.tensor_tensor(knv, knv, ss[:].unsqueeze(2).to_broadcast([P, TL * HN, HD]), ALU.mult) \
                    .then_inc(inv, 1)

            @block.gpsimd
            def _(pool):
                pool.wait_ge(loaded, 64)
                with pool.Fori(0, HN // 2) as i:
                    for u in range(2):
                        if u == 0:
                            pool.wait_ge(vb_copied, 4 * i + 1)
                        pool.wait_ge(vb_copied, 4 * i + 2 * u + 1)
                        pool.wait_ge(vb_copied, 4 * i + 2 * u + 2)
                        pool.tensor_copy(wh[u][:], wvb[:, ds(2 * i + u, 1), :, :]).then_inc(wh_ready, 1)


def stage_cell(nc, KN, QR, V, BT, OUT, ident_d, clear_d=None):
    NCH = 2
    CH = HN // NCH
    CW = CH * HD
    with ExitStack() as stack:
        s = Space(nc, stack, "cell")
        ident = s.sb("ident", [P, P])
        sel = s.sb("sel", [P, P])
        zero = s.sb("zero", [P, D])
        S = [s.sb(f"S{i}", [P, NCH, CW]) for i in range(2)]
        T1 = s.sb("T1", [P, TL, NCH, CH, HD + 1])
        T2 = s.sb("T2", [P, NCH, CW])
        T3 = s.sb("T3", [P, NCH, CW])
        BS = s.sb("BS", [P, NCH, CW])
        DL = s.sb("DL", [P, NCH, CH])
        QB = [s.sb(f"QB{i}", [P, 2, NCH, CW]) for i in range(2)]
        SQ = s.sb("SQ", [P, TL, NCH, CW])
        kb = [s.ps(f"kb{i}", [P, 2, NCH, CW]) for i in range(4)]
        qb = [s.ps(f"qb{i}", [P, 2, NCH, CW]) for i in range(2)]
        loaded = s.sem("loaded")
        sel_ready = s.sem("sel_ready")
        kb_ready = s.sem("kb_ready")
        qb_ready = s.sem("qb_ready")
        qb_copied = s.sem("qb_copied")
        sk_done = s.sem("sk_done")
        v_placed = s.sem("v_placed")
        delta_done = s.sem("delta_done")
        outer_done = s.sem("outer_done")
        sum_done = s.sem("sum_done")
        state_ready = s.sem("state_ready")
        cleared = s.sem("cleared")
        zero_ready = s.sem("zero_ready")
        clear_done = s.sem("clear_done")
        bs_ready = s.sem("bs_ready")
        sq_done = s.sem("sq_done")
        out_done = s.sem("out_done")
        NP = TL // 2

        def count(i, t, c):
            return 2 * TL * i + 2 * t + c + 1

        def keys(t, c):
            return kb[(t // 2) % 4][:, t % 2, c, :]

        h4 = lambda ap: ap.rearrange("p (h j) -> p h j", h=CH)
        with nc.Block() as block:
            @block.sync
            def _(sp):
                sp.dma_start(ident[:], ident_d).then_inc(loaded, 16)
                if clear_d is not None:
                    tiles = clear_d.rearrange("(t p) d -> p t d", p=P)
                    sp.wait_ge(zero_ready, 1)
                    sp.dma_start(tiles, zero[:].unsqueeze(1).to_broadcast(list(tiles.shape))).then_inc(clear_done, 16)
                    sp.wait_ge(clear_done, 16)

            @block.tensor
            def _(pe):
                with pe.Fori(0, TH) as i:
                    pe.wait_ge(sel_ready, i + 1)
                    for pp in range(NP):
                        pe.wait_ge(outer_done, 4 * (NP * i + pp) + 4)
                        pe.matmul(kb[pp % 4][:], sel[:], KN[:, 2 * pp:2 * pp + 2, :],
                                  start=True, stop=True).then_inc(kb_ready, 1)
                        pe.wait_ge(qb_copied, 2 * (NP * i + pp) + 2)
                        pe.matmul(qb[pp % 2][:], sel[:], QR[:, 2 * pp:2 * pp + 2, :],
                                  start=True, stop=True).then_inc(qb_ready, 1)

            @block.vector
            def _(dve):
                dve.memset(SQ[:, TL - 2:TL, :, :], 0.0).then_inc(cleared, 1)
                dve.memset(S[1][:], 0.0).then_inc(state_ready, 2)
                dve.wait_ge(cleared, 1)
                dve.sem_inc(outer_done, 16)
                dve.sem_inc(out_done, TL)

                def reduce_out(row, slot):
                    dve.wait_ge(sq_done, 2 * row + 6)
                    dve.tensor_reduce(OUT[:, ds(row, 1), :],
                                      SQ[:, slot % TL, :, :].rearrange("p c (h j) -> p (c h) j", h=CH),
                                      AX.X, ALU.add).then_inc(out_done, 1)

                with dve.Fori(0, TH) as i:
                    def scaled(t, c):
                        if t % 2 == 0 and c == 0:
                            dve.wait_ge(kb_ready, NP * i + t // 2 + 1)
                        dve.wait_ge(state_ready, count(i, t, c))
                        dve.tensor_tensor(T1[:, t, c, :, 0:HD], h4(S[(t + 1) % 2][:, c, :]), h4(keys(t, c)),
                                          ALU.mult).then_inc(sk_done, 1)

                    def delta(t, c):
                        dve.wait_ge(sk_done, count(i, t, c))
                        if t == 0 and c == 0:
                            dve.wait_ge(v_placed, i + 1)
                        dve.tensor_reduce(DL[:, c, :], T1[:, t, c, :, :], AX.X, ALU.add).then_inc(delta_done, 1)

                    def outer(t, c):
                        dve.wait_ge(delta_done, count(i, t, c))
                        dve.tensor_tensor(h4(T2[:, c, :]), DL[:, c, :].unsqueeze(2).to_broadcast([P, CH, HD]),
                                          h4(keys(t, c)), ALU.mult).then_inc(outer_done, 1)

                    def summed(t, c):
                        dve.wait_ge(outer_done, count(i, t, c) + 16)
                        dve.wait_ge(bs_ready, count(i, t, c))
                        dve.tensor_tensor(T3[:, c, :], BS[:, c, :], T2[:, c, :], ALU.subtract) \
                            .then_inc(sum_done, 1)

                    for t in range(TL):
                        for operation in (scaled, delta, outer, summed):
                            for c in range(NCH):
                                operation(t, c)
                        reduce_out(TL * i + t, t - 2)
                reduce_out(T, TL - 2)
                reduce_out(T + 1, TL - 1)

            @block.scalar
            def _(act):
                act.wait_ge(loaded, 16)
                act.sem_inc(qb_copied, 4)
                rows = ident[:].rearrange("p (b t) -> p b t", b=B)
                with act.Fori(0, TH) as i:
                    def copy_queries(pp, c):
                        act.wait_ge(qb_ready, NP * i + pp + 1)
                        act.wait_ge(sq_done, 2 * TL * i + 4 * pp + 4)
                        act.activation(QB[pp % 2][:, :, c, :], qb[pp % 2][:, :, c, :], ACT.Copy) \
                            .then_inc(qb_copied, 1)

                    act.wait_ge(qb_copied, 2 * NP * i + 4)
                    act.activation(sel[:].rearrange("p (b t) -> p b t", b=B),
                                   rows[:, :, ds(i, 1)].to_broadcast([P, B, Q4]), ACT.Copy).then_inc(sel_ready, 1)
                    act.activation(T1[:, :, :, :, HD].rearrange("p t c h -> p (c h) t"), V[:, :, ds(TL * i, TL)],
                                   ACT.Copy, scale=-1.0).then_inc(v_placed, 1)
                    copy_queries(0, 0)
                    copy_queries(0, 1)
                    for t in range(TL):
                        for c in range(NCH):
                            n = 2 * TL * i + 2 * t + c + 1
                            act.wait_ge(sum_done, n)
                            act.wait_ge(sq_done, n + 4)
                            act.activation(S[t % 2][:, c, :], T3[:, c, :], ACT.Tanh).then_inc(state_ready, 1)
                        for c in range(NCH):
                            if t % 2 == 1 and t < TL - 1:
                                copy_queries(t // 2 + 1, c)

            @block.gpsimd
            def _(pool):
                pool.memset(zero[:], 0.0).then_inc(zero_ready, 1)
                pool.sem_inc(sq_done, 8)
                with pool.Fori(0, TH) as i:
                    def query(t, c):
                        if t % 2 == 0 and c == 0:
                            pool.wait_ge(qb_copied, 2 * (NP * i + t // 2) + 4 + 2)
                        if c == 0:
                            pool.wait_ge(out_done, TL * i + t + 3)
                        pool.tensor_tensor(SQ[:, t, c, :], S[t % 2][:, c, :], QB[(t // 2) % 2][:, t % 2, c, :],
                                           ALU.mult).then_inc(sq_done, 1)

                    for t in range(TL):
                        for c in range(NCH):
                            pool.wait_ge(state_ready, count(i, t, c))
                            pool.wait_ge(outer_done, count(i, t, c) + 14)
                            pool.tensor_tensor(h4(BS[:, c, :]), h4(S[(t + 1) % 2][:, c, :]),
                                               BT[:, c * CH:(c + 1) * CH, ds(TL * i + t, 1)].to_broadcast([P, CH, HD]),
                                               ALU.mult).then_inc(bs_ready, 1)
                        for c in range(NCH):
                            if t:
                                query(t - 1, c)
                    for c in range(NCH):
                        pool.wait_ge(state_ready, count(i, TL, c))
                        query(TL - 1, c)


def stage_cell_out(nc, OUT, Y, w_out):
    with ExitStack() as stack:
        s = Space(nc, stack, "co")
        wo = s.sb("wo", [P, B, HN, D])
        si = [s.sb(f"si{i}", [P, HN, P]) for i in range(2)]
        cc = [s.sb(f"cc{i}", [P, HN, P]) for i in range(2)]
        y = [[s.ps(f"y{i}{b}", [P, 512]) for b in range(B)] for i in range(2)]
        zeroed = s.sem("zeroed")
        loaded = s.sem("loaded")
        si_ready = s.sem("si_ready")
        cc_ready = s.sem("cc_ready")
        mm_done = s.sem("mm_done")
        copied = s.sem("copied")
        with nc.Block() as block:
            @block.sync
            def _(sp):
                sp.wait_ge(zeroed, B)
                for b in range(B):
                    q = slice(Q4 * b, Q4 * b + Q4)
                    sp.dma_start(wo[q, b, :, :], w_out[q]).then_inc(loaded, 16)

            @block.gpsimd
            def _(pool):
                for b in range(B):
                    pool.memset(wo[:, b, :, :], 0.0).then_inc(zeroed, 1)

            @block.scalar
            def _(act):
                def silu(j, f):
                    act.wait_ge(cc_ready, j + 1)
                    act.activation(si[f][:], OUT[:, P * j:P * (j + 1), :].rearrange("p t h -> p h t"), ACT.Silu) \
                        .then_inc(si_ready, 1)

                silu(0, 0)
                silu(1, 1)
                for j in range(TB):
                    f = j % 2
                    if j + 2 < TB:
                        silu(j + 2, f)
                    for b in range(B):
                        act.wait_ge(mm_done, B * j + b + 1)
                        act.activation(Y[:, j + TB * b, :], y[f][b][:, 0:D], ACT.Copy).then_inc(copied, 1)

            @block.vector
            def _(dve):
                dve.sem_inc(cc_ready, 2)
                for j in range(TB):
                    f = j % 2
                    src = OUT[:, j * P:(j + 1) * P, :].rearrange("p t h -> p h t")
                    dve.wait_ge(si_ready, j + 1)
                    if j >= 2:
                        dve.wait_ge(mm_done, B * (j - 1))
                    dve.tensor_tensor(cc[f][:], si[f][:], src, ALU.mult).then_inc(cc_ready, 1)

            @block.tensor
            def _(pe):
                pe.wait_ge(loaded, 16 * B)
                for j in range(TB):
                    f = j % 2
                    pe.wait_ge(cc_ready, j + 3)
                    if j >= 2:
                        pe.wait_ge(copied, B * (j - 1))
                    for b in range(B):
                        for h in range(HN):
                            mm = pe.matmul(y[f][b][:, 0:D], cc[f][:, h, :], wo[:, b, h, :],
                                           start=(h == 0), stop=(h == HN - 1))
                        mm.then_inc(mm_done, 1)



AH = 16
AD = D // AH
AG = 4
NG = AH // AG
NP = 3
Q_PARTS = (range(0, 3), range(0, 2), range(0, 1))
K_PARTS = (0, 1, 2)
QK_ROWS = AD * sum(len(run) for run in Q_PARTS)
QK_LOADS = 2 * len(Q_PARTS)
MAX_ROWS = slice(QK_ROWS, QK_ROWS + NP)


def stage_heads(nc, X, V, split_d, w, bias_cols, v_bias, rope):
    turned = rope is not None
    with ExitStack() as stack:
        s = Space(nc, stack, "hd" + str(nc.next_id()))
        bc = s.sb("bc", [P, 4])
        bv = s.sb("bv", [P, D])
        cs = s.sb("cs", [P, 2, T]) if turned else None
        XS = s.sb("XS", [P, KC, T])
        RA = [s.sb(f"RA{i}", [P, T]) for i in range(2)]
        RB = [s.sb(f"RB{i}", [P, T]) for i in range(2)]
        F = [s.sb(f"F{i}", [P, T]) for i in range(4)]
        R = [s.sb(f"R{i}", [P, T]) for i in range(4)]
        parts = [s.sb(f"parts{i}", [P, NP, T], BF16) for i in range(4)]
        pj = [[s.ps(f"pj{i}{m}", [P, T]) for m in range(2)] for i in range(2)]
        vb = [s.ps(f"vb{i}", [P, 2, D]) for i in range(2)]
        loaded = s.sem("loaded")
        xs_ready = s.sem("xs_ready")
        p_mm = s.sem("p_mm")
        p_free = s.sem("p_free")
        turn = s.sem("turn")
        f_ready = s.sem("f_ready")
        high_ready = s.sem("high_ready")
        rest_ready = s.sem("rest_ready")
        mid_ready = s.sem("mid_ready")
        low_ready = s.sem("low_ready")
        stored = [s.sem(f"stored{i}") for i in range(4)]
        parts_free = s.sem("parts_free")
        v_mm = s.sem("v_mm")
        v_copied = s.sem("v_copied")
        n_load = 2 + turned
        tiles = [(n, half) for n in range(2) for half in range(2)]
        with nc.Block() as block:
            @block.sync
            def _(sp):
                sp.dma_start(bc[:], bias_cols).then_inc(loaded, 16)
                sp.dma_start(bv[:], v_bias.unsqueeze(0).to_broadcast([P, D])).then_inc(loaded, 16)
                if turned:
                    sp.dma_start(cs[:], rope).then_inc(loaded, 16)
                def free(i, n):
                    sp.wait_ge(stored[i], 16 * NP * n)
                    sp.sem_inc(parts_free, 1)

                sp.sem_inc(parts_free, 4)
                with sp.Fori(0, B) as b:
                    for i, (n, half) in enumerate(tiles):
                        sp.wait_ge(low_ready, 4 * b + i + 1)
                        for c in range(NP):
                            sp.dma_start(split_d[n][ds(b, 1), half, c, :, :, :].rearrange("o d h t -> (o h) d t"),
                                         parts[i][:, c, :]).then_inc(stored[i], 16)
                        if i > 1:
                            free(i - 2, b + 1)
                    free(2, b + 1)
                    free(3, b + 1)

            @block.tensor
            def _(pe):
                pe.sem_inc(v_mm, 2)
                with pe.Fori(0, B) as b:
                    for i, (n, half) in enumerate(tiles):
                        pe.wait_ge(p_free, 4 * b + i + 1)
                        for m in range(1 + turned):
                            wm = w["qk"[n] + ("r" if m else "")]
                            for k in range(KC):
                                mm = pe.matmul(pj[i % 2][m][:], wm[:, k, half * P:(half + 1) * P],
                                               X[:, k, ds(b * T, T)], start=(k == 0), stop=(k == KC - 1))
                            mm.then_inc(p_mm, 1)
                    pe.wait_ge(xs_ready, b + 1)
                    for j in range(TB):
                        if j % 2 == 0:
                            pe.wait_ge(v_copied, 2 * b + j // 2 + 1)
                        for k in range(KC):
                            mm = pe.matmul(vb[j // 2][:, j % 2, :], XS[:, k, j * P:(j + 1) * P], w["v"][:, k, :],
                                           start=(k == 0), stop=(k == KC - 1))
                        if j % 2:
                            mm.then_inc(v_mm, 1)

            @block.gpsimd
            def _(pool):
                with pool.Fori(0, B) as b:
                    for i in range(4):
                        pool.wait_ge(mid_ready, 4 * b + i + 1)
                        pool.tensor_tensor(parts[i][:, 2, :], R[i][:], parts[i][:, 1, :], ALU.subtract) \
                            .then_inc(low_ready, 1)

            @block.scalar
            def _(act):
                act.wait_ge(loaded, 16 * n_load)
                if not turned:
                    act.sem_inc(p_free, 2)
                with act.Fori(0, B) as b:
                    act.wait_ge(v_mm, 2 * b + 2)
                    act.activation(XS[:], X[:, :, ds(b * T, T)], ACT.Copy).then_inc(xs_ready, 1)
                    for i in range(4):
                        if not turned:
                            act.wait_ge(p_mm, 4 * b + i + 1)
                            act.wait_ge(rest_ready, 4 * b + i + 1)
                            act.activation(F[i][:], pj[i % 2][0][:], ACT.Identity, bias=bc[:, i:i + 1]) \
                                .then_inc(f_ready, 1)
                        act.wait_ge(f_ready, 4 * b + i + 1)
                        if not turned:
                            act.sem_inc(p_free, 1)
                        act.wait_ge(parts_free, 4 * b + i + 1)
                        act.activation(parts[i][:, 0, :], F[i][:], ACT.Copy).then_inc(high_ready, 1)
                        act.wait_ge(rest_ready, 4 * b + i + 5)
                        act.activation(parts[i][:, 1, :], R[i][:], ACT.Copy).then_inc(mid_ready, 1)

            @block.vector
            def _(dve):
                dve.wait_ge(loaded, 16 * n_load)
                dve.sem_inc(rest_ready, 4)
                dve.sem_inc(v_copied, 2)
                if turned:
                    dve.sem_inc(p_free, 2)
                with dve.Fori(0, B) as b:
                    def combine(i):
                        f = i % 2
                        dve.wait_ge(p_mm, 2 * (4 * b + i) + 2)
                        dve.tensor_tensor(RA[f][:], pj[f][0][:], cs[:, 0, :], ALU.mult).then_inc(turn, 1)
                        dve.tensor_tensor(RB[f][:], pj[f][1][:], cs[:, 1, :], ALU.mult).then_inc(turn, 1)
                        dve.wait_ge(turn, 2 * (4 * b + i) + 2)
                        dve.sem_inc(p_free, 1)
                        dve.tensor_tensor(F[i][:], RA[f][:], RB[f][:], ALU.add).then_inc(f_ready, 1)

                    def leave(i):
                        dve.wait_ge(high_ready, 4 * b + i + 1)
                        dve.tensor_tensor(R[i][:], F[i][:], parts[i][:, 0, :], ALU.subtract) \
                            .then_inc(rest_ready, 1)

                    for i in range(4):
                        if turned:
                            combine(i)
                            if i:
                                leave(i - 1)
                        else:
                            leave(i)
                    if turned:
                        leave(3)
                    for f in range(2):
                        dve.wait_ge(v_mm, 2 * b + f + 3)
                        dve.tensor_tensor(V[:, ds(TB * b + 2 * f, 2), :], vb[f][:],
                                          bv[:].unsqueeze(1).to_broadcast([P, 2, D]), ALU.add) \
                            .then_inc(v_copied, 1)


def stage_softmax(nc, V, AO, split_d, ident_d, causal):
    if causal:
        a_steps = [(0, range(0, 4)), (1, range(0, 2)), (1, range(2, 4))]
        a_steps += [(qt, range(h, h + 1)) for qt in (2, 3) for h in range(AG)]
        b_steps = [(0, range(0, 2)), (0, range(2, 4)), (1, range(0, 2)), (1, range(2, 4)),
                   (2, range(0, 4)), (3, range(0, 4))]
    else:
        a_steps = [(qt, range(h, h + 1)) for qt in range(TB) for h in range(AG)]
        b_steps = [(kt, range(h, h + 2)) for kt in range(TB) for h in (0, 2)]
    NA, NB = len(a_steps), len(b_steps)
    TAIL = 4
    b_upto = [max(i for i, st in enumerate(b_steps) if st[0] == kt) + 1 for kt in range(TB)]
    nk = [(qt + 1) * P if causal else T for qt in range(TB)]
    q0 = [kt * P if causal else 0 for kt in range(TB)]
    pitch = [T, T, T // 2, T // 4] if causal else [T] * TB
    with ExitStack() as stack:
        s = Space(nc, stack, "sm" + str(nc.next_id()))
        ident = s.sb("ident", [P, P])
        identb = s.sb("identb", [P, P], BF16)
        maska = s.sb("maska", [P, AG, P], BF16)
        maskb = s.sb("maskb", [P, AG, P], BF16)
        QS = [s.sb(f"QS{i}", [P, AG, T], BF16) for i in range(4)]
        KS = [s.sb(f"KS{i}", [P, AG, T], BF16) for i in range(4)]
        VG = [s.sb(f"VG{i}", [P, TB, AG, Q4]) for i in range(2)]
        MX = [s.sb(f"MX{i}", [P, TB, AG]) for i in range(2)]
        MR = s.sb("MR", [P, TB, AG])
        MP = s.sb("MP", [P, TB, NP, AG], BF16)
        MT = [s.sb(f"MT{i}", [AG * NP, T], BF16) for i in range(2)]
        EX = s.sb("EX", [P, TB, AG, T])
        at = [s.ps(f"at{i}", [P, T]) for i in range(2)]
        bt = [s.ps(f"bt{i}", [P, 2 * T]) for i in range(2)]
        pv = s.ps("pv", [P, T])
        mt = s.ps("mt", [P, TB, P], BF16)
        loaded = s.sem("loaded")
        identb_ready = s.sem("identb_ready")
        ones_ready = s.sem("ones_ready")
        drawn = s.sem("drawn")
        passed = s.sem("passed")
        qk_loaded = [s.sem(f"qk_loaded{i}") for i in range(4)]
        max_loaded = [s.sem(f"max_loaded{i}") for i in range(4)]
        a_mm = s.sem("a_mm")
        a_max = s.sem("a_max")
        b_mm = s.sem("b_mm")
        b_exp = s.sem("b_exp")
        split_step = s.sem("split_step")
        max_split = s.sem("max_split")
        max_turned = s.sem("max_turned")
        mt_ready = s.sem("mt_ready")
        v_ready = s.sem("v_ready")
        pv_mm = s.sem("pv_mm")
        ao_ready = s.sem("ao_ready")

        def after(b, hg, n):
            b2, g2 = b + (hg + n) // NG, (hg + n) % NG
            return None if isinstance(b2, int) and b2 >= B else (b2, g2)

        def units(eng, turn):
            with eng.Fori(0, B - 1) as b:
                for hg in range(NG):
                    turn(b, hg)
            for hg in range(NG):
                turn(B - 1, hg)

        drawn_all, masks_drawn = [], []
        with nc.Block() as block:
            @block.sync
            def _(sp):
                def load(b, hg):
                    sp.wait_ge(b_mm, NB * (NG * b + hg + 1))
                    row = 0
                    for q_run, k_part in zip(Q_PARTS, K_PARTS):
                        rows = slice(row, row + AD * len(q_run))
                        heads = slice(hg % 2 * AG, (hg % 2 + 1) * AG)
                        q, k = (split_d[n][ds(b, 1), hg // 2, :, :, heads, :] for n in range(2))
                        sp.dma_start(QS[hg][rows, :, :],
                                     q[:, q_run.start:q_run.stop].rearrange("o c d h t -> (o c d) (h t)")) \
                            .then_inc(qk_loaded[hg], 16)
                        sp.dma_start(KS[hg][rows, :, :],
                                     k[:, k_part].rearrange("o d h t -> o d (h t)")
                                     .to_broadcast([len(q_run), AD, AG * T])).then_inc(qk_loaded[hg], 16)
                        row = rows.stop

                def maxima(b, hg):
                    sp.wait_ge(mt_ready, NG * b + hg + 2)
                    sp.dma_start(QS[hg][MAX_ROWS, :, :], MT[hg % 2][:]).then_inc(max_loaded[hg], 16)

                def turn(b, hg):
                    if after(b, hg, 2):
                        load(*after(b, hg, 2))
                    maxima(b, hg)

                sp.dma_start(ident[:], ident_d).then_inc(loaded, 16)
                load(0, 0)
                load(0, 1)
                units(sp, turn)

            @block.gpsimd
            def _(pool):
                c = Tally(drawn)
                if causal:
                    for mask, sign in ((maska, 1), (maskb, -1)):
                        c.inc(pool.memset(mask[:], 0.0))
                        c.wait(pool)
                        c.inc(pool.affine_select(out=mask[:], in_=mask[:], compare_op=ALU.is_ge, fill=-1e30,
                                                 base=0, pattern=[[0, AG], [-sign, P]],
                                                 channel_multiplier=sign))
                masks_drawn.append(c.n)
                for i in range(2):
                    c.inc(pool.memset(VG[i][:], 0.0))
                    c.wait(pool)
                    c.inc(pool.memset(VG[i][:, :, :, AD:AD + 2], 1.0))
                drawn_all.append(c.n)

                def split(b, hg):
                    u, m = NG * b + hg, MX[hg % 2]
                    pool.wait_ge(a_max, NA * (u + 1))
                    if not (isinstance(u, int) and u == 0):
                        pool.wait_ge(max_turned, u)
                    pool.sem_inc(passed, 1)
                    pool.tensor_copy(MP[:, :, 0, :], m[:]).then_inc(split_step, 1)
                    pool.wait_ge(split_step, 4 * u + 1)
                    pool.tensor_tensor(MR[:], m[:], MP[:, :, 0, :], ALU.subtract).then_inc(split_step, 1)
                    pool.wait_ge(split_step, 4 * u + 2)
                    pool.sem_inc(passed, 1)
                    pool.tensor_copy(MP[:, :, 1, :], MR[:]).then_inc(split_step, 1)
                    pool.wait_ge(split_step, 4 * u + 3)
                    pool.tensor_tensor(MP[:, :, 2, :], MR[:], MP[:, :, 1, :], ALU.subtract) \
                        .then_inc(split_step, 1)
                    pool.wait_ge(split_step, 4 * u + 4)
                    pool.sem_inc(max_split, 1)

                def values(b, hg):
                    if not (isinstance(b, int) and NG * b + hg == 0):
                        pool.wait_ge(pv_mm, TB * (NG * b + hg))
                        pool.sem_inc(passed, 1)
                    pool.tensor_copy(VG[hg % 2][:, :, :, 0:AD],
                                     V[:, ds(TB * b, TB), hg * AG * AD:(hg + 1) * AG * AD]
                                     .rearrange("p j (h d) -> p j h d", h=AG)).then_inc(v_ready, 1)

                def turn(b, hg):
                    if after(b, hg, 1):
                        values(*after(b, hg, 1))
                        split(*after(b, hg, 1))

                pool.sem_inc(max_split, 2)
                values(0, 0)
                split(0, 0)
                units(pool, turn)

            @block.tensor
            def _(pe):
                def first_pass(b, hg, i):
                    index = NA * (NG * b + hg) + i
                    qt, heads = a_steps[i]
                    bank = at[(NA * hg + i) % 2]
                    if not (isinstance(index, int) and index < 2):
                        pe.wait_ge(a_max, index - 1)
                    n = nk[qt]
                    for k, h in enumerate(heads):
                        mm = pe.matmul(bank[:, k * n:(k + 1) * n], QS[hg][0:QK_ROWS, h, qt * P:(qt + 1) * P],
                                       KS[hg][0:QK_ROWS, h, 0:n], start=(k == 0), stop=not causal)
                    if causal:
                        at_end = bank[:, 0:len(heads) * n].rearrange("p (h k) -> p h k", k=n)[:, :, n - P:n]
                        mm = pe.matmul(at_end, identb[:], maska[:, 0:len(heads), :], start=False, stop=True)
                    mm.then_inc(a_mm, 1)

                def second_pass(b, hg, i):
                    kt, heads = b_steps[i]
                    bank = bt[i % 2]
                    pe.wait_ge(b_exp, NB * (NG * b + hg) + i + 1)
                    n, w = T - q0[kt], pitch[kt]
                    for k, h in enumerate(heads):
                        mm = pe.matmul(bank[:, k * w:k * w + n], KS[hg][0:MAX_ROWS.stop, h, kt * P:(kt + 1) * P],
                                       QS[hg][0:MAX_ROWS.stop, h, q0[kt]:T],
                                       start=(k % (T // w) == 0), stop=not causal)
                    if causal:
                        per = T // w
                        for k in range(0, len(heads), per):
                            first = bank[:, k * w:(k + per) * w].rearrange("p (h q) -> p h q", q=w)[:, :, 0:P]
                            mm = pe.matmul(first, identb[:], maskb[:, 0:per, :], start=False, stop=True)
                    mm.then_inc(b_mm, 1)

                def turn_maxima(b, hg):
                    u = NG * b + hg
                    pe.wait_ge(max_split, u + 3)
                    pe.wait_ge(mt_ready, u + 1)
                    for qt in range(TB):
                        mm = pe.transpose(mt[0:AG * NP, qt, :], MP[:, qt, :, :].rearrange("p c h -> p (c h)"),
                                          identb[:])
                    mm.then_inc(max_turned, 1)

                def weigh(b, hg, kt):
                    u = NG * b + hg
                    if kt == 0:
                        pe.wait_ge(v_ready, u + 1)
                        pe.wait_ge(ao_ready, u + 1)
                    pe.wait_ge(b_exp, NB * u + b_upto[kt] + 2)
                    for h in range(AG):
                        mm = pe.matmul(pv[h * Q4:(h + 1) * Q4, q0[kt]:T], VG[hg % 2][:, kt, h, :],
                                       EX[:, kt, h, q0[kt]:T], start=(kt == 0), stop=(kt == TB - 1))
                    mm.then_inc(pv_mm, 1)

                def turn(b, hg):
                    ahead = after(b, hg, 2)
                    if ahead:
                        pe.wait_ge(qk_loaded[ahead[1]], 16 * QK_LOADS * (ahead[0] + 1))
                    pe.wait_ge(max_loaded[hg], 16 * (b + 1))
                    done = weighed = 0
                    for i in range(NB):
                        second_pass(b, hg, i)
                        if i == NB // 2 and after(b, hg, 1):
                            turn_maxima(*after(b, hg, 1))
                        upto = (i + 1) * (NA - TAIL) // NB
                        if ahead:
                            for k in range(done, upto):
                                first_pass(*ahead, k)
                        done = upto
                        if i == b_upto[weighed] + 1:
                            weigh(b, hg, weighed)
                            weighed += 1
                    for k in range(done, NA):
                        if k == NA - TAIL // 2:
                            for kt in range(weighed, TB):
                                weigh(b, hg, kt)
                        if ahead:
                            first_pass(*ahead, k)

                pe.wait_ge(loaded, 16)
                pe.wait_ge(identb_ready, 1)
                if causal:
                    pe.wait_ge(drawn, masks_drawn[0])
                pe.sem_inc(b_mm, 4 * NB)
                pe.sem_inc(pv_mm, TB)
                for hg in range(2):
                    pe.wait_ge(qk_loaded[hg], 16 * QK_LOADS)
                    for i in range(NA):
                        if hg and i == NA // 2:
                            turn_maxima(0, 0)
                        first_pass(0, hg, i)
                pe.wait_ge(drawn, drawn_all[0])
                pe.wait_ge(ones_ready, 4)
                units(pe, turn)

            @block.scalar
            def _(act):
                def take_maxima(b, hg):
                    act.wait_ge(max_turned, NG * b + hg + 1)
                    act.activation(MT[hg % 2][:], mt[0:AG * NP, :, :].rearrange("p j t -> p (j t)"), ACT.Copy) \
                        .then_inc(mt_ready, 1)

                def turn(b, hg):
                    u = NG * b + hg
                    for i, (kt, heads) in enumerate(b_steps):
                        act.wait_ge(b_mm, NB * (u + 4) + i + 1)
                        if i == 0 or b_steps[i - 1][0] != kt:
                            act.wait_ge(pv_mm, TB * u + kt + 1)
                        w = pitch[kt]
                        src = bt[i % 2][:, 0:len(heads) * w].rearrange("p (h q) -> p h q", q=w)
                        act.activation(EX[:, kt, heads[0]:heads[-1] + 1, q0[kt]:T], src[:, :, 0:T - q0[kt]],
                                       ACT.Exp, scale=AD ** -0.5).then_inc(b_exp, 1)
                        if i == NB // 2 + 1 and after(b, hg, 1):
                            take_maxima(*after(b, hg, 1))

                act.wait_ge(loaded, 16)
                act.activation(identb[:], ident[:], ACT.Copy).then_inc(identb_ready, 1)
                act.sem_inc(b_exp, 2)
                act.sem_inc(mt_ready, 1)
                take_maxima(0, 0)
                units(act, turn)

            @block.vector
            def _(dve):
                def maxima(b, hg, i):
                    qt, heads = a_steps[i]
                    dve.wait_ge(a_mm, NA * (NG * b + hg) + i + 1)
                    n = nk[qt]
                    dve.tensor_reduce(MX[hg % 2][:, qt, heads[0]:heads[-1] + 1],
                                      at[(NA * hg + i) % 2][:, 0:len(heads) * n]
                                      .rearrange("p (h k) -> p h k", k=n),
                                      AX.X, ALU.max, negate=True).then_inc(a_max, 1)

                for i in range(4):
                    dve.memset(KS[i][MAX_ROWS, :, :], 1.0).then_inc(ones_ready, 1)

                def copy_out(b, hg):
                    u = NG * b + hg
                    dve.wait_ge(pv_mm, TB * (u + 2))
                    dve.tensor_copy(AO[:, hg, ds(b * T, T)], pv[:]).then_inc(ao_ready, 1)

                def turn(b, hg):
                    ahead = after(b, hg, 2)
                    if ahead:
                        dve.wait_ge(max_split, NG * ahead[0] + ahead[1] + 1)
                    for i in range(NA):
                        if i == NA - TAIL // 2:
                            copy_out(b, hg)
                        if ahead:
                            maxima(*ahead, i)

                for hg in range(2):
                    for i in range(NA):
                        maxima(0, hg, i)
                dve.sem_inc(ao_ready, 1)
                units(dve, turn)


def stage_heads_out(nc, AO, Y, wo, out_bias):
    HT = T // 2
    with ExitStack() as stack:
        s = Space(nc, stack, "ho" + str(nc.next_id()))
        sel = s.sb("sel", [P, P])
        SU = s.sb("SU", [P, NG * B * T // Q4])
        RC = s.sb("RC", [P, NG * B * T // Q4])
        ot = [s.sb(f"ot{i}", [P, NG, HT]) for i in range(2)]
        rb = [s.ps(f"rb{i}", [P, NG, HT]) for i in range(2)]
        yb = [s.ps(f"yb{i}", [P, 2, D]) for i in range(2)]
        bo_loaded = s.sem("bo_loaded")
        sums_taken = s.sem("sums_taken")
        inverted = s.sem("inverted")
        sums_back = s.sem("sums_back")
        drawn = s.sem("drawn")
        spread = s.sem("spread")
        ot_ready = s.sem("ot_ready")
        y_mm = s.sem("y_mm")
        y_copied = s.sem("y_copied")
        with nc.Block() as block:
            @block.sync
            def _(sp):
                for h in range(AG):
                    row = slice(h * Q4 + AD, h * Q4 + AD + 1)
                    sp.dma_start(SU[h * Q4:(h + 1) * Q4, :], AO[row, :, :]).then_inc(sums_taken, 16)
                if out_bias is not None:
                    sp.dma_start(wo[AD + 1:AD + 2, 0, :], out_bias.unsqueeze(0)).then_inc(bo_loaded, 16)
                sp.wait_ge(inverted, 1)
                for h in range(AG):
                    row = slice(h * Q4 + AD, h * Q4 + AD + 1)
                    sp.dma_start(AO[row, :, :], RC[h * Q4:(h + 1) * Q4, :]).then_inc(sums_back, 16)

            @block.gpsimd
            def _(pool):
                c = Tally(drawn)
                for h in range(AG):
                    cols = sel[:, h * Q4:(h + 1) * Q4]
                    c.inc(pool.memset(cols, 1.0))
                    c.wait(pool)
                    c.inc(pool.affine_select(out=cols, in_=cols, compare_op=ALU.is_equal, fill=0.0,
                                             base=-(h * Q4 + AD), pattern=[[0, Q4]], channel_multiplier=1))

            @block.tensor
            def _(pe):
                def invert(b, f):
                    pe.wait_ge(ot_ready, 2 * b + f + 1)
                    for g in range(NG):
                        mm = pe.matmul(rb[f][:, g, :], sel[:], AO[:, g, ds(b * T + f * HT, HT)],
                                       start=True, stop=True)
                    mm.then_inc(spread, 1)

                pe.wait_ge(drawn, 2 * AG)
                pe.wait_ge(sums_back, 16 * AG)
                if out_bias is not None:
                    pe.wait_ge(bo_loaded, 16)
                with pe.Fori(0, B) as b:
                    invert(b, 0)
                    invert(b, 1)
                    for f in range(2):
                        pe.wait_ge(ot_ready, 2 * b + f + 3)
                        pe.wait_ge(y_copied, 2 * b + f + 1)
                        for j in range(2):
                            for g in range(NG):
                                mm = pe.matmul(yb[f][:, j, :], ot[f][:, g, j * P:(j + 1) * P], wo[:, g, :],
                                               start=(g == 0), stop=(g == NG - 1))
                        mm.then_inc(y_mm, 1)

            @block.vector
            def _(dve):
                dve.wait_ge(sums_taken, 16 * AG)
                dve.reciprocal(RC[:], SU[:]).then_inc(inverted, 1)
                dve.sem_inc(ot_ready, 2)
                with dve.Fori(0, B) as b:
                    for f in range(2):
                        dve.wait_ge(spread, 2 * b + f + 1)
                        dve.wait_ge(y_copied, 2 * b + f + 1)
                        dve.tensor_tensor(ot[f][:], AO[:, :, ds(b * T + f * HT, HT)], rb[f][:], ALU.mult) \
                            .then_inc(ot_ready, 1)

            @block.scalar
            def _(act):
                act.sem_inc(y_copied, 2)
                with act.Fori(0, B) as b:
                    for f in range(2):
                        act.wait_ge(y_mm, 2 * b + f + 1)
                        act.activation(Y[:, ds(TB * b + 2 * f, 2), :], yb[f][:], ACT.Copy).then_inc(y_copied, 1)


def stage_attention(nc, X, Y, ident_d, split_d, w, bias_cols, v_bias, causal, rope=None, out_bias=None):
    with ExitStack() as stack:
        s = Space(nc, stack, "at" + str(nc.next_id()))
        AO = s.sb("AO", [P, NG, B * T])
        with ExitStack() as inner:
            V = Space(nc, inner, s.name + "v").sb("V", [P, NT, D])
            stage_heads(nc, X, V, split_d, w, bias_cols, v_bias, rope)
            stage_softmax(nc, V, AO, split_d, ident_d, causal)
        stage_heads_out(nc, AO, Y, w["o"], out_bias)



def stage_router(nc, XT, COMB, ident_d, gate_d, E, top, weight, HOT=None):
    with ExitStack() as stack:
        s = Space(nc, stack, "ro" + str(nc.next_id()))
        ident = s.sb("ident", [P, P])
        gate = s.sb("gate", [P, KC, E])
        lt = s.sb("lt", [E, T])
        LG = s.sb("LG", [P, NT, E])
        PR = s.sb("PR", [P, NT, E])
        EQ = s.sb("EQ", [P, NT, E])
        IO = s.sb("IO", [P, NT, E])
        KEY = s.sb("KEY", [P, NT, E])
        MX = s.sb("MX", [P, NT])
        SM = s.sb("SM", [P, NT])
        lo = s.ps("lo", [P, T])
        tp = s.ps("tp", [P, TB, P])
        loaded = s.sem("loaded")
        iota = s.sem("iota")
        pe_passed = s.sem("pe_passed")
        lt_mm = s.sem("lt_mm")
        lt_ready = s.sem("lt_ready")
        turned = s.sem("turned")
        lg_ready = s.sem("lg_ready")
        chain = s.sem("chain")
        less = s.sem("less")
        exps = s.sem("exps")
        bc = lambda ap: ap.unsqueeze(2).to_broadcast([P, NT, E])
        with nc.Block() as block:
            @block.sync
            def _(sp):
                sp.dma_start(ident[:], ident_d).then_inc(loaded, 16)
                sp.dma_start(gate[:], gate_d.rearrange("(c p) e -> p c e", p=P)).then_inc(loaded, 16)

            @block.tensor
            def _(pe):
                pe.wait_ge(loaded, 32)
                with pe.Fori(0, B) as b:
                    pe.wait_ge(lt_ready, b + 1)
                    for k in range(KC):
                        mm = pe.matmul(lo[0:E, :], gate[:, k, :], XT[:, k, ds(T * b, T)],
                                       start=(k == 0), stop=(k == KC - 1))
                    mm.then_inc(lt_mm, 1)
                    pe.wait_ge(lt_ready, b + 2)
                    pe.wait_ge(lg_ready, b + 1)
                    pe.sem_inc(pe_passed, 1)
                    for j in range(TB):
                        mm = pe.transpose(tp[:, j, 0:E], lt[:, j * P:(j + 1) * P], ident[0:E, 0:E])
                    mm.then_inc(turned, 1)

            @block.scalar
            def _(act):
                act.sem_inc(lt_ready, 1)
                act.sem_inc(lg_ready, 1)
                with act.Fori(0, B) as b:
                    act.wait_ge(lt_mm, b + 1)
                    act.activation(lt[:], lo[0:E, :], ACT.Copy).then_inc(lt_ready, 1)
                    act.wait_ge(turned, b + 1)
                    act.activation(LG[:, ds(TB * b, TB), :], tp[:, :, 0:E], ACT.Copy).then_inc(lg_ready, 1)
                act.wait_ge(less, 1)
                act.activation(PR[:], PR[:], ACT.Exp).then_inc(exps, 1)

            @block.gpsimd
            def _(pool):
                for e in range(E):
                    pool.memset(IO[:, :, e:e + 1], float(e)).then_inc(iota, 1)

            @block.vector
            def _(dve):
                c = Tally(chain)
                dve.wait_ge(iota, E)
                dve.wait_ge(lg_ready, B + 1)
                c.inc(dve.tensor_reduce(MX[:], LG[:], AX.X, ALU.max))
                c.wait(dve)
                dve.tensor_tensor(PR[:], LG[:], bc(MX[:]), ALU.subtract).then_inc(less, 1)
                for r in range(top):
                    if r:
                        c.inc(dve.tensor_reduce(MX[:], LG[:], AX.X, ALU.max))
                        c.wait(dve)
                    c.inc(dve.tensor_tensor(EQ[:], LG[:], bc(MX[:]), ALU.is_equal))
                    c.wait(dve)
                    c.inc(dve.scalar_tensor_tensor(KEY[:].rearrange("p t e -> p (t e)"),
                                                   EQ[:].rearrange("p t e -> p (t e)"), -64.0,
                                                   IO[:].rearrange("p t e -> p (t e)"), ALU.mult, ALU.add))
                    c.wait(dve)
                    c.inc(dve.tensor_reduce(SM[:], KEY[:], AX.X, ALU.min))
                    c.wait(dve)
                    hot = EQ if r else COMB if HOT is None else HOT
                    c.inc(dve.tensor_tensor(hot[:], KEY[:], bc(SM[:]), ALU.is_equal))
                    c.wait(dve)
                    if r + 1 < top:
                        c.inc(dve.scalar_tensor_tensor(LG[:].rearrange("p t e -> p (t e)"),
                                                       COMB[:].rearrange("p t e -> p (t e)"), -1e30,
                                                       LG[:].rearrange("p t e -> p (t e)"), ALU.mult, ALU.add))
                        c.wait(dve)
                    if r:
                        c.inc(dve.tensor_tensor(COMB[:], COMB[:], EQ[:], ALU.add))
                        c.wait(dve)
                dve.wait_ge(exps, 1)
                if weight == "softmax":
                    c.inc(dve.tensor_reduce(SM[:], PR[:], AX.X, ALU.add))
                    c.wait(dve)
                if weight != "one":
                    c.inc(dve.tensor_tensor(COMB[:], (COMB if HOT is None else HOT)[:], PR[:], ALU.mult))
                    c.wait(dve)
                    if weight == "renormed":
                        c.inc(dve.tensor_reduce(SM[:], COMB[:], AX.X, ALU.add))
                        c.wait(dve)
                    c.inc(dve.reciprocal(MX[:], SM[:]))
                    c.wait(dve)
                    c.inc(dve.tensor_tensor(COMB[:], COMB[:], bc(MX[:]), ALU.mult))
                    c.wait(dve)


def stage_experts(nc, XT, Y, COMB, E, F, func, w1_d, w3_d, w2_d, b1_d=None, b2_d=None, fresh=False,
                  resident=None):
    FC = F // P
    NS = min(E, 2)
    NC = FC
    gated = w3_d is not None
    with ExitStack() as stack:
        s = Space(nc, stack, "ex" + str(nc.next_id()))
        w1 = [s.sb(f"w1{i}", [P, KC, F]) for i in range(NS)] if resident is None else [resident[0]]
        w3 = [s.sb(f"w3{i}", [P, KC, F]) for i in range(NS)] if gated else None
        w2 = [s.sb(f"w2{i}", [P, FC, D]) for i in range(NS)] if resident is None else [resident[1]]
        b1 = [s.sb(f"b1{i}", [P, FC]) for i in range(NS)] if b1_d is not None else None
        b2 = [s.sb(f"b2{i}", [P, D]) for i in range(NS)] if b2_d is not None else None
        HT = s.sb("HT", [P, FC, T])
        GA = [s.sb(f"GA{i}", [P, T]) for i in range(2)] if gated else None
        YB = s.sb("YB", [P, TB, D])
        first = [s.ps(f"first{i}", [P, T]) for i in range(4)]
        yp = [s.ps(f"yp{i}", [P, 512]) for i in range(TB)]
        w_loaded = [s.sem(f"w_loaded{i}") for i in range(NS)]
        first_mm = s.sem("first_mm")
        ht_ready = s.sem("ht_ready")
        ga_ready = s.sem("ga_ready")
        y_mm = s.sem("y_mm")
        yb_ready = s.sem("yb_ready")
        y_ready = s.sem("y_ready")
        y_part = s.sem("y_part")
        zeroed = s.sem("zeroed")
        pe_passed = s.sem("pe_passed")
        act_passed = s.sem("act_passed")
        dve_passed = s.sem("dve_passed")
        n_dma = 2 * (resident is None) + gated + (b1 is not None) + (b2 is not None)
        ring = 2 if gated else 4
        with nc.Block() as block:
            @block.sync
            def _(sp):
                for e in range(E):
                    i = e % NS
                    if e >= NS:
                        sp.wait_ge(y_ready, B * (e - NS + 1) + 1)
                    if resident is None:
                        sp.dma_start(w1[i][:], w1_d[e].rearrange("(c p) f -> p c f", p=P)).then_inc(w_loaded[i], 16)
                    if gated:
                        sp.dma_start(w3[i][:], w3_d[e].rearrange("(c p) f -> p c f", p=P)).then_inc(w_loaded[i], 16)
                    if b1 is not None:
                        sp.dma_start(b1[i][:], b1_d[e]).then_inc(w_loaded[i], 16)
                    if resident is None:
                        sp.dma_start(w2[i][:], w2_d[e].rearrange("(c p) f -> p c f", p=P)).then_inc(w_loaded[i], 16)
                    if b2 is not None:
                        sp.dma_start(b2[i][:], b2_d[e].unsqueeze(0).to_broadcast([P, D])).then_inc(w_loaded[i], 16)

            @block.tensor
            def _(pe):
                with pe.Fori(0, E // NS) as i2:
                    for i in range(NS):
                        pe.wait_ge(w_loaded[i], 16 * n_dma * i2 + 16 * n_dma)
                        pe.sem_inc(pe_passed, 1)
                        with pe.Fori(0, B) as b:
                            g = B * (NS * i2 + i) + b

                            def layer1(f):
                                pe.wait_ge(ht_ready, NC * g + f + 1)
                                for v, w in enumerate((w1, w3) if gated else (w1,)):
                                    ps = first[2 * (f % 2) + v] if gated else first[f % 4]
                                    for k in range(KC):
                                        mm = pe.matmul(ps[:], w[i][:, k, f * P:(f + 1) * P], XT[:, k, ds(T * b, T)],
                                                       start=(k == 0), stop=(k == KC - 1))
                                mm.then_inc(first_mm, 1)

                            def layer2(f):
                                pe.wait_ge(ht_ready, NC * g + f + 1 + ring)
                                if f == 0:
                                    pe.wait_ge(y_ready, g + 1)
                                for j in range(TB):
                                    mm = pe.matmul(yp[j][:, 0:D], HT[:, f, j * P:(j + 1) * P], w2[i][:, f, :],
                                                   start=(f == 0), stop=(f == FC - 1))
                                return mm

                            layer1(0)
                            for f in range(1, FC):
                                layer1(f)
                                layer2(f - 1)
                            layer2(FC - 1).then_inc(y_mm, 1)

            @block.scalar
            def _(act):
                if not gated:
                    act.sem_inc(ht_ready, ring)
                with act.Fori(0, E // NS) as i2:
                    for i in range(NS):
                        act.wait_ge(w_loaded[i], 16 * n_dma * i2 + 16 * n_dma)
                        act.sem_inc(act_passed, 1)
                        with act.Fori(0, B) as b:
                            g = B * (NS * i2 + i) + b
                            for f in range(FC):
                                act.wait_ge(first_mm, FC * g + f + 1)
                                if gated:
                                    act.wait_ge(ht_ready, FC * g + f + 1)
                                    act.activation(GA[f % 2][:], first[2 * (f % 2)][:], func).then_inc(ga_ready, 1)
                                else:
                                    if f == 0:
                                        act.wait_ge(y_ready, g + 1)
                                    bias = b1[i][:, f:f + 1] if b1 is not None else 0.0
                                    act.activation(HT[:, f, :], first[f % 4][:], func, bias=bias).then_inc(ht_ready, 1)

            @block.vector
            def _(dve):
                dve.sem_inc(y_ready, 1)
                if gated:
                    dve.sem_inc(ht_ready, ring)
                if fresh:
                    dve.memset(Y[:], 0.0).then_inc(zeroed, 1)
                    dve.wait_ge(zeroed, 1)
                with dve.Fori(0, E // NS) as i2:
                    for i in range(NS):
                        dve.wait_ge(w_loaded[i], 16 * n_dma * i2 + 16 * n_dma)
                        dve.sem_inc(dve_passed, 1)
                        with dve.Fori(0, B) as b:
                            g = B * (NS * i2 + i) + b
                            if gated:
                                for f in range(FC):
                                    dve.wait_ge(ga_ready, FC * g + f + 1)
                                    dve.tensor_tensor(HT[:, f, :], GA[f % 2][:], first[2 * (f % 2) + 1][:], ALU.mult) \
                                        .then_inc(ht_ready, 1)
                            dve.wait_ge(y_mm, g + 1)
                            for j in range(TB):
                                src = yp[j][:, 0:D]
                                if b2 is not None:
                                    dve.tensor_tensor(YB[:, j, :], src, b2[i][:], ALU.add).then_inc(yb_ready, 1)
                            for j in range(TB):
                                src = yp[j][:, 0:D]
                                if b2 is not None:
                                    dve.wait_ge(yb_ready, TB * g + j + 1)
                                    src = YB[:, j, :]
                                dst = Y[:, ds(TB * b + j, 1), :]
                                if COMB is None:
                                    ins = dve.tensor_tensor(dst, src.unsqueeze(1), dst, ALU.add)
                                else:
                                    share = COMB[:, ds(TB * b + j, 1), ds(NS * i2 + i, 1)].rearrange("p a b -> p (a b)")
                                    ins = dve.scalar_tensor_tensor(dst, src.unsqueeze(1), share, dst, ALU.mult, ALU.add)
                                if j == TB - 1:
                                    ins.then_inc(y_ready, 1)
                                else:
                                    ins.then_inc(y_part, 1)
                            dve.wait_ge(y_ready, g + 2)
                            dve.wait_ge(y_part, (TB - 1) * g + TB - 1)



def stage_chosen_experts(nc, X, GOT, Y, SPARE, HOT, COMB, ident_d, x_d, y_d, E, func, w1_d, w3_d, w2_d, b1_d=None,
                         b2_d=None, affine=None):
    F = w2_d.shape[1]
    FC, HF = F // P, F // 2
    gated = w3_d is not None
    NS = NT + E - 1
    x_d, y_d = x_d[0:NS * P, :], y_d[0:NS * P, :]
    with ExitStack() as stack:
        s = Space(nc, stack, "sp" + str(nc.next_id()))
        w1 = s.sb("w1", [P, E, KC, F])
        w3 = s.sb("w3", [P, E, KC, F]) if gated else None
        w2 = s.sb("w2", [P, E, FC, D])
        b2 = s.sb("b2", [1, E, D]) if b2_d is not None else None
        b1 = s.sb("b1", [P, E, FC]) if b1_d is not None else None
        B1S = s.sb("B1S", [P, NS, FC]) if b1_d is not None else None
        ident = s.sb("ident", [P, P])
        below = s.sb("below", [P, P])
        ones = s.sb("ones", [P, P])
        step = s.sb("step", [P, NS])
        TOT = s.sb("TOT", [P, NT, E])
        SC = [s.sb(f"SC{i}", [P, NT, E]) for i in range(2)]
        CMP = s.sb("CMP", [P, E, NS])
        TE = s.sb("TE", [P, E])
        EN = [s.sb(f"EN{i}", [P, E]) for i in range(2)]
        PF = s.sb("PF", [P, NT])
        POS = s.sb("POS", [P, NT], mybir.dt.int32)
        XF = s.sb("XF", [P, NS])
        XI = s.sb("XI", [P, NS], mybir.dt.int32)
        WT = s.sb("WT", [P, NT])
        B1T = s.sb("B1T", [P, NS, FC]) if b1_d is not None else None
        XG = s.sb("XG", [P, D])
        wb = s.sb("wb", [P, 2, KC]) if affine is not None else None
        xt = s.sb("xt", [P, KC, P])
        ys = s.sb("ys", [P, D])
        G = s.sb("G", [P, F]) if gated else None
        h = SPARE[:, 0, 0:F]
        ht = SPARE[:, 1, 0:F].rearrange("p (c n) -> p c n", n=P)
        first = [s.ps(f"first{i}", [P, HF]) for i in range(2)]
        second = [s.ps(f"second{i}", [P, HF]) for i in range(2)] if gated else None
        hp = [s.ps(f"hp{i}", [P, HF // P, P]) for i in range(2)]
        yp = s.ps("yp", [P, D])
        xp = s.ps("xp", [P, KC, P])
        total = yp[:, 0:NT * E].rearrange("p (t e) -> p t e", e=E)
        before = xp[:].rearrange("p c n -> p (c n)")[:, 0:NT * E].rearrange("p (t e) -> p t e", e=E)
        w_loaded = [s.sem(f"w_loaded{e}") for e in range(E)]
        experts_ready = s.sem("experts_ready")
        ident_loaded = s.sem("ident_loaded")
        b_loaded = s.sem("b_loaded")
        wb_loaded = s.sem("wb_loaded")
        drawn = s.sem("drawn")
        counted = s.sem("counted")
        chain = s.sem("chain")
        placed = s.sem("placed")
        scattered = s.sem("scattered")
        x_loaded = s.sem("x_loaded")
        x_turned = s.sem("x_turned")
        xt_ready = s.sem("xt_ready")
        first_mm = s.sem("first_mm")
        gate_ready = s.sem("gate_ready")
        h_ready = s.sem("h_ready")
        h_turned = s.sem("h_turned")
        ht_ready = s.sem("ht_ready")
        y_mm = s.sem("y_mm")
        y_ready = s.sem("y_ready")
        stored = s.sem("stored")
        y_free = s.sem("y_free")
        gathered = [s.sem(f"gathered{i}") for i in range(TB)]
        n_w = 2 + gated
        drawn_all = []

        def scan(dve, c, bufs, n, view):
            a, b = bufs
            d = 1
            while d < n:
                c.inc(dve.tensor_copy(view(b, 0, d), view(a, 0, d)))
                c.inc(dve.tensor_tensor(view(b, d, n), view(a, d, n), view(a, 0, n - d), ALU.add))
                c.wait(dve)
                a, b = b, a
                d *= 2
            return a, b

        with nc.Block() as block:
            @block.sync
            def _(sp):
                sp.dma_start(ident[:], ident_d).then_inc(ident_loaded, 16)
                for i, part in enumerate(affine or ()):
                    sp.dma_start(wb[:, i, :], part).then_inc(wb_loaded, 16)
                sp.wait_ge(scattered, 16 * NT)
                sp.dma_start(XG[:], x_d[0:P, :]).then_inc(x_loaded, 16)
                sp.sem_inc(y_free, 1)

                def load(t):
                    sp.wait_ge(x_turned, t)
                    sp.dma_start(XG[:], x_d[ds(t * P, P), :]).then_inc(x_loaded, 16)

                def store(t, first=False):
                    if not first:
                        sp.wait_ge(stored, 16 * t)
                        sp.sem_inc(y_free, 1)
                    sp.wait_ge(y_ready, t + 2)
                    sp.dma_start(y_d[ds(t * P, P), :], ys[:]).then_inc(stored, 16)

                load(1)
                load(2)
                store(0, first=True)
                with sp.Fori(1, NS - 2) as t:
                    load(t + 2)
                    store(t)
                store(NS - 2)
                store(NS - 1)
                sp.wait_ge(stored, 16 * NS)
                sp.sem_inc(y_free, 1)

            @block.gpsimd
            def _(pool):
                c = Tally(drawn)
                c.inc(pool.memset(ones[:], 1.0))
                c.inc(pool.memset(below[:], 1.0))
                for j in range(NS):
                    c.inc(pool.memset(step[:, j:j + 1], float(j)))
                c.wait(pool)
                c.inc(pool.affine_select(out=below[:], in_=below[:], compare_op=ALU.is_gt, fill=0.0, base=0,
                                         pattern=[[1, P]], channel_multiplier=-1))
                drawn_all.append(c.n)
                pool.wait_ge(placed, 1)
                for t in range(NT):
                    pool.indirect_dma_start(x_d, bass.IndirectOffsetOnAxis(ap=POS[:, t:t + 1], axis=0), X[:, t, :],
                                            None, bounds_check=NS * P - 1).then_inc(scattered, 16)
                for e in range(E):
                    pool.wait_ge(w_loaded[e], 16 * n_w)
                    pool.sem_inc(experts_ready, 1 if e < E - 1 else NS)
                pool.wait_ge(y_free, NS + 1)
                for t in range(NT):
                    pool.indirect_dma_start(GOT[:, t, :], None, y_d,
                                            bass.IndirectOffsetOnAxis(ap=POS[:, t:t + 1], axis=0),
                                            bounds_check=NS * P - 1).then_inc(gathered[t // TB], 16)
                for i in range(TB):
                    pool.wait_ge(gathered[i], 16 * TB)

            @block.tensor
            def _(pe):
                pe.wait_ge(drawn, drawn_all[0])
                pe.matmul(before.rearrange("p t e -> p (t e)"), below[:], HOT[:].rearrange("p t e -> p (t e)"),
                          start=True, stop=True)
                pe.matmul(total.rearrange("p t e -> p (t e)"), ones[:], HOT[:].rearrange("p t e -> p (t e)"),
                          start=True, stop=True).then_inc(counted, 1)
                pe.sem_inc(first_mm, 2)
                pe.sem_inc(h_turned, 2)
                pe.sem_inc(y_mm, 1)
                pe.wait_ge(ident_loaded, 16)
                pe.wait_ge(placed, 1)

                def expert(t):
                    return pe.value_load(XI[0:1, ds(t, 1)], min_val=0, max_val=E - 1)

                def turn_x(t):
                    pe.wait_ge(x_loaded, 16 * (t + 1))
                    pe.wait_ge(xt_ready, t + 1)
                    for k in range(KC):
                        mm = pe.transpose(xp[:, k, :], XG[:, k * P:(k + 1) * P], ident[:])
                    mm.then_inc(x_turned, 1)

                def layer1(t):
                    e = expert(t)
                    pe.wait_ge(experts_ready, t + 1)
                    pe.wait_ge(xt_ready, t + 2)
                    for q in range(2):
                        pe.wait_ge(h_ready, 2 * t + q + 1)
                        for v, w in enumerate((w1, w3) if gated else (w1,)):
                            for k in range(KC):
                                mm = pe.matmul((second if v else first)[q][:], xt[:, k, :],
                                               w[:, ds(e, 1), k, q * HF:(q + 1) * HF],
                                               start=(k == 0), stop=(k == KC - 1))
                        mm.then_inc(first_mm, 1)

                def turn_h(t):
                    for q in range(2):
                        pe.wait_ge(h_ready, 2 * t + q + 3)
                        pe.wait_ge(ht_ready, 2 * t + q + 1)
                        for c in range(FC // 2):
                            f = q * FC // 2 + c
                            mm = pe.transpose(hp[q][:, c, :], h[:, f * P:(f + 1) * P], ident[:])
                        mm.then_inc(h_turned, 1)

                def layer2(t):
                    e = expert(t)
                    pe.wait_ge(ht_ready, 2 * t + 4)
                    pe.wait_ge(y_ready, t + 1)
                    if b2 is not None:
                        pe.matmul(yp[:], ones[0:1, :], b2[0:1, ds(e, 1), :], start=True, stop=False)
                    for f in range(FC):
                        mm = pe.matmul(yp[:], ht[:, f, :], w2[:, ds(e, 1), f, :],
                                       start=(f == 0 and b2 is None), stop=(f == FC - 1))
                    mm.then_inc(y_mm, 1)

                if b2 is not None:
                    pe.wait_ge(b_loaded, 32)
                turn_x(0)
                layer1(0)
                with pe.Fori(0, NS - 1) as t:
                    turn_x(t + 1)
                    turn_h(t)
                    layer1(t + 1)
                    layer2(t)
                turn_h(NS - 1)
                layer2(NS - 1)

            @block.scalar
            def _(act):
                for e in range(E):
                    act.dma_start(w1[:, e, :, :], w1_d[e].rearrange("(c p) f -> p c f", p=P)).then_inc(w_loaded[e], 16)
                    if gated:
                        act.dma_start(w3[:, e, :, :], w3_d[e].rearrange("(c p) f -> p c f", p=P)) \
                            .then_inc(w_loaded[e], 16)
                    act.dma_start(w2[:, e, :, :], w2_d[e].rearrange("(c p) f -> p c f", p=P)).then_inc(w_loaded[e], 16)
                    if e == 0 and b1 is not None:
                        act.dma_start(b1[:], b1_d.rearrange("e p c -> p e c")).then_inc(b_loaded, 16)
                        act.dma_start(b2[:], b2_d.unsqueeze(0)).then_inc(b_loaded, 16)
                if gated:
                    act.sem_inc(ht_ready, 2)
                else:
                    act.sem_inc(h_ready, 2)
                act.sem_inc(y_ready, 1)
                act.wait_ge(placed, 1)

                def take_first(t):
                    for q in range(2):
                        act.wait_ge(first_mm, 2 * t + q + 3)
                        if gated:
                            act.wait_ge(h_ready, 2 * t + q + 1)
                            act.activation(G[:, q * HF:(q + 1) * HF], first[q][:], func).then_inc(gate_ready, 1)
                        else:
                            act.wait_ge(h_turned, 2 * t + 2)
                            act.activation(h[:, q * HF:(q + 1) * HF], first[q][:], ACT.Copy).then_inc(h_ready, 1)

                def take_turned(t):
                    act.wait_ge(y_mm, t + 1)
                    for q in range(2):
                        act.wait_ge(h_turned, 2 * t + q + 3)
                        act.activation(ht[:, q * FC // 2:(q + 1) * FC // 2, :], hp[q][:], ACT.Copy) \
                            .then_inc(ht_ready, 1)

                def take_y(t):
                    act.wait_ge(y_mm, t + 2)
                    act.wait_ge(y_free, t + 1)
                    act.activation(ys[:], yp[:], ACT.Copy).then_inc(y_ready, 1)

                take_first(0)
                with act.Fori(0, NS - 1) as t:
                    if gated:
                        take_turned(t)
                    take_first(t + 1)
                    take_y(t)
                if gated:
                    take_turned(NS - 1)
                take_y(NS - 1)

            @block.vector
            def _(dve):
                c = Tally(chain)
                dve.wait_ge(drawn, drawn_all[0])
                dve.wait_ge(counted, 1)
                c.inc(dve.tensor_copy(TOT[:], total))
                c.inc(dve.tensor_copy(SC[0][:], total))
                c.wait(dve)
                upto, other = scan(dve, c, SC, NT, lambda b, i, j: b[:, i:j, :])
                c.inc(dve.tensor_scalar(TE[:], upto[:, NT - 1, :], 1.0 / P, None, ALU.mult))
                c.wait(dve)
                c.inc(dve.tensor_tensor(CMP[:, :, 0:NT], TE[:].unsqueeze(2).to_broadcast([P, E, NT]),
                                        step[:, 0:NT].unsqueeze(1).to_broadcast([P, E, NT]), ALU.is_gt))
                c.wait(dve)
                c.inc(dve.tensor_reduce(TE[:], CMP[:, :, 0:NT], AX.X, ALU.add))
                c.wait(dve)
                c.inc(dve.tensor_scalar(TE[:], TE[:], 1.0, None, ALU.max))
                c.wait(dve)
                c.inc(dve.tensor_copy(EN[0][:], TE[:]))
                c.wait(dve)
                ends, starts = scan(dve, c, EN, E, lambda b, i, j: b[:, i:j])
                c.inc(dve.tensor_tensor(starts[:], ends[:], TE[:], ALU.subtract))
                c.inc(dve.tensor_tensor(other[:], upto[:], TOT[:], ALU.subtract))
                c.wait(dve)
                c.inc(dve.tensor_scalar(starts[:], starts[:], float(P), None, ALU.mult))
                c.inc(dve.tensor_tensor(other[:], other[:], before, ALU.add))
                c.wait(dve)
                c.inc(dve.tensor_tensor(other[:], other[:], starts[:].unsqueeze(1).to_broadcast([P, NT, E]), ALU.add))
                c.wait(dve)
                c.inc(dve.tensor_tensor(other[:], other[:], HOT[:], ALU.mult))
                c.wait(dve)
                c.inc(dve.tensor_reduce(PF[:], other[:], AX.X, ALU.add))
                c.wait(dve)
                c.inc(dve.tensor_copy(POS[:], PF[:]))
                c.inc(dve.tensor_tensor(CMP[:], ends[:].unsqueeze(2).to_broadcast([P, E, NS]),
                                        step[:, 0:NS].unsqueeze(1).to_broadcast([P, E, NS]), ALU.is_le))
                c.wait(dve)
                c.inc(dve.tensor_reduce(XF[:], CMP[:].rearrange("p e s -> p s e"), AX.X, ALU.add))
                c.wait(dve)
                c.inc(dve.tensor_scalar(XF[:], XF[:], float(E - 1), None, ALU.min))
                c.wait(dve)
                c.inc(dve.tensor_copy(XI[:], XF[:]))
                c.wait(dve)
                dve.sem_inc(placed, 1)
                dve.sem_inc(xt_ready, 1)
                if gated:
                    dve.sem_inc(h_ready, 2)
                else:
                    dve.sem_inc(ht_ready, 2)
                if b1 is not None:
                    dve.wait_ge(b_loaded, 32)
                    for e in range(E):
                        c.inc(dve.tensor_scalar(CMP[:, 0, :], XF[:], float(e), None, ALU.is_equal))
                        c.wait(dve)
                        hot = CMP[:, 0, :].unsqueeze(2).to_broadcast([P, NS, FC])
                        row = b1[:, e, :].unsqueeze(1).to_broadcast([P, NS, FC])
                        if e == 0:
                            c.inc(dve.tensor_tensor(B1S[:], hot, row, ALU.mult))
                        else:
                            c.inc(dve.tensor_tensor(B1T[:], hot, row, ALU.mult))
                            c.wait(dve)
                            c.inc(dve.tensor_tensor(B1S[:], B1S[:], B1T[:], ALU.add))
                        c.wait(dve)
                if COMB is not None:
                    c.inc(dve.tensor_reduce(WT[:], COMB[:], AX.X, ALU.add))
                    c.wait(dve)

                def take_x(t):
                    dve.wait_ge(x_turned, t + 1)
                    dve.wait_ge(first_mm, 2 * t + 2)
                    if affine is None:
                        dve.tensor_copy(xt[:], xp[:]).then_inc(xt_ready, 1)
                        return
                    for k in range(KC):
                        ins = dve.tensor_scalar(xt[:, k, :], xp[:, k, :], wb[:, 0, k:k + 1], wb[:, 1, k:k + 1],
                                                ALU.mult, ALU.add)
                    ins.then_inc(xt_ready, 1)

                def gate(t):
                    for q in range(2):
                        dve.wait_ge(gate_ready, 2 * t + q + 1)
                        dve.wait_ge(h_turned, 2 * t + 2)
                        dve.tensor_tensor(h[:, q * HF:(q + 1) * HF], G[:, q * HF:(q + 1) * HF], second[q][:],
                                          ALU.mult).then_inc(h_ready, 1)

                def bias_relu(t):
                    dve.wait_ge(y_mm, t + 1)
                    for q in range(2):
                        dve.wait_ge(h_turned, 2 * t + q + 3)
                        for k in range(FC // 2):
                            f = q * FC // 2 + k
                            ins = dve.tensor_scalar(ht[:, f, :], hp[q][:, k, :], B1S[:, ds(t, 1), f], 0.0,
                                                    ALU.add, ALU.max)
                        ins.then_inc(ht_ready, 1)

                if affine is not None:
                    dve.wait_ge(wb_loaded, 32)
                take_x(0)
                if gated:
                    gate(0)
                with dve.Fori(0, NS - 1) as t:
                    take_x(t + 1)
                    if not gated:
                        bias_relu(t)
                    if gated:
                        gate(t + 1)
                if not gated:
                    bias_relu(NS - 1)
                if COMB is not None or GOT is not Y:
                    for i in range(TB):
                        rows = slice(i * TB, (i + 1) * TB)
                        dve.wait_ge(gathered[i], 16 * TB)
                        if COMB is not None:
                            c.inc(dve.tensor_tensor(GOT[:, rows, :], GOT[:, rows, :],
                                                    WT[:, rows].unsqueeze(2).to_broadcast([P, TB, D]), ALU.mult))
                            c.wait(dve)
                        if GOT is not Y:
                            c.inc(dve.tensor_tensor(Y[:, rows, :], Y[:, rows, :], GOT[:, rows, :], ALU.add))


def stage_load(nc, name, pairs):
    with nc.semaphore(name) as loaded, nc.Block() as block:
        @block.sync
        def _(sp):
            for dst, src in pairs:
                sp.dma_start(dst, src).then_inc(loaded, 16)
            sp.wait_ge(loaded, 16 * len(pairs))


def stage_spectral(nc, W, qkv_d, u_qkv, sp_qkv, proj_d, u_proj, sp_proj):
    with ExitStack() as stack:
        s = Space(nc, stack, "sn")
        ones = s.sb("ones", [P, P])
        loaded = s.sem("loaded")
        ones_ready = s.sem("ones_ready")
        chain = s.sem("chain")
        mm_done = s.sem("mm_done")
        root = s.sem("root")
        parts = []
        for name, wd, u, sp_, n in (("qkv", qkv_d, u_qkv, sp_qkv, 3 * D), ("proj", proj_d, u_proj, sp_proj, D)):
            parts.append(dict(
                n=n, wd=wd, u=u, sp=sp_, w=s.sb("w" + name, [P, KC, n]), ub=s.sb("u" + name, [P, n]),
                pr=s.sb("pr" + name, [P, KC, n]), v=s.sb("v" + name, [P, KC]), sq=s.sb("sq" + name, [P, n // P]),
                r=s.sb("r" + name, [P, 1]), t=s.sb("t" + name, [P, 2]), u2=s.sb("u2" + name, [P, n // P]),
                c=s.sb("c" + name, [P, 1]), nrm=s.ps("nrm" + name, [P, 1]), col=s.ps("col" + name, [P, n // P])))
        with nc.Block() as block:
            @block.sync
            def _(sp):
                for p in parts:
                    sp.dma_start(p["w"][:], p["wd"].rearrange("(c p) n -> p c n", p=P)).then_inc(loaded, 16)
                    sp.dma_start(p["ub"][:], p["u"].unsqueeze(0).to_broadcast([P, p["n"]])).then_inc(loaded, 16)
                    sp.dma_start(p["c"][:], p["sp"].unsqueeze(0).to_broadcast([P, 1])).then_inc(loaded, 16)

            @block.vector
            def _(dve):
                c = Tally(chain)
                dve.memset(ones[:], 1.0).then_inc(ones_ready, 1)
                dve.wait_ge(loaded, 96)
                for k, p in enumerate(parts):
                    n = p["n"]
                    c.inc(dve.tensor_tensor(p["pr"][:], p["w"][:], p["ub"][:].unsqueeze(1).to_broadcast([P, KC, n]),
                                            ALU.mult))
                    c.wait(dve)
                    c.inc(dve.tensor_reduce(p["v"][:], p["pr"][:], AX.X, ALU.add))
                    c.wait(dve)
                    for src, width in ((p["v"], KC), (p["u2"], n // P)):
                        if width != KC or src is p["u2"]:
                            dve.wait_ge(mm_done, 3 * k + 2)
                            c.inc(dve.tensor_copy(src[:], p["col"][:]))
                            c.wait(dve)
                        c.inc(dve.tensor_tensor(p["sq"][:, 0:width], src[:], src[:], ALU.mult))
                        c.wait(dve)
                        c.inc(dve.tensor_reduce(p["r"][:], p["sq"][:, 0:width], AX.X, ALU.add))
                        p.setdefault("ready", []).append(c.n)
                        c.wait(dve)
                        if src is p["v"]:
                            dve.wait_ge(root, 2 * k + 1)
                            c.inc(dve.reciprocal(p["t"][:, 1:2], p["t"][:, 0:1]))
                            c.wait(dve)
                            c.inc(dve.tensor_scalar(p["v"][:], p["v"][:], p["t"][:, 1:2], None, ALU.mult))
                            p["v_ready"] = c.n
                            c.wait(dve)
                        else:
                            dve.wait_ge(root, 2 * k + 2)
                            c.inc(dve.reciprocal(p["t"][:, 1:2], p["t"][:, 0:1]))
                            c.wait(dve)
                            c.inc(dve.tensor_scalar(p["c"][:], p["c"][:], p["t"][:, 1:2], None, ALU.mult))
                            c.wait(dve)
                for m in ("q", "k", "v"):
                    c.inc(dve.tensor_scalar(W[m][:], W[m][:], parts[0]["c"][:], None, ALU.mult))
                c.inc(dve.tensor_scalar(W["o"][:], W["o"][:], parts[1]["c"][:], None, ALU.mult))

            @block.tensor
            def _(pe):
                pe.wait_ge(ones_ready, 1)
                for k, p in enumerate(parts):
                    pe.wait_ge(chain, p["ready"][0])
                    pe.matmul(p["nrm"][:], ones[:], p["r"][:], start=True, stop=True).then_inc(mm_done, 1)
                    pe.wait_ge(chain, p["v_ready"])
                    for m in range(p["n"] // P):
                        for q in range(KC):
                            mm = pe.matmul(p["col"][:, m:m + 1], p["w"][:, q, m * P:(m + 1) * P], p["v"][:, q:q + 1],
                                           start=(q == 0), stop=(q == KC - 1))
                    mm.then_inc(mm_done, 1)
                    pe.wait_ge(chain, p["ready"][1])
                    pe.matmul(p["nrm"][:], ones[:], p["r"][:], start=True, stop=True).then_inc(mm_done, 1)

            @block.scalar
            def _(act):
                for k, p in enumerate(parts):
                    for m in range(2):
                        act.wait_ge(mm_done, 3 * k + 1 + 2 * m)
                        act.activation(p["t"][:, 0:1], p["nrm"][:], ACT.Sqrt).then_inc(root, 1)


def stage_binary(nc, W):
    with ExitStack() as stack:
        s = Space(nc, stack, "bi")
        ones = s.sb("ones", [P, P])
        shapes = {"q": (P, KC, D), "k": (P, KC, D), "v": (P, KC, D), "o": (P, NG, D)}
        view = {n: W[n][:] for n in shapes}
        SG = {n: s.sb("sg" + n, list(sh)) for n, sh in shapes.items()}
        AB = {n: s.sb("ab" + n, list(sh)) for n, sh in shapes.items()}
        al = {n: s.ps("al" + n, [sh[0], sh[2]]) for n, sh in shapes.items()}
        ones_ready = s.sem("ones_ready")
        signs = s.sem("signs")
        sizes = s.sem("sizes")
        mm_done = s.sem("mm_done")
        chain = s.sem("chain")
        with nc.Block() as block:
            @block.scalar
            def _(act):
                for n in shapes:
                    act.activation(AB[n][:], view[n], ACT.Abs).then_inc(sizes, 1)
                    act.activation(SG[n][:], view[n], ACT.Sign).then_inc(signs, 1)

            @block.tensor
            def _(pe):
                pe.wait_ge(ones_ready, 1)
                for i, (n, (rows, chunks, width)) in enumerate(shapes.items()):
                    pe.wait_ge(sizes, i + 1)
                    for k in range(chunks):
                        mm = pe.matmul(al[n][:], ones[0:rows, 0:rows], AB[n][:, k, :],
                                       start=(k == 0), stop=(k == chunks - 1))
                    mm.then_inc(mm_done, 1)

            @block.vector
            def _(dve):
                dve.memset(ones[:], 1.0).then_inc(ones_ready, 1)
                c = Tally(chain)
                for i, (n, (rows, chunks, width)) in enumerate(shapes.items()):
                    dve.wait_ge(signs, i + 1)
                    c.inc(dve.tensor_tensor(SG[n][:], SG[n][:], view[n], ALU.subtract))
                    c.wait(dve)
                    c.inc(dve.tensor_tensor(view[n], view[n], SG[n][:], ALU.add))
                    c.wait(dve)
                    dve.wait_ge(mm_done, i + 1)
                    for k in range(chunks):
                        c.inc(dve.scalar_tensor_tensor(view[n][:, k, :], al[n][:], 1.0 / D, view[n][:, k, :],
                                                       ALU.mult, ALU.mult))


def stage_ternary(nc, tensors):
    with ExitStack() as stack:
        s = Space(nc, stack, "te")
        ones = s.sb("ones", [P, P])
        ones_ready = s.sem("ones_ready")
        chain = s.sem("chain")
        mm_done = s.sem("mm_done")
        sums = [s.sb(f"sum{i}", [P, 1]) for i in range(2)]
        thr = [s.sb(f"thr{i}", [P, 2]) for i in range(2)]
        low = [s.sb(f"low{i}", [P, 2048]) for i in range(2)]
        tot = [s.ps(f"tot{i}", [P, 1]) for i in range(2)]
        count = float(1024 * D)
        ready = []
        with nc.Block() as block:
            @block.vector
            def _(dve):
                dve.memset(ones[:], 1.0).then_inc(ones_ready, 1)
                c = Tally(chain)
                for i, w in enumerate(tensors):
                    c.inc(dve.tensor_reduce(sums[i][:], w, AX.XY, ALU.add, apply_absolute_value=True))
                    ready.append(c.n)
                for i, w in enumerate(tensors):
                    lo = low[i][:].rearrange("p (a b) -> p a b", a=w.shape[1])
                    dve.wait_ge(mm_done, i + 1)
                    for m, sign in enumerate((0.5, -0.5)):
                        c.inc(dve.tensor_scalar(thr[i][:, m:m + 1], tot[i][:], sign / count, sign * 1e-5,
                                                ALU.mult, ALU.add))
                    c.wait(dve)
                    c.inc(dve.tensor_scalar(lo, w, thr[i][:, 1:2], None, ALU.is_lt))
                    c.wait(dve)
                    c.inc(dve.scalar_tensor_tensor(w, w, thr[i][:, 0:1], lo, ALU.is_gt, ALU.subtract))

            @block.tensor
            def _(pe):
                pe.wait_ge(ones_ready, 1)
                for i in range(len(tensors)):
                    pe.wait_ge(chain, ready[i])
                    pe.matmul(tot[i][:], ones[:], sums[i][:], start=True, stop=True).then_inc(mm_done, 1)


def stage_conv(nc, XT, XC, taps_d):
    with ExitStack() as stack:
        s = Space(nc, stack, "cv")
        taps = s.sb("taps", [P, KC, 3])
        loaded = s.sem("loaded")
        summed = s.sem("summed")
        with nc.Block() as block:
            @block.sync
            def _(sp):
                sp.dma_start(taps[:], taps_d.rearrange("(c p) w -> p c w", p=P)).then_inc(loaded, 16)

            @block.vector
            def _(dve):
                c = Tally(summed)
                dve.wait_ge(loaded, 16)
                for k in range(KC):
                    x = XT[:, k, :].rearrange("p (b t) -> p b t", b=B)
                    y = XC[:, k, :].rearrange("p (b t) -> p b t", b=B)
                    c.inc(dve.tensor_scalar(y, x, taps[:, k, 2:3], None, ALU.mult))
                    for lag in (1, 2):
                        c.wait(dve)
                        c.inc(dve.scalar_tensor_tensor(y[:, :, lag:T], x[:, :, 0:T - lag],
                                                       taps[:, k, 2 - lag:3 - lag], y[:, :, lag:T],
                                                       ALU.mult, ALU.add))



def stage_linear(nc, XT, Y, ident_d, wqk_d, wv_d, wo_d, bqk_d, bv_d, bo_d):
    E1 = AD + 1
    OWN = 1
    with ExitStack() as stack:
        s = Space(nc, stack, "li")
        ident = s.sb("ident", [P, P])
        wqk = s.sb("wqk", [P, KC, 2 * D])
        wv = s.sb("wv", [P, KC, D])
        wo = s.sb("wo", [P, KC, D])
        bqk = s.sb("bqk", [P, 2 * D])
        bv = s.sb("bv", [P, D])
        bo = s.sb("bo", [P, D])
        XS = [s.sb(f"XS{i}", [P, KC, P]) for i in range(TB)]
        QK = [s.sb(f"QK{i}", [P, 2 * D]) for i in range(TB)]
        EX = [s.sb(f"EX{i}", [P, 2 * D]) for i in range(TB)]
        V1 = [s.sb(f"V1{i}", [P, AH, E1]) for i in range(TB)]
        KV = s.sb("KV", [P, AD, E1])
        PR = [s.sb(f"PR{i}", [P, AD, E1, AH]) for i in range(2)]
        PQ = s.sb("PQ", [P, AH, E1, AD])
        QV = s.sb("QV", [P, AH, E1])
        RI = s.sb("RI", [P, AH])
        AT = [s.sb(f"AT{i}", [P, D]) for i in range(2)]
        ATT = [s.sb(f"ATT{i}", [P, KC, P]) for i in range(2)]
        pqk = [s.ps(f"pqk{i}", [P, 2 * D]) for i in range(2)]
        pv = [s.ps(f"pv{i}", [P, 512]) for i in range(2)]
        tp = [s.ps(f"tp{i}", [P, KC, 2 * P]) for i in range(2)]
        yo = [s.ps(f"yo{i}", [P, 512]) for i in range(2)]
        loaded = s.sem("loaded")
        ones_ready = s.sem("ones_ready")
        xs_ready = s.sem("xs_ready")
        qkv_mm = s.sem("qkv_mm")
        qk_added = s.sem("qk_added")
        v_ready = s.sem("v_ready")
        low_ready = s.sem("low_ready")
        exp_ready = s.sem("exp_ready")
        elu_ready = s.sem("elu_ready")
        kv_product = s.sem("kv_product")
        kv_ready = s.sem("kv_ready")
        chain = s.sem("chain")
        at_ready = s.sem("at_ready")
        turned = s.sem("turned")
        att_ready = s.sem("att_ready")
        o_mm = s.sem("o_mm")
        y_ready = s.sem("y_ready")
        own_product = s.sem("own_product")

        def keys_values(j):
            k = QK[j][:, D:2 * D].rearrange("p (h d) -> p d h", h=AH)
            v = V1[j][:].rearrange("p h e -> p e h")
            return (k.unsqueeze(2).to_broadcast([P, AD, E1, AH]), v.unsqueeze(1).to_broadcast([P, AD, E1, AH]))

        with nc.Block() as block:
            @block.sync
            def _(sp):
                sp.dma_start(ident[:], ident_d).then_inc(loaded, 16)
                for dst, src in ((wqk, wqk_d), (wv, wv_d), (wo, wo_d)):
                    sp.dma_start(dst[:], src.rearrange("(c p) n -> p c n", p=P)).then_inc(loaded, 16)
                for dst, src in ((bqk, bqk_d), (bv, bv_d), (bo, bo_d)):
                    sp.dma_start(dst[:], src.unsqueeze(0).to_broadcast([P, src.shape[0]])).then_inc(loaded, 16)

            @block.gpsimd
            def _(pool):
                for j in range(TB):
                    pool.memset(V1[j][:], 1.0).then_inc(ones_ready, 1)
                pool.sem_inc(kv_product, 1)
                with pool.Fori(0, B) as b:
                    for j in range(TB):
                        pool.wait_ge(qk_added, TB * b + j + 1)
                        pool.tensor_copy(XS[j][:], XT[:, :, ds(T * b + P * j, P)]).then_inc(xs_ready, 1)
                    for j in range(OWN, TB):
                        pool.wait_ge(elu_ready, TB * b + j + 1)
                        pool.wait_ge(v_ready, TB * b + j + 1 + TB)
                        pool.wait_ge(kv_ready, TB * b + j + 1)
                        pool.tensor_tensor(PR[j % 2][:], *keys_values(j), ALU.mult).then_inc(kv_product, 1)

            @block.tensor
            def _(pe):
                pe.wait_ge(loaded, 16 * 7)
                with pe.Fori(0, B) as b:
                    for j in range(TB):
                        f = j % 2
                        pe.wait_ge(xs_ready, TB * b + j + 1)
                        pe.wait_ge(qk_added, TB * b + j + 3)
                        pe.wait_ge(v_ready, TB * b + j + 3)
                        for k in range(KC):
                            pe.matmul(pqk[f][:], XS[j][:, k, :], wqk[:, k, :], start=(k == 0), stop=(k == KC - 1))
                        for k in range(KC):
                            mm = pe.matmul(pv[f][:, 0:D], XS[j][:, k, :], wv[:, k, :],
                                           start=(k == 0), stop=(k == KC - 1))
                        mm.then_inc(qkv_mm, 1)
                    for j in range(TB):
                        f = j % 2
                        pe.wait_ge(at_ready, TB * b + j + 1)
                        pe.wait_ge(att_ready, TB * b + j + 1)
                        for k in range(KC):
                            mm = pe.transpose(tp[f][:, k, 0:P], AT[f][:, k * P:(k + 1) * P], ident[:])
                        mm.then_inc(turned, 1)
                        pe.wait_ge(att_ready, TB * b + j + 3)
                        pe.wait_ge(y_ready, TB * b + j + 1)
                        for k in range(KC):
                            mm = pe.matmul(yo[f][:, 0:D], ATT[f][:, k, :], wo[:, k, :],
                                           start=(k == 0), stop=(k == KC - 1))
                        mm.then_inc(o_mm, 1)

            @block.scalar
            def _(act):
                act.sem_inc(att_ready, 2)
                with act.Fori(0, B) as b:
                    for j in range(TB):
                        act.wait_ge(low_ready, TB * b + j + 1)
                        act.activation(EX[j][:], EX[j][:], ACT.Exp).then_inc(exp_ready, 1)
                    for j in range(TB):
                        act.wait_ge(turned, TB * b + j + 1)
                        act.wait_ge(y_ready, TB * b + j + 1)
                        act.activation(ATT[j % 2][:], tp[j % 2][:, :, 0:P], ACT.Copy).then_inc(att_ready, 1)

            @block.vector
            def _(dve):
                dve.wait_ge(loaded, 16 * 7)
                dve.wait_ge(ones_ready, TB)
                dve.sem_inc(qk_added, TB)
                dve.sem_inc(v_ready, TB)
                dve.sem_inc(kv_ready, 2)
                dve.sem_inc(y_ready, 2)
                per = 4 * TB

                with dve.Fori(0, B) as b:
                    c = Tally(chain, per * b)
                    for j in range(TB):
                        n = TB * b + j
                        f = j % 2
                        dve.wait_ge(qkv_mm, n + 1)
                        dve.wait_ge(kv_product, (TB - OWN) * b + 1)
                        dve.tensor_tensor(QK[j][:], pqk[f][:], bqk[:], ALU.add).then_inc(qk_added, 1)
                        dve.tensor_tensor(V1[j][:, :, 0:AD], pv[f][:, 0:D].rearrange("p (h e) -> p h e", h=AH),
                                          bv[:].rearrange("p (h e) -> p h e", h=AH), ALU.add).then_inc(v_ready, 1)
                        dve.wait_ge(qk_added, n + 1 + TB)
                        dve.tensor_scalar(EX[j][:], QK[j][:], 0.0, None, ALU.min).then_inc(low_ready, 1)
                    for j in range(TB):
                        n = TB * b + j
                        dve.wait_ge(exp_ready, n + 1)
                        dve.scalar_tensor_tensor(QK[j][:], QK[j][:], 0.0, EX[j][:], ALU.max, ALU.add) \
                            .then_inc(elu_ready, 1)

                    def add_out(j):
                        dve.wait_ge(o_mm, TB * b + j + 1)
                        dve.tensor_tensor(Y[:, ds(TB * b + j, 1), :], yo[j % 2][:, 0:D].unsqueeze(1),
                                          bo[:].unsqueeze(1), ALU.add).then_inc(y_ready, 1)

                    for j in range(TB):
                        n = TB * b + j
                        if j < OWN:
                            dve.wait_ge(elu_ready, n + 1)
                            dve.tensor_tensor(PR[j % 2][:], *keys_values(j), ALU.mult).then_inc(own_product, 1)
                            dve.wait_ge(own_product, OWN * b + j + 1)
                        else:
                            dve.wait_ge(kv_product, (TB - OWN) * b + j - OWN + 2)
                        dve.tensor_reduce(KV[:], PR[j % 2][:], AX.X, ALU.add).then_inc(kv_ready, 1)
                        dve.wait_ge(kv_ready, n + 3)
                        q = QK[j][:, 0:D].rearrange("p (h d) -> p h d", h=AH)
                        c.inc(dve.tensor_tensor(PQ[:], q.unsqueeze(2).to_broadcast([P, AH, E1, AD]),
                                                KV[:].rearrange("p d e -> p e d").unsqueeze(1)
                                                .to_broadcast([P, AH, E1, AD]), ALU.mult))
                        c.wait(dve)
                        c.inc(dve.tensor_reduce(QV[:], PQ[:], AX.X, ALU.add))
                        c.wait(dve)
                        c.inc(dve.reciprocal(RI[:], QV[:, :, AD]))
                        c.wait(dve)
                        dve.wait_ge(att_ready, n + 1)
                        c.inc(dve.tensor_tensor(AT[j % 2][:].rearrange("p (h e) -> p h e", h=AH), QV[:, :, 0:AD],
                                                RI[:].unsqueeze(2).to_broadcast([P, AH, AD]), ALU.mult))
                        c.wait(dve)
                        dve.sem_inc(at_ready, 1)
                        if j:
                            add_out(j - 1)
                    add_out(TB - 1)



def tower(nc, a, out):
    ident = a["ident"]
    RETIRED.clear()
    split_d = [nc.dram_tensor(f"split_{n}", (B, 2, NP, AD, AH // 2, T), BF16, kind="Internal").ap() for n in ("q", "k")]
    sorted_x = nc.dram_tensor("sorted_x", ((NT + 8) * P, D), F32, kind="Internal").ap()
    sorted_y = nc.dram_tensor("sorted_y", ((NT + 8) * P, D), F32, kind="Internal").ap()
    with ExitStack() as whole:
        def buf(stack, name, shape, dt=F32):
            return stack.enter_context(nc.sbuf_tensor(name, shape, dt))

        def attention_weights(stack, prefix, names):
            w = {n: buf(stack, f"{prefix}_{n}", [P, KC, D]) for n in names}
            w["o"] = buf(stack, f"{prefix}_o", [P, NG, D])
            return w, [(w[n][:], a[f"{prefix}_{n}"]) for n in w]

        H = buf(whole, "H", [P, NT, D])
        Y = buf(whole, "Y", [P, NT, D])
        XT = buf(whole, "XT", [P, KC, B * T])

        stage_tokens(nc, H, a["xk"], a["wsT"], a["wtok"])
        stage_rows(nc, H, None, XT, ident)
        with ExitStack() as st:
            OUT = buf(st, "OUT", [P, 2 + T, HN])
            with ExitStack() as cell:
                KN = buf(cell, "KN", [P, TL, D])
                QR = buf(cell, "QR", [P, TL, D])
                V = buf(cell, "V", [P, HN, T])
                BT = buf(cell, "BT", [P, HN, T])
                stage_cell_inputs(nc, XT, KN, QR, V, BT, a["w_in"], a["w_kq"], a["w_vb"], a["b_beta"])
                stage_cell(nc, KN, QR, V, BT, OUT, ident, sorted_x)
            stage_cell_out(nc, OUT[:, 2:, :], Y, a["w_out"])
        stage_rows(nc, H, Y, XT, ident, post="ln", second="rms", w=a["g1"])
        with ExitStack() as st:
            w, pairs = attention_weights(st, "a0", ("q", "k", "v", "qr", "kr"))
            stage_load(nc, "a0_loaded", pairs)
            stage_attention(nc, XT, Y, ident, split_d, w, a["no_bias"], a["no_v_bias"], True, a["rope"])
        stage_rows(nc, H, Y, XT, ident, post="add", second="rms", w=a["g2"])
        with ExitStack() as st:
            COMB = buf(st, "COMB0", [P, NT, 4])
            stage_router(nc, XT, COMB, ident, a["gate0"], 4, 2, "renormed")
            stage_experts(nc, XT, Y, COMB, 4, 768, ACT.Silu, a["e0_w1"], a["e0_w3"], a["e0_w2"])
        stage_rows(nc, H, Y, XT, ident, post="ln")

        with ExitStack() as st:
            w, pairs = attention_weights(st, "a1", ("q", "k", "v"))
            stage_load(nc, "a1_loaded", pairs)
            stage_spectral(nc, w, a["w_qkv"], a["u_qkv"], a["sp_qkv"], a["w_proj"], a["u_proj"], a["sp_proj"])
            stage_attention(nc, XT, Y, ident, split_d, w, a["no_bias"], a["no_v_bias"], True)
        stage_rows(nc, H, Y, XT, ident, post="ln")
        with ExitStack() as st:
            COMB = buf(st, "COMB1", [P, NT, 8])
            HOT = buf(st, "HOT1", [P, NT, 8])
            stage_router(nc, XT, COMB, ident, a["gate1"], 8, 1, "softmax", HOT)
            stage_chosen_experts(nc, H, Y, Y, XT, HOT, COMB, ident, sorted_x, sorted_y, 8, ACT.Relu,
                                 a["e1_w1"], None, a["e1_w2"], a["e1_b1"], a["e1_b2"])
        stage_rows(nc, H, Y, XT, ident, post="ln")

        with ExitStack() as st:
            w, pairs = attention_weights(st, "a2", ("q", "k", "v"))
            stage_load(nc, "a2_loaded", pairs)
            stage_binary(nc, w)
            stage_attention(nc, XT, Y, ident, split_d, w, a["a2_bias"], a["a2_bv"], False, out_bias=a["a2_bo"])
        stage_rows(nc, H, Y, XT, ident, post="ln", second="ln", w=a["c_ln1_w"], b=a["c_ln1_b"])
        with ExitStack() as st:
            XC = buf(st, "XC", [P, KC, B * T])
            stage_conv(nc, XT, XC, a["taps"])
            w, pairs = attention_weights(st, "a3", ("q", "k", "v", "qr", "kr"))
            stage_load(nc, "a3_loaded", pairs)
            stage_attention(nc, XC, Y, ident, split_d, w, a["no_bias"], a["no_v_bias"], True, a["rope"])
        with ExitStack() as st:
            XR = buf(st, "XR", [P, NT, D])
            HOT = buf(st, "HOT2", [P, NT, 4])
            stage_rows(nc, H, Y, XT, ident, post="add", second="ln", w=a["c_ln2_w"], b=a["c_ln2_b"], rows=XR)
            stage_router(nc, XT, HOT, ident, a["gate2"], 4, 1, "one")
            stage_chosen_experts(nc, XR, XR, Y, XT, HOT, None, ident, sorted_x, sorted_y, 4, ACT.Silu,
                                 a["e2_w1"], a["e2_w3"], a["e2_w2"], affine=(a["c_ln2_w"], a["c_ln2_b"]))
        stage_rows(nc, H, Y, XT, ident, post="ln", second="ln", w=a["d_ln1_w"], b=a["d_ln1_b"])

        stage_linear(nc, XT, Y, ident, a["l_wqk"], a["l_wv"], a["l_wo"], a["l_bqk"], a["l_bv"], a["l_bo"])
        stage_rows(nc, H, Y, XT, ident, post="add", second="ln", w=a["d_ln2_w"], b=a["d_ln2_b"])
        stage_experts(nc, XT, Y, None, 1, 1024, ACT.Gelu, a["fc_w"], None, a["fp_w"], a["fc_b"], a["fp_b"])
        stage_rows(nc, H, Y, XT, ident, post="ln")
        with ExitStack() as st:
            w1 = buf(st, "t_w1", [P, KC, 1024])
            w2 = buf(st, "t_w2", [P, 8, D])
            stage_load(nc, "t_loaded", [(w1[:], a["t_w1"]), (w2[:], a["t_w2"])])
            stage_ternary(nc, [w1[:], w2[:]])
            stage_experts(nc, XT, Y, None, 1, 1024, ACT.Relu, None, None, None, a["t_b1"], a["t_b2"], fresh=True,
                          resident=(w1, w2))
        stage_rows(nc, H, Y, None, ident, post="ln", out=out)



def layout(i):
    def rows(w):
        return w.reshape(KC, P, D).transpose(1, 0, 2)

    def columns(v):
        return v.reshape(KC, P).T

    def turned(w):
        return w.reshape(D, AH, 2, AD // 2)[:, :, ::-1, :].reshape(D, D)

    def bias(*bs):
        return np.stack(bs).reshape(4, P).T

    def out_rows(w):
        o = np.zeros((NG, AG, Q4, D), np.float32)
        o[:, :, :AD] = w.reshape(NG, AG, AD, D)
        return o.reshape(NG, P, D).transpose(1, 0, 2)

    def expert_bias(b):
        return b.reshape(b.shape[0], -1, P).transpose(0, 2, 1)

    freq = 1.0 / 10000.0 ** (np.arange(0, AD, 2, dtype=np.float32) / AD)
    angle = freq.astype(np.float32)[:, None] * np.arange(T, dtype=np.float32)[None, :]
    rope = np.zeros((2, P // AD, AD, T), np.float32)
    for half, sign in ((0, -1), (1, 1)):
        rows_of = slice(half * AD // 2, (half + 1) * AD // 2)
        rope[0, :, rows_of] = np.cos(angle)
        rope[1, :, rows_of] = sign * np.sin(angle)
    vb = np.stack([i["L0_attn_W_v"].reshape(HN, HD, D), i["L0_attn_W_beta"].reshape(HN, HD, D)], 1)
    kv_heads = lambda w: np.repeat(w.reshape(D, NG, AD), AG, axis=1).reshape(D, D)
    a = {
        "ident": np.eye(P, dtype=np.float32),
        "xk": i["x"].reshape(B * T, D, 4).transpose(2, 1, 0).reshape(4 * KC, P, B * T),
        "wsT": i["L0_tok_weighted_sum"].T.reshape(KC, P, D),
        "wtok": i["L0_tok_weight"].T,
        "w_in": i["L0_attn_W_in"].T.reshape(KC, P, D),
        "w_kq": np.concatenate([i["L0_attn_W_k"].T, i["L0_attn_W_q"].T], 1).reshape(KC, P, 2 * D),
        "w_vb": vb.reshape(HN, 2 * HD, KC, P).transpose(0, 3, 2, 1),
        "b_beta": np.tile(i["L0_attn_b_beta"].T, (B, 1)),
        "w_out": np.tile(i["L0_attn_W_out"].T.reshape(HN, HD, D).transpose(1, 0, 2), (B, 1, 1)),
        "g1": columns(i["L0_ffn_g1"]), "g2": columns(i["L0_ffn_g2"]),
        "rope": rope.reshape(2, P, T).transpose(1, 0, 2),
        "no_bias": np.zeros((P, 4), np.float32), "no_v_bias": np.zeros(D, np.float32),
        "a0_q": rows(i["L0_ffn_wq"]), "a0_qr": rows(turned(i["L0_ffn_wq"])),
        "a0_k": rows(kv_heads(i["L0_ffn_wk"])), "a0_kr": rows(turned(kv_heads(i["L0_ffn_wk"]))),
        "a0_v": rows(kv_heads(i["L0_ffn_wv"])), "a0_o": out_rows(i["L0_ffn_wo"]),
        "gate0": i["L0_ffn_gate"],
        "e0_w1": i["L0_ffn_w1"], "e0_w3": i["L0_ffn_w3"], "e0_w2": i["L0_ffn_w2"],
        "w_qkv": i["L1_attn_W_qkv"], "u_qkv": i["L1_attn_u_qkv"], "sp_qkv": i["L1_attn_sigma_qkv"],
        "w_proj": i["L1_attn_W_proj"], "u_proj": i["L1_attn_u_proj"], "sp_proj": i["L1_attn_sigma_proj"],
        "a1_q": rows(i["L1_attn_W_qkv"][:, 0:D]), "a1_k": rows(i["L1_attn_W_qkv"][:, D:2 * D]),
        "a1_v": rows(i["L1_attn_W_qkv"][:, 2 * D:]), "a1_o": out_rows(i["L1_attn_W_proj"]),
        "gate1": i["L1_ffn_gate_w"].T,
        "e1_w1": i["L1_ffn_w1"], "e1_w2": i["L1_ffn_w2"], "e1_b1": expert_bias(i["L1_ffn_b1"]),
        "e1_b2": i["L1_ffn_b2"],
        "a2_q": rows(i["L2_attn_Wq"].T), "a2_k": rows(i["L2_attn_Wk"].T), "a2_v": rows(i["L2_attn_Wv"].T),
        "a2_o": out_rows(i["L2_attn_Wp"].T), "a2_bo": i["L2_attn_bp"],
        "a2_bias": bias(i["L2_attn_bq"], i["L2_attn_bk"]), "a2_bv": i["L2_attn_bv"],
        "c_ln1_w": columns(i["L2_ffn_ln1_w"]), "c_ln1_b": columns(i["L2_ffn_ln1_b"]),
        "c_ln2_w": columns(i["L2_ffn_ln2_w"]), "c_ln2_b": columns(i["L2_ffn_ln2_b"]),
        "taps": i["L2_ffn_conv_w"][:, 0, :],
        "a3_q": rows(i["L2_ffn_attn_w"][:, 0:D]), "a3_qr": rows(turned(i["L2_ffn_attn_w"][:, 0:D])),
        "a3_k": rows(i["L2_ffn_attn_w"][:, D:2 * D]), "a3_kr": rows(turned(i["L2_ffn_attn_w"][:, D:2 * D])),
        "a3_v": rows(i["L2_ffn_attn_w"][:, 2 * D:]), "a3_o": out_rows(i["L2_ffn_proj_w"]),
        "gate2": i["L2_ffn_router_w"],
        "e2_w1": i["L2_ffn_expert_wv"][:, :, 0:1024], "e2_w3": i["L2_ffn_expert_wv"][:, :, 1024:],
        "e2_w2": i["L2_ffn_expert_proj"],
        "d_ln1_w": columns(i["L3_attn_ln1_w"]), "d_ln1_b": columns(i["L3_attn_ln1_b"]),
        "d_ln2_w": columns(i["L3_attn_ln2_w"]), "d_ln2_b": columns(i["L3_attn_ln2_b"]),
        "l_wqk": np.concatenate([i["L3_attn_q_w"].T, i["L3_attn_k_w"].T], 1),
        "l_wv": i["L3_attn_v_w"].T, "l_wo": i["L3_attn_o_w"].T,
        "l_bqk": np.concatenate([i["L3_attn_q_b"], i["L3_attn_k_b"]]),
        "l_bv": i["L3_attn_v_b"], "l_bo": i["L3_attn_o_b"],
        "fc_w": i["L3_attn_fc_w"].T[None], "fp_w": i["L3_attn_proj_w"].T[None],
        "fc_b": expert_bias(i["L3_attn_fc_b"][None]), "fp_b": i["L3_attn_proj_b"][None],
        "t_w1": i["L3_ffn_W1"].T.reshape(KC, P, 1024).transpose(1, 0, 2),
        "t_w2": i["L3_ffn_W2"].T.reshape(8, P, D).transpose(1, 0, 2),
        "t_b1": expert_bias(i["L3_ffn_b1"][None]), "t_b2": i["L3_ffn_b2"][None],
    }
    return {n: np.ascontiguousarray(v) for n, v in a.items()}


def kernel(**inputs):
    import concourse.bacc as _bacc
    from concourse.bass_utils import run_bass_kernel_spmd as _run

    nc = _bacc.Bacc("TRN2", target_bir_lowering=False, num_devices=1)
    arrays = layout({n: np.asarray(v) for n, v in inputs.items()})
    aps = {n: nc.dram_tensor("in_" + n, v.shape, mybir.dt.from_np(v.dtype), kind="ExternalInput").ap()
           for n, v in arrays.items()}
    out = nc.dram_tensor("out", (B, T, D), F32, kind="ExternalOutput").ap()
    tower(nc, aps, out)
    r = _run(nc, [{"in_" + n: v for n, v in arrays.items()}], core_ids=[0])
    return r.results[0]["out"]
```
